# Optimizing a Trainium2 kernel written in Bass

```python
import numpy as np
import jax
import jax.numpy as jnp

def _softmax(x, axis=-1):
    return jax.nn.softmax(x, axis=axis)
def _gelu(x):
    return jax.nn.gelu(x, approximate=True)
def _silu(x):
    return jax.nn.silu(x)
def _sigmoid(x):
    return jax.nn.sigmoid(x)
def _layernorm(x, axis=-1, eps=1e-5):
    m = jnp.mean(x, axis=axis, keepdims=True)
    v = jnp.var(x, axis=axis, keepdims=True)
    return (x - m) / jnp.sqrt(v + eps)
def _scatter_add(tgt, idx, src, axis=0):
    return tgt.at[idx].add(src)
def _segment_sum(src, seg, n):
    return jax.ops.segment_sum(src, seg, n)

kernel_name = 'mk_adj_preln_d2_adj_512_b33270'

def setup_inputs(seed: int = 0):
    np.random.seed(seed)
    _w = jnp.asarray
    def _rec_inputs():
        import jax
        import jax.numpy as jnp
        _gk = jax.random.key(seed)
        x = -0.0005207 + 1.001 * jax.random.normal(jax.random.fold_in(_gk, 1), (4096, 512), jnp.float32)
        _a = jax.random.bernoulli(jax.random.fold_in(_gk, 2), 0.00195312, (4096, 4096))
        _a = jnp.logical_or(_a, jnp.swapaxes(_a, -1, -2))
        _a = jnp.logical_or(_a, jnp.eye(4096, dtype=bool))
        _af = _a.astype(jnp.float32)
        _af = _af * jax.random.uniform(jax.random.fold_in(_gk, 3), (4096, 4096), jnp.float32, 0.05, 1e+09)
        adj = _af
        return x, adj
    x, adj = _rec_inputs()
    def _L0_gnn_setup():
        import jax, jax.numpy as jnp
        import numpy as np
        N, IN_DIM, H, D = (4096, 512, 8, 64)
        NEG = -1000000000.0
        key = jax.random.key(seed)
        k1, k2, k3, k4, k5, k6 = jax.random.split(key, 6)
        data = jax.random.normal(k1, (N, IN_DIM), dtype=jnp.float32)
        r = jax.random.uniform(k2, (N, N), dtype=jnp.float32)
        connectivity = jnp.where(r < 0.05, 0.0, NEG).astype(jnp.float32)
        lim_w = float(np.sqrt(6.0 / (IN_DIM + H * D)))
        W = jax.random.uniform(k3, (H * D, IN_DIM), jnp.float32, -lim_w, lim_w)
        b = jnp.zeros((H * D,), jnp.float32)
        lim_p = float(np.sqrt(6.0 / (H * D + 1)))
        src_proj = jax.random.uniform(k4, (1, H, D), jnp.float32, -lim_p, lim_p)
        trg_proj = jax.random.uniform(k5, (1, H, D), jnp.float32, -lim_p, lim_p)
        return {'data': data, 'connectivity': connectivity, 'W': W, 'b': b, 'src_proj': src_proj, 'trg_proj': trg_proj}
    _L0_gnn_all = _L0_gnn_setup()
    _L0_gnn_in = {k: v for k, v in _L0_gnn_all.items() if k in ('W', 'b', 'src_proj', 'trg_proj', )}
    del _L0_gnn_all

    def _L1_gnn_setup():
        import jax, jax.numpy as jnp
        import numpy as np
        N = 4096
        INPUT_DIM = 512
        KEY_DIM = 64
        OUT_DIM = 512
        N_HEADS = 8

        def _xavier_normal(key, shape, gain):
            fan_in, fan_out = (shape[-2], shape[-1])
            std = gain * (2.0 / (fan_in + fan_out)) ** 0.5
            return jax.random.normal(key, shape, dtype=jnp.float32) * std
        key = jax.random.key(seed)
        kx, ka, kk, kq, kv, ko = jax.random.split(key, 6)
        gain = 2.0 ** 0.5
        node_matrix = jax.random.normal(kx, (N, INPUT_DIM), dtype=jnp.float32)
        adjacency_matrix = jax.random.randint(ka, (N, N), 0, 2).astype(jnp.float32)
        Wks = _xavier_normal(kk, (N_HEADS, INPUT_DIM, KEY_DIM), gain)
        Wqs = _xavier_normal(kq, (N_HEADS, INPUT_DIM, KEY_DIM), gain)
        Wvs = _xavier_normal(kv, (N_HEADS, INPUT_DIM, KEY_DIM), gain)
        Wo = _xavier_normal(ko, (N_HEADS, KEY_DIM, OUT_DIM), gain)
        return {'node_matrix': node_matrix, 'adjacency_matrix': adjacency_matrix, 'Wks': Wks, 'Wqs': Wqs, 'Wvs': Wvs, 'Wo': Wo}
    _L1_gnn_all = _L1_gnn_setup()
    _L1_gnn_in = {k: v for k, v in _L1_gnn_all.items() if k in ('Wks', 'Wqs', 'Wvs', 'Wo', )}
    del _L1_gnn_all

    return {
        "x": x,
        "adj": adj,
        "L0_gnn_W": _L0_gnn_in["W"],
        "L0_gnn_b": _L0_gnn_in["b"],
        "L0_gnn_src_proj": _L0_gnn_in["src_proj"],
        "L0_gnn_trg_proj": _L0_gnn_in["trg_proj"],
        "L1_gnn_Wks": _L1_gnn_in["Wks"],
        "L1_gnn_Wqs": _L1_gnn_in["Wqs"],
        "L1_gnn_Wvs": _L1_gnn_in["Wvs"],
        "L1_gnn_Wo": _L1_gnn_in["Wo"],
    }

def reference(x, adj, L0_gnn_W, L0_gnn_b, L0_gnn_src_proj, L0_gnn_trg_proj, L1_gnn_Wks, L1_gnn_Wqs, L1_gnn_Wvs, L1_gnn_Wo):
    import jax
    import jax.numpy as jnp
    def _L0_gnn_ref(data, connectivity, W, b, src_proj, trg_proj):
        import jax, jax.numpy as jnp
        import numpy as np
        N, IN_DIM, H, D = (4096, 512, 8, 64)
        NEG = -1000000000.0
        data1 = (data @ W.T + b).reshape(N, H, D)
        src = jnp.einsum('nhd,xhd->nh', data1, src_proj)
        trg = jnp.einsum('nhd,xhd->nh', data1, trg_proj)
        e = src.T[:, :, None] + trg.T[:, None, :]
        e = jnp.where(e >= 0, e, 0.01 * e)
        e = e + connectivity[None, :, :]
        scores = jax.nn.softmax(e, axis=-1)
        out = jnp.einsum('hnm,hmd->hnd', scores, data1.transpose(1, 0, 2))
        out = out.transpose(1, 0, 2).reshape(N, H * D)
        return out

    def _L1_gnn_ref(node_matrix, adjacency_matrix, Wks, Wqs, Wvs, Wo):
        import jax, jax.numpy as jnp
        import numpy as np
        N = 4096
        INPUT_DIM = 512
        KEY_DIM = 64
        OUT_DIM = 512
        N_HEADS = 8

        def _xavier_normal(key, shape, gain):
            fan_in, fan_out = (shape[-2], shape[-1])
            std = gain * (2.0 / (fan_in + fan_out)) ** 0.5
            return jax.random.normal(key, shape, dtype=jnp.float32) * std
        n = adjacency_matrix.shape[0]
        adj = jnp.maximum(adjacency_matrix, jnp.eye(n, dtype=adjacency_matrix.dtype))
        keys = jnp.einsum('nj,hjk->hnk', node_matrix, Wks)
        queries = jnp.einsum('nj,hjk->hnk', node_matrix, Wqs)
        values = jnp.einsum('nj,hjk->hnk', node_matrix, Wvs)
        key_dim = Wks.shape[-1]
        atts = jnp.einsum('hqk,hmk->hqm', queries, keys) / key_dim ** 0.5
        atts = atts - 1e+16 * (1.0 - adj)[None, :, :]
        atts = jax.nn.softmax(atts, axis=-1)
        return jnp.einsum('hqm,hmk,hko->qo', atts, values, Wo)

    h = jnp.maximum(_layernorm(x, axis=-1), 0.0)
    x = x + _L0_gnn_ref(h, adj, L0_gnn_W, L0_gnn_b, L0_gnn_src_proj, L0_gnn_trg_proj)
    h = jnp.maximum(_layernorm(x, axis=-1), 0.0)
    x = x + _L1_gnn_ref(h, adj, L1_gnn_Wks, L1_gnn_Wqs, L1_gnn_Wvs, L1_gnn_Wo)
    return x


_drawn_inputs = setup_inputs


def setup_inputs(seed=0):
    import zlib

    import numpy as np

    out = dict(_drawn_inputs(seed))
    spreads = {'L0_gnn_b': (0.0, 0.1)}
    factors = {}
    for name, (base, spread) in spreads.items():
        noise = np.random.default_rng([zlib.crc32(name.encode()), seed]).standard_normal(out[name].shape)
        drawn = base * np.exp(spread * noise) if base else spread * noise
        out[name] = jnp.asarray(drawn.astype(out[name].dtype))
    for name, factor in factors.items():
        out[name] = (out[name] * factor).astype(out[name].dtype)
    return out
```

```python
from contextlib import ExitStack

import concourse.bass as bass
from concourse import mybir

F32 = mybir.dt.float32
F16 = mybir.dt.float16
BF16 = mybir.dt.bfloat16
ALU = mybir.AluOpType
ACT = mybir.ActivationFunctionType
AX = mybir.AxisListType

P = 128
N = 4096
F = 512
H = 8
D = 64
HP = H // 2
NT = N // P
KC = F // P
QB = 512
NB = N // QB
SUB = QB // P
EPS = 1e-5

G_RING = 6
P_RING = 8
DEN = 32
QUAD = P // DEN
LEAD = 4
QK_SCALE = 256.0
C_ROW = 4096.0
CREDIT = 2 * HP * NT


def wait_apart(eng, sem, value, passed):
    eng.wait_ge(sem, value)
    eng.sem_inc(passed, 1)


def layer0_project(nc, T, DR):
    with ExitStack() as ctx:
        def sb(name, shape, dt=F32):
            return ctx.enter_context(nc.sbuf_tensor(name, shape, dt))

        def pb(name, shape, dt=F32):
            return ctx.enter_context(nc.psum_tensor(name, shape, dt))

        def sem(name):
            return ctx.enter_context(nc.semaphore("a_" + name))

        rows = [sb(f"a_rows{s}", [P, N]) for s in range(SUB)]
        xg = sb("a_xg", [P, SUB, F])
        h = sb("a_h", [P, SUB, F])
        hT = sb("a_hT", [P, KC, QB])
        wT = sb("a_wT", [P, KC, F])
        wn = sb("a_wn", [P, KC, F])
        pj = sb("a_pj", [P, KC, 2 * H])
        wpj = sb("a_wpj", [P, KC, 2 * H])
        bcol = sb("a_bcol", [P, KC])
        bias = sb("a_bias", [P, F])
        bp = sb("a_bp", [2 * H, 1])
        stats = sb("a_stats", [P, SUB, 6])
        mv = sb("a_mv", [P, SUB, 2])
        std = sb("a_std", [P, SUB])
        rstd = sb("a_rstd", [P, SUB])
        nmr = sb("a_nmr", [P, SUB])
        eps = sb("a_eps", [P, 1])
        st = sb("a_st", [2 * H, QB])
        r_sb = sb("a_r", [H, QB])
        am_row = sb("a_am_row", [NT, P])

        tp = [pb(f"a_tp{i}", [P, QB]) for i in range(2)]
        vp = [pb(f"a_vp{i}", [P, F]) for i in range(2)]
        stp = pb("a_stp", [2 * H, QB])
        tq = pb("a_tq", [P, SUB, 2 * H])
        setup = pb("a_setup", [P, KC * 2 * H])
        amp = pb("a_amp", [NT, P])

        s_passed = sem("waits_passed")
        s_w = sem("w_in")
        s_row = [sem(f"row_in{s}") for s in range(SUB)]
        s_x = [sem(f"x_in{s}") for s in range(SUB)]
        s_rank = sem("row_ranked")
        s_chain = sem("vector_chain")
        s_eps = sem("eps")
        s_mv = sem("variance")
        s_std = sem("std")
        s_norm = sem("norm")
        s_h = sem("h")
        s_tp = sem("transposed")
        s_hT = sem("hT")
        s_set = sem("projected_weights")
        s_setc = sem("projected_weights_copied")
        s_stp = sem("st_psum")
        s_st = sem("st")
        s_tq = sem("t_columns")
        s_wv = sem("wv")
        s_r = sem("r")
        s_rout = sem("r_stored")
        s_vp = sem("v_psum")
        s_v = sem("v_done")
        s_amp = sem("amax_transposed")
        s_am = sem("amax_row")
        s_amout = sem("amax_stored")

        block = ctx.enter_context(nc.Block())

        @block.sync
        def _(sp):
            sp.dma_start(T["identf"][:, :], DR["identf"]).then_inc(s_w, 16)
            sp.dma_start(T["identb"][:, :], DR["identb"]).then_inc(s_w, 16)
            sp.dma_start(wT[:, :, :], DR["W0T"].rearrange("(c p) n -> p c n", p=P)).then_inc(s_w, 16)
            sp.dma_start(wn[:, :, :], DR["W0"].rearrange("(c p) n -> p c n", p=P)).then_inc(s_w, 16)
            sp.dma_start(pj[:, :, :], DR["proj"].rearrange("(c p) n -> p c n", p=P)).then_inc(s_w, 16)
            sp.dma_start(bcol[:, :], DR["bcol"]).then_inc(s_w, 16)
            sp.dma_start(bias[:, :], DR["b"].partition_broadcast(P)).then_inc(s_w, 16)
            sp.sem_inc(s_rank, SUB)
            with sp.Fori(0, NB) as g:
                for s in range(SUB):
                    sp.wait_ge(s_rank, g * SUB + (s + 1))
                    sp.dma_start(rows[s][:, :], DR["adj"][bass.ds(g * QB + s * P, P), :]).then_inc(s_row[s], 16)
            sp.wait_ge(s_am, 1)
            sp.dma_start(DR["amax"].rearrange("(t p) -> t p", p=P), am_row[:, :]).then_inc(s_amout, 16)
            sp.wait_ge(s_amout, 16)

        @block.gpsimd
        def _(pool):
            pool.memset(eps[:, :], EPS).then_inc(s_eps, 1)
            pool.sem_inc(s_h, SUB)
            with pool.Fori(0, NB) as g:
                for s in range(SUB):
                    wait_apart(pool, s_h, g * SUB + (s + 1), s_passed)
                    pool.dma_start(xg[:, s, :], DR["x"][bass.ds(g * QB + s * P, P), :]).then_inc(s_x[s], 16)

        @block.vector
        def _(dve):
            dve.wait_ge(s_set, 1)
            nc.vector.tensor_copy(wpj[:, :, :], setup[:, :].rearrange("p (c k) -> p c k", c=KC)).then_inc(s_setc, 1)
            dve.wait_ge(s_set, 2)
            nc.vector.tensor_copy(bp[:, :], setup[0:2 * H, 0:1]).then_inc(s_setc, 1)
            with dve.Fori(0, NB) as g:
                for s in range(SUB):
                    dve.wait_ge(s_x[s], g * 16 + 16)
                    nc.vector.bn_stats(stats[:, s, :], xg[:, s, :]).then_inc(s_chain, 1)
                wait_apart(dve, s_chain, g * (SUB + 1) + SUB, s_passed)
                for s in range(SUB):
                    nc.vector.bn_aggr(mv[:, s, :], stats[:, s, :]).then_inc(s_mv, 1)
                dve.wait_ge(s_std, g + 1)
                nc.vector.reciprocal(rstd[:, :], std[:, :]).then_inc(s_chain, 1)
                dve.wait_ge(s_chain, g * (SUB + 1) + (SUB + 1))
                nc.vector.scalar_tensor_tensor(out=nmr[:, :], in0=mv[:, :, 0], scalar=-1.0, in1=rstd[:, :],
                                               op0=ALU.mult, op1=ALU.mult).then_inc(s_norm, 1)
                for s in range(SUB):
                    dve.wait_ge(s_row[s], g * 16 + 16)
                    nc.vector.reduce_max(T["amax"][:, bass.ds(g * SUB + s, 1)], rows[s][:, :], AX.X).then_inc(s_rank, 1)
                    if s % 2 == 1:
                        for u in (s - 1, s):
                            dve.wait_ge(s_vp, g * SUB + (u + 1))
                            nc.vector.tensor_tensor(
                                T["V"][:, bass.ds(g * SUB + u, 1), :].rearrange("p a n -> p (a n)"),
                                vp[u % 2][:, :], bias[:, :], ALU.add).then_inc(s_v, 1)
                dve.wait_ge(s_wv, g * 2 + 2)
                nc.vector.tensor_scalar(T["nv"][:, bass.ds(g * SUB, SUB), :], T["v"][:, bass.ds(g * SUB, SUB), :],
                                        -1.0, None, ALU.mult).then_inc(s_v, 1)
            dve.wait_ge(s_amp, 1)
            nc.vector.tensor_copy(am_row[:, :], amp[:, :]).then_inc(s_am, 1)

        @block.scalar
        def _(act):
            act.wait_ge(s_eps, 1)
            act.sem_inc(s_rout, 16)
            with act.Fori(0, NB) as g:
                act.wait_ge(s_mv, g * SUB + SUB)
                nc.scalar.activation(std[:, :], mv[:, :, 1], ACT.Sqrt, bias=eps[:, :]).then_inc(s_std, 1)
                act.wait_ge(s_norm, g + 1)
                for s in range(SUB):
                    nc.scalar.activation(h[:, s, :], xg[:, s, :], ACT.Relu, bias=nmr[:, s:s + 1],
                                         scale=rstd[:, s:s + 1]).then_inc(s_h, 1)
                for c in range(KC):
                    act.wait_ge(s_tp, g * KC + (c + 1))
                    nc.scalar.activation(hT[:, c, :], tp[c % 2][:, :], ACT.Copy).then_inc(s_hT, 1)
                act.wait_ge(s_stp, g + 1)
                act.wait_ge(s_setc, 2)
                nc.scalar.activation(st[:, :], stp[:, :], ACT.Identity, bias=bp[:, :]).then_inc(s_st, 1)
                act.wait_ge(s_rout, g * 16 + 16)
                act.wait_ge(s_st, g + 1)
                nc.scalar.activation(r_sb[:, :], st[0:H, :], ACT.Exp, scale=0.99).then_inc(s_r, 1)
                act.wait_ge(s_r, g + 1)
                act.dma_start(DR["r"][:, bass.ds(g * QB, QB)], r_sb[:, :]).then_inc(s_rout, 16)
                act.wait_ge(s_tq, g + 1)
                nc.scalar.activation(T["w"][:, bass.ds(g * SUB, SUB), :], tq[:, :, H:2 * H], ACT.Exp).then_inc(s_wv, 1)
                nc.scalar.activation(T["v"][:, bass.ds(g * SUB, SUB), :], tq[:, :, H:2 * H], ACT.Exp,
                                     scale=0.01).then_inc(s_wv, 1)
            act.wait_ge(s_rout, 16 * NB + 16)

        @block.tensor
        def _(pe):
            pe.wait_ge(s_w, 16 * 7)
            for c in range(KC):
                for k in range(KC):
                    mm = nc.tensor.matmul(setup[:, c * 2 * H:(c + 1) * 2 * H], wn[:, k, c * P:(c + 1) * P], pj[:, k, :],
                                          start=(k == 0), stop=(k == KC - 1), skip_group_check=True)
            mm.then_inc(s_set, 1)
            pe.wait_ge(s_setc, 1)
            for k in range(KC):
                mm = nc.tensor.matmul(setup[0:2 * H, 0:1], pj[:, k, :], bcol[:, k:k + 1],
                                      start=(k == 0), stop=(k == KC - 1))
            mm.then_inc(s_set, 1)
            pe.sem_inc(s_hT, 2)
            pe.sem_inc(s_v, 2)
            with pe.Fori(0, NB) as g:
                pe.wait_ge(s_h, g * SUB + 2 * SUB)
                for c in range(KC):
                    pe.wait_ge(s_hT, g * KC + (c + 1))
                    for s in range(SUB):
                        mm = nc.tensor.transpose(tp[c % 2][:, s * P:(s + 1) * P], h[:, s, c * P:(c + 1) * P],
                                                 T["identf"][:, :])
                    mm.then_inc(s_tp, 1)
                pe.wait_ge(s_hT, g * KC + KC + 2)
                for c in range(KC):
                    mm = nc.tensor.matmul(stp[:, :], wpj[:, c, :], hT[:, c, :], start=(c == 0), stop=(c == KC - 1))
                mm.then_inc(s_stp, 1)
                for s in range(SUB):
                    pe.wait_ge(s_v, g * (SUB + 1) + (1 if s < 2 else s + 1))
                    for c in range(KC):
                        mm = nc.tensor.matmul(vp[s % 2][:, :], hT[:, c, s * P:(s + 1) * P], wT[:, c, :],
                                              start=(c == 0), stop=(c == KC - 1))
                    mm.then_inc(s_vp, 1)
                wait_apart(pe, s_st, g + 1, s_passed)
                for s in range(SUB):
                    mm = nc.tensor.transpose(tq[:, s, :], st[:, s * P:(s + 1) * P], T["identf"][0:2 * H, 0:2 * H])
                mm.then_inc(s_tq, 1)
            pe.wait_ge(s_rank, SUB + NT)
            nc.tensor.transpose(amp[:, :], T["amax"][:, :], T["identf"][:, :]).then_inc(s_amp, 1)


def layer0_attention(nc, T, DR):
    TILES = 2 * HP * NT
    GROUPS = 4
    PER = NT // GROUPS
    with ExitStack() as ctx:
        def sb(name, shape, dt=F32):
            return ctx.enter_context(nc.sbuf_tensor(name, shape, dt))

        def pb(name, shape, dt=F32):
            return ctx.enter_context(nc.psum_tensor(name, shape, dt))

        def sem(name):
            return ctx.enter_context(nc.semaphore("b_" + name))

        A = sb("b_A", [P, NT, QB])
        R = sb("b_R", [P, H, QB])
        am = sb("b_am", [P, QB])
        G = sb("b_G", [P, G_RING, QB])
        PT = sb("b_P", [P, P_RING, QB])
        ones = sb("b_ones", [P, DEN])
        xg = sb("b_xg", [P, SUB, F])
        oT = sb("b_oT", [P, QB])
        dT = sb("b_dT", [P, QB])
        dsum = sb("b_dsum", [P, SUB, 2])
        rden = sb("b_rden", [P, SUB, 2])
        o = sb("b_o", [P, SUB, P])

        acc = [pb(f"b_acc{i}", [P, QB]) for i in range(2)]
        den = [pb(f"b_den{i}", [P, QB]) for i in range(2)]
        fin_o = pb("b_fin_o", [P, SUB, P])
        fin_d = pb("b_fin_d", [P, SUB, P])

        s_passed = sem("waits_passed")
        s_ones = sem("ones")
        s_am = sem("amax_in")
        s_R = [sem(f"r_in{i}") for i in range(HP)]
        s_A = [sem(f"adj_in{i}") for i in range(GROUPS)]
        s_sub = sem("adj_shifted")
        s_exp = sem("adj_exp")
        s_G = sem("g_ready")
        s_P = sem("p_ready")
        s_used = sem("p_used")
        s_copy = sem("acc_copied")
        s_fin = sem("fin_ready")
        s_chain = sem("vector_chain")
        s_done = sem("x1_part_done")
        s_x = sem("x_in")
        s_out = sem("x1_stored")

        block = ctx.enter_context(nc.Block())

        @block.sync
        def _(sp):
            with sp.Fori(0, NB) as nb:
                sp.wait_ge(s_sub, nb * NT + NT)
                sp.dma_start(am[:, :], DR["amax"][bass.ds(nb * QB, QB)].partition_broadcast(P)).then_inc(s_am, 16)

                def load_r(hp):
                    sp.wait_ge(s_G, nb * TILES + 2 * NT * (hp + 1))
                    for x in range(2):
                        src = DR["r"][2 * hp + x, bass.ds(nb * QB, QB)]
                        sp.dma_start(R[:, 2 * hp + x, :], src.partition_broadcast(P)).then_inc(s_R[hp], 16)

                for hp in range(HP - 1):
                    load_r(hp)
                for i in range(GROUPS):
                    sp.wait_ge(s_P, nb * TILES + 2 * (NT * (HP - 1) + PER * (i + 1)))
                    src = DR["adjT"][i * PER * P:(i + 1) * PER * P, bass.ds(nb * QB, QB)]
                    sp.dma_start(A[:, i * PER:(i + 1) * PER, :], src.rearrange("(m p) n -> p m n", p=P)).then_inc(s_A[i], 16)
                load_r(HP - 1)

        @block.gpsimd
        def _(pool):
            pool.memset(ones[:, :], 1.0).then_inc(s_ones, 1)
            with pool.Fori(0, NB) as nb:
                pool.dma_start(xg[:, :, :], DR["x"][bass.ds(nb * QB, QB), :].rearrange("(s p) f -> p s f", p=P)).then_inc(s_x, 16)
                wait_apart(pool, s_done, nb * HP + (HP + 1), s_passed)
                pool.dma_start(DR["x1"][bass.ds(nb * QB, QB), :].rearrange("(s p) f -> p s f", p=P), xg[:, :, :]).then_inc(s_out, 16)
                wait_apart(pool, s_out, nb * 16 + 16, s_passed)

        @block.scalar
        def _(act):
            act.sem_inc(s_G, CREDIT)

            def exp_adj(nb, mb):
                act.wait_ge(s_sub, nb * NT + (NT + mb + 1))
                nc.scalar.activation(A[:, mb, :], A[:, mb, :], ACT.Exp).then_inc(s_exp, 1)

            with act.Fori(0, NB) as nb:
                for mb in range(LEAD):
                    exp_adj(nb, mb)
                for hp in range(HP):
                    act.wait_ge(s_R[hp], nb * 32 + 32)
                    for mb in range(NT):
                        if hp == 0 and mb + LEAD < NT:
                            exp_adj(nb, mb + LEAD)
                        for x in range(2):
                            t = 2 * (hp * NT + mb) + x
                            act.wait_ge(s_P, nb * TILES + (CREDIT + t - G_RING + 1))
                            head = 2 * hp + x
                            nc.scalar.activation(G[:, t % G_RING, :], R[:, head, :], ACT.Relu,
                                                 bias=T["nv"][:, mb, head:head + 1],
                                                 scale=T["w"][:, mb, head:head + 1]).then_inc(s_G, 1)

        @block.vector
        def _(dve):
            dve.sem_inc(s_P, CREDIT)
            dve.sem_inc(s_sub, NT)

            def shift_adj(nb, mb):
                dve.wait_ge(s_A[mb // PER], nb * 16 + 16)
                ins = nc.vector.tensor_tensor(A[:, mb, :], A[:, mb, :], am[:, :], ALU.subtract)
                ins.then_inc(s_sub, 1)

            def copy_acc(nb, hp):
                dve.wait_ge(s_used, nb * (TILES // QUAD) + (P_RING // QUAD + (hp + 1) * 2 * NT // QUAD))
                nc.vector.tensor_copy(oT[:, :], acc[hp % 2][:, :]).then_inc(s_copy, 1)
                nc.vector.tensor_copy(dT[:, :], den[hp % 2][:, :]).then_inc(s_copy, 1)

            def finish(nb, hp):
                dve.wait_ge(s_fin, nb * HP + (hp + 1))
                view = fin_d[:, :, :].rearrange("p s (e j c) -> p s j e c", e=2, j=2)[:, :, :, :, 0]
                nc.vector.tensor_reduce(dsum[:, :, :], view, AX.X, ALU.add).then_inc(s_chain, 1)
                at = nb * (HP * 3) + hp * 3
                dve.wait_ge(s_chain, at + 1)
                nc.vector.reciprocal(rden[:, :, :], dsum[:, :, :]).then_inc(s_chain, 1)
                dve.wait_ge(s_chain, at + 2)
                nc.vector.tensor_tensor(o[:, :, :].rearrange("p s (j d) -> p s j d", j=2),
                                        fin_o[:, :, :].rearrange("p s (j d) -> p s j d", j=2),
                                        rden[:, :, :].unsqueeze(3).to_broadcast([P, SUB, 2, D]), ALU.mult).then_inc(s_chain, 1)
                dve.wait_ge(s_chain, at + 3)
                if hp == 0:
                    dve.wait_ge(s_x, nb * 16 + 16)
                cols = slice(hp * P, (hp + 1) * P)
                nc.vector.tensor_tensor(xg[:, :, cols], xg[:, :, cols], o[:, :, :], ALU.add).then_inc(s_done, 1)

            with dve.Fori(0, NB) as nb:
                dve.wait_ge(s_am, nb * 16 + 16)
                for mb in range(LEAD):
                    shift_adj(nb, mb)
                for hp in range(HP):
                    for mb in range(NT):
                        if hp == 0 and mb + LEAD < NT:
                            shift_adj(nb, mb + LEAD)
                        if hp == 0:
                            dve.wait_ge(s_exp, nb * NT + (mb + 1))
                        for x in range(2):
                            t = 2 * (hp * NT + mb) + x
                            if t % QUAD == 0:
                                dve.wait_ge(s_used, nb * (TILES // QUAD) + (t // QUAD + 1))
                            dve.wait_ge(s_G, nb * TILES + (CREDIT + t + 1))
                            nc.vector.scalar_tensor_tensor(out=PT[:, t % P_RING, :], in0=G[:, t % G_RING, :],
                                                           scalar=T["v"][:, mb, 2 * hp + x:2 * hp + x + 1], in1=A[:, mb, :],
                                                           op0=ALU.add, op1=ALU.mult).then_inc(s_P, 1)
                        if hp > 0 and mb == 4:
                            copy_acc(nb, hp - 1)
                        if hp > 0 and mb == 10:
                            finish(nb, hp - 1)
                copy_acc(nb, HP - 1)
                finish(nb, HP - 1)

        @block.tensor
        def _(pe):
            pe.wait_ge(s_ones, 1)
            pe.sem_inc(s_used, P_RING // QUAD)
            pe.sem_inc(s_copy, 4)
            pe.sem_inc(s_done, 1)

            def transposes(nb, hp):
                pe.wait_ge(s_copy, nb * (2 * HP) + (2 * hp + 6))
                pe.wait_ge(s_done, nb * HP + (hp + 1))
                for s in range(SUB):
                    nc.tensor.transpose(fin_o[:, s, :], oT[:, s * P:(s + 1) * P], T["identf"][:, :])
                for s in range(SUB):
                    mm = nc.tensor.transpose(fin_d[:, s, :], dT[:, s * P:(s + 1) * P], T["identf"][:, :])
                mm.then_inc(s_fin, 1)

            with pe.Fori(0, NB) as nb:
                for hp in range(HP):
                    pe.wait_ge(s_copy, nb * (2 * HP) + (2 * hp + 2))
                    for j in range(2 * NT // QUAD):
                        t0 = 2 * hp * NT + QUAD * j
                        for i in range(QUAD):
                            t = t0 + i
                            mb, x = (t // 2) % NT, t % 2
                            head = 2 * hp + x
                            pe.wait_ge(s_P, nb * TILES + (CREDIT + t + 1))
                            nc.tensor.matmul(acc[hp % 2][x * D:(x + 1) * D, :], T["V"][:, mb, head * D:(head + 1) * D],
                                             PT[:, t % P_RING, :], start=(mb == 0), stop=(mb == NT - 1))
                        for i in range(QUAD):
                            t = t0 + i
                            mm = nc.tensor.matmul(den[hp % 2][i * DEN:(i + 1) * DEN, :], ones[:, :], PT[:, t % P_RING, :],
                                                  start=(j == 0), stop=(j == 2 * NT // QUAD - 1), tile_position=(0, i * DEN))
                        mm.then_inc(s_used, 1)
                        if hp > 0 and j == 3:
                            transposes(nb, hp - 1)
                transposes(nb, HP - 1)


def layer1_project(nc, T, DR):
    RING = 4
    PAIRS = 2 * HP
    with ExitStack() as ctx:
        def sb(name, shape, dt=F32):
            return ctx.enter_context(nc.sbuf_tensor(name, shape, dt))

        def pb(name, shape, dt=F32):
            return ctx.enter_context(nc.psum_tensor(name, shape, dt))

        def sem(name):
            return ctx.enter_context(nc.semaphore("c_" + name))

        xg = sb("c_xg", [P, SUB, F])
        h = sb("c_h", [P, SUB, F])
        hT = sb("c_hT", [P, KC, QB])
        wq = sb("c_wq", [P, KC, F])
        wk = sb("c_wk", [P, KC, F])
        wv = sb("c_wv", [P, KC, F])
        stats = sb("c_stats", [P, SUB, 6])
        mv = sb("c_mv", [P, SUB, 2])
        std = sb("c_std", [P, SUB])
        rstd = sb("c_rstd", [P, SUB])
        nmr = sb("c_nmr", [P, SUB])
        eps = sb("c_eps", [P, 1])
        hi = sb("c_hi", [P, RING, QB], F16)
        lo = sb("c_lo", [P, RING, QB], F16)
        vt = sb("c_vt", [P, SUB, F])

        tp = [pb(f"c_tp{i}", [P, QB]) for i in range(2)]
        qp = [pb(f"c_qp{i}", [P, QB]) for i in range(2)]
        vp = [pb(f"c_vp{i}", [P, F]) for i in range(2)]

        s_passed = sem("waits_passed")
        s_w = sem("w_in")
        s_x = [sem(f"x_in{s}") for s in range(SUB)]
        s_chain = sem("vector_chain")
        s_eps = sem("eps")
        s_mv = sem("variance")
        s_std = sem("std")
        s_norm = sem("norm")
        s_h = sem("h")
        s_tp = sem("transposed")
        s_hT = sem("hT")
        s_qp = sem("qk_psum")
        s_hi = sem("hi")
        s_lo = sem("lo")
        s_qout = [sem(f"qk_stored{i}") for i in range(RING)]
        s_vp = sem("v_psum")
        s_v = sem("v_copied")
        s_vout = sem("v_stored")

        block = ctx.enter_context(nc.Block())

        @block.sync
        def _(sp):
            for w, name in ((wq, "Wq"), (wk, "Wk"), (wv, "Wv")):
                sp.dma_start(w[:, :, :], DR[name].rearrange("(c p) n -> p c n", p=P)).then_inc(s_w, 16)
            for i in range(RING):
                sp.sem_inc(s_qout[i], 32)
            sp.sem_inc(s_vout, 16)
            with sp.Fori(0, NB) as g:
                for j in range(PAIRS):
                    sp.wait_ge(s_lo, g * PAIRS + (j + 1))
                    row, i, to = (j % HP) * P, j % RING, "qk"[j // HP]
                    for half, tile in (("h", hi), ("l", lo)):
                        sp.dma_start(DR[to + half][row:row + P, bass.ds(g * QB, QB)], tile[:, i, :]).then_inc(s_qout[i], 16)
                sp.wait_ge(s_v, g * SUB + (SUB + 2))
                sp.dma_start(DR["v1"][bass.ds(g * QB, QB), :].rearrange("(s p) f -> p s f", p=P), vt[:, :, :]).then_inc(s_vout, 16)
            for i in range(RING):
                sp.wait_ge(s_qout[i], 32 * (NB * PAIRS // RING + 1))
            sp.wait_ge(s_vout, 16 * (NB + 1))

        @block.gpsimd
        def _(pool):
            pool.memset(eps[:, :], EPS).then_inc(s_eps, 1)
            pool.sem_inc(s_h, SUB)
            with pool.Fori(0, NB) as g:
                for s in range(SUB):
                    wait_apart(pool, s_h, g * SUB + (s + 1), s_passed)
                    pool.dma_start(xg[:, s, :], DR["x1"][bass.ds(g * QB + s * P, P), :]).then_inc(s_x[s], 16)

        @block.vector
        def _(dve):
            with dve.Fori(0, NB) as g:
                for s in range(SUB):
                    dve.wait_ge(s_x[s], g * 16 + 16)
                    nc.vector.bn_stats(stats[:, s, :], xg[:, s, :]).then_inc(s_chain, 1)
                wait_apart(dve, s_chain, g * (SUB + 1) + SUB, s_passed)
                for s in range(SUB):
                    nc.vector.bn_aggr(mv[:, s, :], stats[:, s, :]).then_inc(s_mv, 1)
                dve.wait_ge(s_std, g + 1)
                nc.vector.reciprocal(rstd[:, :], std[:, :]).then_inc(s_chain, 1)
                dve.wait_ge(s_chain, g * (SUB + 1) + (SUB + 1))
                nc.vector.scalar_tensor_tensor(out=nmr[:, :], in0=mv[:, :, 0], scalar=-1.0, in1=rstd[:, :],
                                               op0=ALU.mult, op1=ALU.mult).then_inc(s_norm, 1)
                for j in range(PAIRS):
                    dve.wait_ge(s_hi, g * PAIRS + (j + 1))
                    nc.vector.scalar_tensor_tensor(out=lo[:, j % RING, :], in0=qp[j % 2][:, :], scalar=QK_SCALE,
                                                   in1=hi[:, j % RING, :], op0=ALU.mult, op1=ALU.subtract).then_inc(s_lo, 1)
                dve.wait_ge(s_vout, g * 16 + 16)
                for s in range(SUB):
                    dve.wait_ge(s_vp, g * SUB + (s + 1))
                    nc.vector.tensor_copy(vt[:, s, :], vp[s % 2][:, :]).then_inc(s_v, 1)

        @block.scalar
        def _(act):
            act.wait_ge(s_eps, 1)
            with act.Fori(0, NB) as g:
                act.wait_ge(s_mv, g * SUB + SUB)
                nc.scalar.activation(std[:, :], mv[:, :, 1], ACT.Sqrt, bias=eps[:, :]).then_inc(s_std, 1)
                act.wait_ge(s_norm, g + 1)
                for s in range(SUB):
                    nc.scalar.activation(h[:, s, :], xg[:, s, :], ACT.Relu, bias=nmr[:, s:s + 1],
                                         scale=rstd[:, s:s + 1]).then_inc(s_h, 1)
                for c in range(KC):
                    act.wait_ge(s_tp, g * KC + (c + 1))
                    nc.scalar.activation(hT[:, c, :], tp[c % 2][:, :], ACT.Copy).then_inc(s_hT, 1)
                for j in range(PAIRS):
                    act.wait_ge(s_qout[j % RING], g * (32 * PAIRS // RING) + 32 * (j // RING + 1))
                    act.wait_ge(s_qp, g * PAIRS + (j + 1))
                    nc.scalar.activation(hi[:, j % RING, :], qp[j % 2][:, :], ACT.Copy, scale=QK_SCALE).then_inc(s_hi, 1)

        @block.tensor
        def _(pe):
            pe.wait_ge(s_w, 16 * 3)
            pe.sem_inc(s_hT, 2)
            pe.sem_inc(s_v, 2)
            with pe.Fori(0, NB) as g:
                pe.wait_ge(s_h, g * SUB + 2 * SUB)
                for c in range(KC):
                    pe.wait_ge(s_hT, g * KC + (c + 1))
                    for s in range(SUB):
                        mm = nc.tensor.transpose(tp[c % 2][:, s * P:(s + 1) * P], h[:, s, c * P:(c + 1) * P],
                                                 T["identf"][:, :])
                    mm.then_inc(s_tp, 1)
                pe.wait_ge(s_hT, g * KC + KC + 2)
                for j in range(PAIRS):
                    if j >= 2:
                        pe.wait_ge(s_lo, g * PAIRS + (j - 1))
                    w, col = (wq, wk)[j // HP], (j % HP) * P
                    for c in range(KC):
                        mm = nc.tensor.matmul(qp[j % 2][:, :], w[:, c, col:col + P], hT[:, c, :],
                                              start=(c == 0), stop=(c == KC - 1))
                    mm.then_inc(s_qp, 1)
                for s in range(SUB):
                    pe.wait_ge(s_v, g * SUB + (s + 1))
                    for c in range(KC):
                        mm = nc.tensor.matmul(vp[s % 2][:, :], hT[:, c, s * P:(s + 1) * P], wv[:, c, :],
                                              start=(c == 0), stop=(c == KC - 1))
                    mm.then_inc(s_vp, 1)
                pe.wait_ge(s_lo, g * PAIRS + PAIRS)


def layer1_attention(nc, T, DR):
    TILES = 2 * HP * NT
    PAIR = 2 * NT
    QUADS = PAIR // QUAD
    GROUPS = 4
    PER = NT // GROUPS
    MC = N // QB
    GUARDS = 2 * SUB * MC
    CW = 1024
    CH = N // CW
    LEAD1 = 2
    M0_USES = NT + 2 * HP
    M1_USES = HP + SUB
    ROW_OPS = 2 * CH + 3
    MASK_OPS = 1 + SUB * ROW_OPS
    FIRST_G, LAST_G = 4, 30
    EXP_SCALE = 1.0 / (QK_SCALE * QK_SCALE * D ** 0.5)
    MASK_SCALE = 1e16 / EXP_SCALE
    MASK_FLOOR = -32768.0 / EXP_SCALE

    def guards_of(mb):
        def upto(step):
            return GUARDS * min(max(step - FIRST_G + 1, 0), LAST_G - FIRST_G + 1) // (LAST_G - FIRST_G + 1)
        return range(upto(mb - 1), upto(mb))

    def crow_of(mb):
        for x in range(2):
            last = next(m for m in range(NT) if (x + 1) * GUARDS // 2 - 1 in guards_of(m))
            if mb == min(last + 2, NT - 1):
                return x
        return None

    m0_index, use = {}, 0
    for hp_ in range(HP):
        for mb_ in range(NT):
            if hp_ == 0:
                for m in ([*range(LEAD1 + 1)] if mb_ == 0 else [mb_ + LEAD1]):
                    if m < NT:
                        m0_index["mask", m] = use
                        use += 1
            if crow_of(mb_) is not None:
                m0_index["crow", hp_, crow_of(mb_)] = use
                use += 1
    assert use == M0_USES

    with ExitStack() as ctx:
        def sb(name, shape, dt=F32):
            return ctx.enter_context(nc.sbuf_tensor(name, shape, dt))

        def pb(name, shape, dt=F32):
            return ctx.enter_context(nc.psum_tensor(name, shape, dt))

        def sem(name):
            return ctx.enter_context(nc.semaphore("d_" + name))

        KA = sb("d_KA", [P, 2, 2, N], F16)
        KB = sb("d_KB", [P, 2, N], F16)
        V = sb("d_V", [P, NT, P])
        QA = sb("d_QA", [P, 2, 2, QB], F16)
        QL = sb("d_QL", [P, 2, 2, QB], F16)
        MR = sb("d_MR", [P, SUB, N], BF16)
        MT = sb("d_MT", [P, NT, QB], BF16)
        stage = sb("d_stage", [P, 2, CW])
        dblk = sb("d_dblk", [P, SUB, P])
        brow = sb("d_brow", [P, SUB])
        PT = sb("d_P", [P, P_RING, QB])
        oN = sb("d_oN", [P, HP, QB])
        wo = sb("d_wo", [P, HP, F])
        xr = sb("d_xr", [P, SUB, F])
        rb = sb("d_rb", [P, QB])
        dT = sb("d_dT", [P, QB])
        junk = sb("d_junk", [P, 2, QB], BF16)
        gm = sb("d_gm", [P, SUB, MC])
        cm = sb("d_cm", [P, SUB])
        dg = sb("d_dg", [P, SUB, P], F16)
        ones = sb("d_ones", [P, DEN])
        selc = sb("d_selc", [P, P], F16)
        seld = sb("d_seld", [P, P])
        idh = sb("d_idh", [P, P], F16)

        sc = [pb(f"d_sc{i}", [P, QB]) for i in range(2)]
        gd = [pb(f"d_gd{i}", [P, QB]) for i in range(2)]
        acc = pb("d_acc", [P, QB])
        den = pb("d_den", [P, QB])
        misc0 = pb("d_misc0", [P, QB])
        misc1 = pb("d_misc1", [P, QB])
        misc0h = misc0[:, :].bitcast(BF16)

        s_passed = sem("waits_passed")
        s_const = sem("const_in")
        s_set = sem("constants_set")
        s_KA = [[sem(f"ka_in{i}{x}") for x in range(2)] for i in range(2)]
        s_Q = [sem(f"q_in{i}") for i in range(2)]
        s_KB = [sem(f"kb_in{i}") for i in range(GROUPS)]
        s_V = [sem(f"v_in{i}") for i in range(GROUPS)]
        s_stage = [sem(f"adj_in{i}") for i in range(2)]
        s_dblk = sem("adj_diagonal_in")
        s_mk = sem("mask_made")
        s_mtp = sem("mask_transposed")
        s_m0 = sem("misc0_read")
        s_S = sem("scores")
        s_P = sem("p_ready")
        s_used = sem("p_used")
        s_G = sem("guard_scores")
        s_gm = sem("guard_max")
        s_cm = sem("row_max")
        s_dg = sem("row_max_diagonal")
        s_crow = sem("max_row")
        s_ac = sem("acc_copied")
        s_dc = sem("den_copied")
        s_m1w = sem("misc1_written")
        s_m1 = sem("misc1_read")
        s_rb = sem("reciprocal")
        s_oN = sem("normalised")
        s_x = sem("x1_in")
        s_out = sem("out_stored")

        block = ctx.enter_context(nc.Block())

        def load_ka(sp, par, hp):
            for x in range(2):
                row = (2 * hp + x) * D
                sp.dma_start(KA[0:D, par, x, :], DR["kh"][row:row + D, :]).then_inc(s_KA[par][x], 16)
                sp.dma_start(KA[D:P, par, x, :], DR["kl"][row:row + D, :]).then_inc(s_KA[par][x], 16)

        def load_q(sp, par, hp, nb):
            for x in range(2):
                row = (2 * hp + x) * D
                for half in range(2):
                    sp.dma_start(QA[half * D:(half + 1) * D, par, x, :], DR["qh"][row:row + D, bass.ds(nb * QB, QB)]).then_inc(s_Q[par], 16)
                sp.dma_start(QL[0:D, par, x, :], DR["ql"][row:row + D, bass.ds(nb * QB, QB)]).then_inc(s_Q[par], 16)

        def load_kb(sp, hp, i):
            cols = slice(i * PER * P, (i + 1) * PER * P)
            for x in range(2):
                row = (2 * hp + x) * D
                sp.dma_start(KB[0:D, x, cols], DR["kh"][row:row + D, cols]).then_inc(s_KB[i], 16)

        def load_v(sp, hp, i):
            rows = slice(i * PER * P, (i + 1) * PER * P)
            sp.dma_start(V[:, i * PER:(i + 1) * PER, :],
                         DR["v1"][rows, hp * P:(hp + 1) * P].rearrange("(m p) n -> p m n", p=P)).then_inc(s_V[i], 16)

        @block.sync
        def _(sp):
            for tile, name in ((selc, "selc"), (seld, "seld"), (idh, "idh")):
                sp.dma_start(tile[:, :], DR[name]).then_inc(s_const, 16)
            sp.dma_start(wo[:, :, :], DR["Wo"].rearrange("(c p) n -> p c n", p=P)).then_inc(s_const, 16)
            load_ka(sp, 0, 0)
            load_q(sp, 0, 0, 0)
            for i in range(GROUPS):
                load_kb(sp, 0, i)
                load_v(sp, 0, i)
            with sp.Fori(0, NB) as nb:
                for hp in range(HP):
                    nxt, par = (hp + 1) % HP, (hp + 1) % 2
                    sp.wait_ge(s_S, nb * TILES + (hp * PAIR + CREDIT))
                    load_ka(sp, par, nxt)
                    load_q(sp, par, nxt, nb if hp < HP - 1 else (nb + 1) % NB)
                    for i in range(GROUPS):
                        sp.wait_ge(s_S, nb * TILES + (hp * PAIR + 2 * PER * (i + 1) + CREDIT))
                        load_kb(sp, nxt, i)
                        sp.wait_ge(s_used, nb * (HP * QUADS) + (hp * QUADS + (i + 1) * 2 * PER // QUAD + P_RING // QUAD))
                        load_v(sp, nxt, i)
            for par in range(2):
                for x in range(2):
                    sp.wait_ge(s_KA[par][x], 32 * (2 * NB + 1 - par))
                sp.wait_ge(s_Q[par], 96 * (2 * NB + 1 - par))
            for i in range(GROUPS):
                sp.wait_ge(s_KB[i], 32 * (HP * NB + 1))
                sp.wait_ge(s_V[i], 16 * (HP * NB + 1))

        @block.gpsimd
        def _(pool):
            def load_adj(nb, ahead):
                for s in range(SUB):
                    pool.dma_start(dblk[:, s, :], DR["adj"][bass.ds(nb * QB + s * P, P), bass.ds(nb * QB + s * P, P)]).then_inc(s_dblk, 16)
                for ci in range(SUB * CH):
                    s, c = divmod(ci, CH)
                    if ahead is not None or ci >= 2:
                        back = ci - 2
                        done = 1 + ROW_OPS * (back // CH) + 2 * (back % CH) + 2 if back >= 0 else \
                            1 + ROW_OPS * (SUB - 1) + 2 * (CH + back) + 2 - MASK_OPS
                        wait_apart(pool, s_mk, done if ahead is None else ahead * MASK_OPS + (MASK_OPS + done), s_passed)
                    pool.dma_start(stage[:, ci % 2, :], DR["adj"][bass.ds(nb * QB + s * P, P), c * CW:(c + 1) * CW]).then_inc(s_stage[ci % 2], 16)

            load_adj(0, None)
            with pool.Fori(0, NB) as nb:
                pool.dma_start(xr[:, :, :], DR["x1"][bass.ds(nb * QB, QB), :].rearrange("(s p) f -> p s f", p=P)).then_inc(s_x, 16)
                wait_apart(pool, s_mk, nb * MASK_OPS + MASK_OPS, s_passed)
                load_adj((nb + 1) % NB, nb)
                wait_apart(pool, s_m1, nb * M1_USES + (M1_USES + 1), s_passed)
                pool.dma_start(DR["out"][bass.ds(nb * QB, QB), :].rearrange("(s p) f -> p s f", p=P), xr[:, :, :]).then_inc(s_out, 16)
                wait_apart(pool, s_out, nb * 16 + 16, s_passed)

        @block.scalar
        def _(act):
            act.wait_ge(s_const, 16 * 4)
            act.sem_inc(s_P, CREDIT)
            act.sem_inc(s_ac, 1)

            def copy_crow(count, par, x):
                act.wait_ge(s_crow, count)
                nc.scalar.activation(QL[D:P, par, x, :], misc0[D:P, :], ACT.Copy).then_inc(s_m0, 1)

            def copy_acc(nb, hp):
                act.wait_ge(s_used, nb * (HP * QUADS) + ((hp + 1) * QUADS + P_RING // QUAD))
                if hp == 0:
                    act.wait_ge(s_m1w, nb * M1_USES + 1)
                nc.scalar.activation(oN[:, hp, :], acc[:, :], ACT.Copy).then_inc(s_ac, 1)

            for x in range(2):
                copy_crow(x + 1, 0, x)
            with act.Fori(0, NB) as nb:
                for hp in range(HP):
                    for mb in range(NT):
                        if hp == 0:
                            for m in ([*range(LEAD1 + 1)] if mb == 0 else [mb + LEAD1]):
                                if m < NT:
                                    act.wait_ge(s_mtp, nb * NT + (m + 1))
                                    nc.scalar.activation(MT[:, m, :], misc0h[:, 0:QB], ACT.Copy).then_inc(s_m0, 1)
                        for x in range(2):
                            t = hp * PAIR + 2 * mb + x
                            if t % QUAD == 0:
                                act.wait_ge(s_used, nb * (HP * QUADS) + (t // QUAD + 1))
                            act.wait_ge(s_S, nb * TILES + (CREDIT + t + 1))
                            nc.scalar.activation(PT[:, t % P_RING, :], sc[t % 2][:, :], ACT.Exp, scale=EXP_SCALE).then_inc(s_P, 1)
                        if crow_of(mb) is not None:
                            copy_crow(nb * (2 * HP) + (2 * hp + crow_of(mb) + 3), (hp + 1) % 2, crow_of(mb))
                        if hp > 0 and mb == 2:
                            copy_acc(nb, hp - 1)
                copy_acc(nb, HP - 1)

        @block.vector
        def _(dve):
            dve.wait_ge(s_const, 16 * 4)
            nc.vector.memset(ones[:, :], 1.0).then_inc(s_set, 1)
            nc.vector.memset(KB[D:P, :, :], 0.0).then_inc(s_set, 1)
            dve.wait_ge(s_set, 2)
            nc.vector.memset(KB[D:D + 1, :, :], C_ROW).then_inc(s_set, 1)
            dve.sem_inc(s_dc, 1)
            dve.sem_inc(s_m1, 1)

            def mask_setup(run, nb):
                nc.vector.tensor_scalar(brow[:, :], T["amax"][:, bass.ds(nb * SUB, SUB)], 1.0, -1.0,
                                        ALU.max, ALU.add).then_inc(s_mk, 1)

            def mask_row(run, nb, s):
                at = run * MASK_OPS + (1 + s * ROW_OPS)
                for c in range(CH):
                    ci = s * CH + c
                    dve.wait_ge(s_stage[ci % 2], run * (16 * SUB * CH // 2) + 16 * (ci // 2 + 1))
                    dve.wait_ge(s_mk, at + 2 * c)
                    nc.vector.tensor_scalar(stage[:, ci % 2, :], stage[:, ci % 2, :], -1.0, brow[:, s:s + 1],
                                            ALU.add, ALU.subtract).then_inc(s_mk, 1)
                    dve.wait_ge(s_mk, at + (2 * c + 1))
                    nc.vector.tensor_scalar(MR[:, s, c * CW:(c + 1) * CW], stage[:, ci % 2, :], MASK_SCALE, MASK_FLOOR,
                                            ALU.mult, ALU.max).then_inc(s_mk, 1)
                dve.wait_ge(s_dblk, run * (16 * SUB) + 16 * SUB)
                at = at + 2 * CH
                nc.vector.tensor_tensor(dblk[:, s, :], dblk[:, s, :], T["identf"][:, :], ALU.max).then_inc(s_mk, 1)
                dve.wait_ge(s_mk, at + 1)
                nc.vector.tensor_scalar(dblk[:, s, :], dblk[:, s, :], -1.0, brow[:, s:s + 1],
                                        ALU.add, ALU.subtract).then_inc(s_mk, 1)
                dve.wait_ge(s_mk, at + 2)
                nc.vector.tensor_scalar(MR[:, s, bass.ds(nb * QB + s * P, P)], dblk[:, s, :], MASK_SCALE, MASK_FLOOR,
                                        ALU.mult, ALU.max).then_inc(s_mk, 1)

            def guard(it, gi):
                x, s, c = gi // (SUB * MC), gi // MC % SUB, gi % MC
                if gi >= 2 or not isinstance(it, int):
                    dve.wait_ge(s_gm, it * GUARDS + (gi - 1))
                wait_apart(dve, s_G, it * GUARDS + (gi + 1), s_passed)
                nc.vector.tensor_tensor_reduce(out=junk[:, gi % 2, :], in0=gd[gi % 2][:, :], in1=MR[:, s, c * QB:(c + 1) * QB],
                                               scale=1.0, scalar=-3.0e38, op0=ALU.add, op1=ALU.max,
                                               accum_out=gm[:, s, c:c + 1]).then_inc(s_gm, 1)
                if c == MC - 1:
                    n = x * SUB + s
                    dve.wait_ge(s_gm, it * GUARDS + (gi + 1))
                    nc.vector.reduce_max(cm[:, s:s + 1], gm[:, s, :], AX.X).then_inc(s_cm, 1)
                    dve.wait_ge(s_cm, it * (2 * SUB) + (n + 1))
                    if s == 0 and not (isinstance(it, int) and x == 0):
                        dve.wait_ge(s_crow, it * 2 + x)
                    nc.vector.tensor_scalar(dg[:, s, :], idh[:, :], cm[:, s:s + 1], -1.0 / C_ROW,
                                            ALU.mult, ALU.mult).then_inc(s_dg, 1)

            def copy_den(nb, hp):
                dve.wait_ge(s_used, nb * (HP * QUADS) + ((hp + 1) * QUADS + P_RING // QUAD))
                nc.vector.tensor_copy(dT[:, :], den[:, :]).then_inc(s_dc, 1)

            def normalise(nb, hp):
                dve.wait_ge(s_m1w, nb * M1_USES + (hp + 2))
                nc.vector.reciprocal(rb[:, :], misc1[:, :]).then_inc(s_m1, 1)
                dve.wait_ge(s_m1, nb * M1_USES + (hp + 2))
                dve.wait_ge(s_ac, nb * HP + (hp + 2))
                nc.vector.tensor_tensor(oN[:, hp, :], oN[:, hp, :], rb[:, :], ALU.mult).then_inc(s_oN, 1)

            mask_setup(0, 0)
            for s in range(SUB):
                mask_row(0, 0, s)
            dve.wait_ge(s_mk, MASK_OPS)
            for gi in range(GUARDS):
                guard(0, gi)
            with dve.Fori(0, NB) as nb:
                for hp in range(HP):
                    for mb in range(NT):
                        for gi in guards_of(mb):
                            guard(nb * HP + (hp + 1), gi)
                        if hp > 0 and mb == 2:
                            copy_den(nb, hp - 1)
                        if hp > 0 and mb == 6:
                            normalise(nb, hp - 1)
                        if hp == HP - 2:
                            for s in range(SUB - 1):
                                if GUARDS // 2 + (s + 1) * MC - 1 in guards_of(mb):
                                    if s == 0:
                                        dve.wait_ge(s_mtp, nb * NT + NT)
                                        mask_setup(nb + 1, (nb + 1) % NB)
                                        dve.wait_ge(s_mk, nb * MASK_OPS + (MASK_OPS + 1))
                                    mask_row(nb + 1, (nb + 1) % NB, s)
                        if hp == HP - 1 and mb == 0:
                            mask_row(nb + 1, (nb + 1) % NB, SUB - 1)
                            dve.wait_ge(s_mk, nb * MASK_OPS + 2 * MASK_OPS)
                copy_den(nb, HP - 1)
                normalise(nb, HP - 1)
                dve.wait_ge(s_x, nb * 16 + 16)
                for s in range(SUB):
                    dve.wait_ge(s_m1w, nb * M1_USES + (HP + s + 2))
                    nc.vector.tensor_tensor(xr[:, s, :], misc1[:, :], xr[:, s, :], ALU.add).then_inc(s_m1, 1)

        @block.tensor
        def _(pe):
            pe.wait_ge(s_const, 16 * 4)
            pe.wait_ge(s_set, 3)
            pe.sem_inc(s_S, CREDIT)
            pe.sem_inc(s_used, P_RING // QUAD)
            pe.sem_inc(s_m1w, 1)

            def guard(it, par, gi, count=None):
                x, s, c = gi // (SUB * MC), gi // MC % SUB, gi % MC
                if s == 0 and c == 0:
                    if x == 0:
                        pe.wait_ge(s_Q[par], count * 96 + 96)
                    pe.wait_ge(s_KA[par][x], count * 32 + 32)
                if gi >= 2 or not isinstance(it, int):
                    pe.wait_ge(s_gm, it * GUARDS + (gi - 1))
                nc.tensor.matmul(gd[gi % 2][:, :], QA[:, par, x, s * P:(s + 1) * P], KA[:, par, x, c * QB:(c + 1) * QB],
                                 start=True, stop=True).then_inc(s_G, 1)

            def crow(it, x, wait):
                pe.wait_ge(s_dg, it * (2 * SUB) + SUB * (x + 1))
                if wait is not None:
                    pe.wait_ge(s_m0, wait)
                for s in range(SUB):
                    mm = nc.tensor.matmul(misc0[:, s * P:(s + 1) * P], selc[:, :], dg[:, s, :], start=True, stop=True)
                mm.then_inc(s_crow, 1)

            def scores(nb, hp, mb, x):
                par, t = hp % 2, hp * PAIR + 2 * mb + x
                pe.wait_ge(s_P, nb * TILES + (CREDIT + t - 1))
                bank = sc[t % 2][:, :]
                nc.tensor.matmul(bank, KA[:, par, x, mb * P:(mb + 1) * P], QA[:, par, x, :], start=True, stop=False)
                nc.tensor.matmul(bank, KB[:, x, mb * P:(mb + 1) * P], QL[:, par, x, :], start=False, stop=False)
                nc.tensor.matmul(bank, T["identb"][:, :], MT[:, mb, :], start=False, stop=True).then_inc(s_S, 1)

            def products(nb, hp, q):
                t0 = hp * PAIR + q * QUAD
                if q == 0:
                    pe.wait_ge(s_ac, nb * HP + (hp + 1))
                    pe.wait_ge(s_dc, nb * HP + (hp + 1))
                if q % (QUADS // GROUPS) == 0:
                    pe.wait_ge(s_V[q // (QUADS // GROUPS)], nb * (16 * HP) + 16 * (hp + 1))
                for i in range(QUAD):
                    t = t0 + i
                    mb, x = (t // 2) % NT, t % 2
                    pe.wait_ge(s_P, nb * TILES + (CREDIT + t + 1))
                    nc.tensor.matmul(acc[x * D:(x + 1) * D, :], V[:, mb, x * D:(x + 1) * D], PT[:, t % P_RING, :],
                                     start=(mb == 0), stop=(mb == NT - 1))
                for i in range(QUAD):
                    mm = nc.tensor.matmul(den[i * DEN:(i + 1) * DEN, :], ones[:, :], PT[:, (t0 + i) % P_RING, :],
                                          start=(q == 0), stop=(q == QUADS - 1), tile_position=(0, i * DEN))
                mm.then_inc(s_used, 1)

            def spread_den(nb, hp):
                pe.wait_ge(s_dc, nb * HP + (hp + 2))
                pe.wait_ge(s_m1, nb * M1_USES + (hp + 1))
                nc.tensor.matmul(misc1[:, :], seld[:, :], dT[:, :], start=True, stop=True).then_inc(s_m1w, 1)

            for gi in range(GUARDS):
                guard(0, 0, gi, 0)
                if gi == GUARDS // 2 + 2:
                    crow(0, 0, None)
            crow(0, 1, 1)
            with pe.Fori(0, NB) as nb:
                base = nb * M0_USES
                for hp in range(HP):
                    for mb in range(NT):
                        if hp == 0:
                            if mb == 0:
                                pe.wait_ge(s_mk, nb * MASK_OPS + MASK_OPS)
                            for m in ([*range(LEAD1 + 1)] if mb == 0 else [mb + LEAD1]):
                                if m < NT:
                                    pe.wait_ge(s_m0, base + (m0_index["mask", m] + 2))
                                    for s in range(SUB):
                                        mm = nc.tensor.transpose(misc0h[:, s * P:(s + 1) * P], MR[:, s, m * P:(m + 1) * P],
                                                                 T["identb"][:, :])
                                    mm.then_inc(s_mtp, 1)
                            pe.wait_ge(s_m0, base + (m0_index["mask", mb] + 3))
                        if mb == 0:
                            count = nb * 2 + hp // 2
                            pe.wait_ge(s_Q[hp % 2], count * 96 + 96)
                            for x in range(2):
                                pe.wait_ge(s_KA[hp % 2][x], count * 32 + 32)
                            if hp:
                                pe.wait_ge(s_m0, base + (m0_index["crow", hp - 1, 1] + 3))
                        if mb % PER == 0:
                            pe.wait_ge(s_KB[mb // PER], nb * (32 * HP) + 32 * (hp + 1))
                        for x in range(2):
                            scores(nb, hp, mb, x)
                        for gi in guards_of(mb):
                            guard(nb * HP + (hp + 1), (hp + 1) % 2, gi, nb * 2 + (hp + 1) // 2)
                        if crow_of(mb) is not None:
                            x = crow_of(mb)
                            crow(nb * HP + (hp + 1), x, base + (m0_index["crow", hp, x] + 2))
                        if mb % 2 == 1:
                            if mb > 1:
                                products(nb, hp, mb // 2 - 1)
                            elif hp:
                                products(nb, hp - 1, QUADS - 1)
                        if hp and mb == 5:
                            spread_den(nb, hp - 1)
                products(nb, HP - 1, QUADS - 1)
                spread_den(nb, HP - 1)
                pe.wait_ge(s_oN, nb * HP + HP)
                for s in range(SUB):
                    pe.wait_ge(s_m1, nb * M1_USES + (HP + s + 1))
                    for c in range(HP):
                        mm = nc.tensor.matmul(misc1[:, :], oN[:, c, s * P:(s + 1) * P], wo[:, c, :],
                                              start=(c == 0), stop=(c == HP - 1))
                    mm.then_inc(s_m1w, 1)


def build(nc, DR):
    with ExitStack() as ctx:
        def sb(name, shape, dt=F32):
            return ctx.enter_context(nc.sbuf_tensor(name, shape, dt))

        T = {
            "identf": sb("identf", [P, P]), "identb": sb("identb", [P, P], BF16),
            "amax": sb("amax", [P, NT]),
        }
        with ExitStack() as layer0:
            def sb0(name, shape, dt=F32):
                return layer0.enter_context(nc.sbuf_tensor(name, shape, dt))

            T["V"] = sb0("V0", [P, NT, F])
            T["w"], T["v"], T["nv"] = (sb0(x, [P, NT, H]) for x in ("w", "v", "nv"))
            layer0_project(nc, T, DR)
            layer0_attention(nc, T, DR)
        layer1_project(nc, T, DR)
        layer1_attention(nc, T, DR)


_SCRATCH = [("amax", (N,), F32), ("r", (H, N), F32), ("x1", (N, F), F32), ("v1", (N, F), F32),
            ("qh", (F, N), F16), ("ql", (F, N), F16), ("kh", (F, N), F16), ("kl", (F, N), F16)]


def kernel(**inputs):
    import numpy as np
    import concourse.bacc as bacc
    from concourse.bass_utils import run_bass_kernel_spmd

    a = {k: np.asarray(v) for k, v in inputs.items()}
    proj = np.zeros((F, 2 * H), np.float32)
    for hd in range(H):
        proj[hd * D:(hd + 1) * D, hd] = a["L0_gnn_src_proj"][0, hd]
        proj[hd * D:(hd + 1) * D, H + hd] = a["L0_gnn_trg_proj"][0, hd]
    arrays = {
        "x": a["x"], "adj": a["adj"], "adjT": a["adj"].T, "W0": a["L0_gnn_W"], "W0T": a["L0_gnn_W"].T,
        "b": a["L0_gnn_b"], "bcol": a["L0_gnn_b"].reshape(KC, P).T, "proj": proj,
        "Wk": a["L1_gnn_Wks"].transpose(1, 0, 2).reshape(F, F), "Wq": a["L1_gnn_Wqs"].transpose(1, 0, 2).reshape(F, F),
        "Wv": a["L1_gnn_Wvs"].transpose(1, 0, 2).reshape(F, F), "Wo": a["L1_gnn_Wo"].reshape(F, F),
        "selc": np.eye(1, P, D, dtype=np.float16).repeat(P, 0),
        "seld": np.eye(P, dtype=np.float32)[[0, 32]].repeat(D, 0).T + np.eye(P, dtype=np.float32)[[64, 96]].repeat(D, 0).T,
        "idh": np.eye(P, dtype=np.float16),
        "identf": np.eye(P, dtype=np.float32), "identb": np.eye(P, dtype=np.float32).astype(mybir.dt.np(BF16)),
    }
    arrays = {f"in_{k}": np.ascontiguousarray(v) for k, v in arrays.items()}
    nc = bacc.Bacc("TRN2", target_bir_lowering=False, num_devices=1)
    DR = {k[3:]: nc.dram_tensor(k, v.shape, mybir.dt.from_np(v.dtype), kind="ExternalInput").ap() for k, v in arrays.items()}
    DR |= {k: nc.dram_tensor(f"scratch_{k}", shape, dt, kind="Internal").ap() for k, shape, dt in _SCRATCH}
    DR["out"] = nc.dram_tensor("out_dram", (N, F), F32, kind="ExternalOutput").ap()
    build(nc, DR)
    return run_bass_kernel_spmd(nc, [arrays], core_ids=[0]).results[0]["out_dram"]
```

```python
import math
from contextlib import ExitStack

import concourse.bass as bass
from concourse import mybir

F32 = mybir.dt.float32
F16 = mybir.dt.float16
BF16 = mybir.dt.bfloat16
ALU = mybir.AluOpType
ACT = mybir.ActivationFunctionType
AX = mybir.AxisListType

P = 128
N = 4096
F = 512
H = 8
D = 64
HP = H // 2
NT = N // P
KC = F // P
QB = 512
NB = N // QB
SUB = QB // P
EPS = 1e-5

G_RING = 8
P_RING = 8
DEN = 32
QUAD = P // DEN
QK_SCALE = 256.0
C_ROW = 4096.0
CREDIT = 2 * HP * NT


def wait_apart(eng, sem, value, passed):
    eng.wait_ge(sem, value)
    eng.sem_inc(passed, 1)


def layer0_project(nc, T, DR):
    with ExitStack() as ctx:
        def sb(name, shape, dt=F32):
            return ctx.enter_context(nc.sbuf_tensor(name, shape, dt))

        def pb(name, shape, dt=F32):
            return ctx.enter_context(nc.psum_tensor(name, shape, dt))

        def sem(name):
            return ctx.enter_context(nc.semaphore("a_" + name))

        rows = [sb(f"a_rows{s}", [P, N]) for s in range(SUB)]
        xg = sb("a_xg", [P, SUB, F])
        h = sb("a_h", [P, SUB, F])
        hT = sb("a_hT", [P, KC, QB])
        wT = sb("a_wT", [P, KC, F])
        wn = sb("a_wn", [P, KC, F])
        pj = sb("a_pj", [P, KC, 2 * H])
        wpj = sb("a_wpj", [P, KC, 2 * H])
        bcol = sb("a_bcol", [P, KC])
        bias = sb("a_bias", [P, F])
        bp = sb("a_bp", [2 * H, 1])
        stats = sb("a_stats", [P, SUB, 6])
        mv = sb("a_mv", [P, SUB, 2])
        std = sb("a_std", [P, SUB])
        rstd = sb("a_rstd", [P, SUB])
        nmr = sb("a_nmr", [P, SUB])
        eps = sb("a_eps", [P, 1])
        st = sb("a_st", [2 * H, QB])
        r_sb = sb("a_r", [H, QB])
        am_row = sb("a_am_row", [NT, P])

        tp = [pb(f"a_tp{i}", [P, QB]) for i in range(2)]
        vp = [pb(f"a_vp{i}", [P, F]) for i in range(2)]
        stp = pb("a_stp", [2 * H, QB])
        tq = pb("a_tq", [P, SUB, 2 * H])
        setup = pb("a_setup", [P, KC * 2 * H])
        amp = pb("a_amp", [NT, P])

        s_passed = sem("waits_passed")
        s_w = sem("w_in")
        s_row = [sem(f"row_in{s}") for s in range(SUB)]
        s_x = [sem(f"x_in{s}") for s in range(SUB)]
        s_rank = sem("row_ranked")
        s_chain = sem("vector_chain")
        s_eps = sem("eps")
        s_mv = sem("variance")
        s_std = sem("std")
        s_norm = sem("norm")
        s_h = sem("h")
        s_tp = sem("transposed")
        s_hT = sem("hT")
        s_set = sem("projected_weights")
        s_setc = sem("projected_weights_copied")
        s_stp = sem("st_psum")
        s_st = sem("st")
        s_tq = sem("t_columns")
        s_wv = sem("wv")
        s_r = sem("r")
        s_rout = sem("r_stored")
        s_vp = sem("v_psum")
        s_v = sem("v_done")
        s_amp = sem("amax_transposed")
        s_am = sem("amax_row")
        s_amout = sem("amax_stored")

        block = ctx.enter_context(nc.Block())

        @block.sync
        def _(sp):
            sp.dma_start(T["identf"][:, :], DR["identf"]).then_inc(s_w, 16)
            sp.dma_start(T["identb"][:, :], DR["identb"]).then_inc(s_w, 16)
            sp.dma_start(wT[:, :, :], DR["W0T"].rearrange("(c p) n -> p c n", p=P)).then_inc(s_w, 16)
            sp.dma_start(wn[:, :, :], DR["W0"].rearrange("(c p) n -> p c n", p=P)).then_inc(s_w, 16)
            sp.dma_start(pj[:, :, :], DR["proj"].rearrange("(c p) n -> p c n", p=P)).then_inc(s_w, 16)
            sp.dma_start(bcol[:, :], DR["bcol"]).then_inc(s_w, 16)
            sp.dma_start(bias[:, :], DR["b"].partition_broadcast(P)).then_inc(s_w, 16)
            sp.sem_inc(s_rank, SUB)
            with sp.Fori(0, NB) as g:
                for s in range(SUB):
                    sp.wait_ge(s_rank, g * SUB + (s + 1))
                    sp.dma_start(rows[s][:, :], DR["adj"][bass.ds(g * QB + s * P, P), :]).then_inc(s_row[s], 16)
            sp.wait_ge(s_am, 1)
            sp.dma_start(DR["amax"].rearrange("(t p) -> t p", p=P), am_row[:, :]).then_inc(s_amout, 16)
            sp.wait_ge(s_amout, 16)

        @block.gpsimd
        def _(pool):
            pool.memset(eps[:, :], EPS).then_inc(s_eps, 1)
            pool.sem_inc(s_h, SUB)
            with pool.Fori(0, NB) as g:
                for s in range(SUB):
                    wait_apart(pool, s_h, g * SUB + (s + 1), s_passed)
                    pool.dma_start(xg[:, s, :], DR["x"][bass.ds(g * QB + s * P, P), :]).then_inc(s_x[s], 16)

        @block.vector
        def _(dve):
            dve.wait_ge(s_set, 1)
            nc.vector.tensor_copy(wpj[:, :, :], setup[:, :].rearrange("p (c k) -> p c k", c=KC)).then_inc(s_setc, 1)
            dve.wait_ge(s_set, 2)
            nc.vector.tensor_copy(bp[:, :], setup[0:2 * H, 0:1]).then_inc(s_setc, 1)
            with dve.Fori(0, NB) as g:
                for s in range(SUB):
                    dve.wait_ge(s_x[s], g * 16 + 16)
                    nc.vector.bn_stats(stats[:, s, :], xg[:, s, :]).then_inc(s_chain, 1)
                wait_apart(dve, s_chain, g * (SUB + 1) + SUB, s_passed)
                for s in range(SUB):
                    nc.vector.bn_aggr(mv[:, s, :], stats[:, s, :]).then_inc(s_mv, 1)
                dve.wait_ge(s_std, g + 1)
                nc.vector.reciprocal(rstd[:, :], std[:, :]).then_inc(s_chain, 1)
                dve.wait_ge(s_chain, g * (SUB + 1) + (SUB + 1))
                nc.vector.scalar_tensor_tensor(out=nmr[:, :], in0=mv[:, :, 0], scalar=-1.0, in1=rstd[:, :],
                                               op0=ALU.mult, op1=ALU.mult).then_inc(s_norm, 1)
                for s in range(SUB):
                    dve.wait_ge(s_row[s], g * 16 + 16)
                    nc.vector.reduce_max(T["amax"][:, bass.ds(g * SUB + s, 1)], rows[s][:, :], AX.X).then_inc(s_rank, 1)
                    if s % 2 == 1:
                        for u in (s - 1, s):
                            dve.wait_ge(s_vp, g * SUB + (u + 1))
                            nc.vector.tensor_tensor(
                                T["V"][:, bass.ds(g * SUB + u, 1), :].rearrange("p a n -> p (a n)"),
                                vp[u % 2][:, :], bias[:, :], ALU.add).then_inc(s_v, 1)
                dve.wait_ge(s_wv, g * 2 + 2)
                nc.vector.tensor_scalar(T["nv"][:, bass.ds(g * SUB, SUB), :], T["v"][:, bass.ds(g * SUB, SUB), :],
                                        -1.0, None, ALU.mult).then_inc(s_v, 1)
            dve.wait_ge(s_amp, 1)
            nc.vector.tensor_copy(am_row[:, :], amp[:, :]).then_inc(s_am, 1)

        @block.scalar
        def _(act):
            act.wait_ge(s_eps, 1)
            act.sem_inc(s_rout, 16)
            with act.Fori(0, NB) as g:
                act.wait_ge(s_mv, g * SUB + SUB)
                nc.scalar.activation(std[:, :], mv[:, :, 1], ACT.Sqrt, bias=eps[:, :]).then_inc(s_std, 1)
                act.wait_ge(s_norm, g + 1)
                for s in range(SUB):
                    nc.scalar.activation(h[:, s, :], xg[:, s, :], ACT.Relu, bias=nmr[:, s:s + 1],
                                         scale=rstd[:, s:s + 1]).then_inc(s_h, 1)
                for c in range(KC):
                    act.wait_ge(s_tp, g * KC + (c + 1))
                    nc.scalar.activation(hT[:, c, :], tp[c % 2][:, :], ACT.Copy).then_inc(s_hT, 1)
                act.wait_ge(s_stp, g + 1)
                act.wait_ge(s_setc, 2)
                nc.scalar.activation(st[:, :], stp[:, :], ACT.Identity, bias=bp[:, :]).then_inc(s_st, 1)
                act.wait_ge(s_rout, g * 16 + 16)
                act.wait_ge(s_st, g + 1)
                nc.scalar.activation(r_sb[:, :], st[0:H, :], ACT.Exp, scale=0.99).then_inc(s_r, 1)
                act.wait_ge(s_r, g + 1)
                act.dma_start(DR["r"][:, bass.ds(g * QB, QB)], r_sb[:, :]).then_inc(s_rout, 16)
                act.wait_ge(s_tq, g + 1)
                nc.scalar.activation(T["w"][:, bass.ds(g * SUB, SUB), :], tq[:, :, H:2 * H], ACT.Exp).then_inc(s_wv, 1)
                nc.scalar.activation(T["v"][:, bass.ds(g * SUB, SUB), :], tq[:, :, H:2 * H], ACT.Exp,
                                     scale=0.01).then_inc(s_wv, 1)
            act.wait_ge(s_rout, 16 * NB + 16)

        @block.tensor
        def _(pe):
            pe.wait_ge(s_w, 16 * 7)
            for c in range(KC):
                for k in range(KC):
                    mm = nc.tensor.matmul(setup[:, c * 2 * H:(c + 1) * 2 * H], wn[:, k, c * P:(c + 1) * P], pj[:, k, :],
                                          start=(k == 0), stop=(k == KC - 1), skip_group_check=True)
            mm.then_inc(s_set, 1)
            pe.wait_ge(s_setc, 1)
            for k in range(KC):
                mm = nc.tensor.matmul(setup[0:2 * H, 0:1], pj[:, k, :], bcol[:, k:k + 1],
                                      start=(k == 0), stop=(k == KC - 1))
            mm.then_inc(s_set, 1)
            pe.sem_inc(s_hT, 2)
            pe.sem_inc(s_v, 2)
            with pe.Fori(0, NB) as g:
                pe.wait_ge(s_h, g * SUB + 2 * SUB)
                for c in range(KC):
                    pe.wait_ge(s_hT, g * KC + (c + 1))
                    for s in range(SUB):
                        mm = nc.tensor.transpose(tp[c % 2][:, s * P:(s + 1) * P], h[:, s, c * P:(c + 1) * P],
                                                 T["identf"][:, :])
                    mm.then_inc(s_tp, 1)
                pe.wait_ge(s_hT, g * KC + KC + 2)
                for c in range(KC):
                    mm = nc.tensor.matmul(stp[:, :], wpj[:, c, :], hT[:, c, :], start=(c == 0), stop=(c == KC - 1))
                mm.then_inc(s_stp, 1)
                for s in range(SUB):
                    pe.wait_ge(s_v, g * (SUB + 1) + (1 if s < 2 else s + 1))
                    for c in range(KC):
                        mm = nc.tensor.matmul(vp[s % 2][:, :], hT[:, c, s * P:(s + 1) * P], wT[:, c, :],
                                              start=(c == 0), stop=(c == KC - 1))
                    mm.then_inc(s_vp, 1)
                wait_apart(pe, s_st, g + 1, s_passed)
                for s in range(SUB):
                    mm = nc.tensor.transpose(tq[:, s, :], st[:, s * P:(s + 1) * P], T["identf"][0:2 * H, 0:2 * H])
                mm.then_inc(s_tq, 1)
            pe.wait_ge(s_rank, SUB + NT)
            nc.tensor.transpose(amp[:, :], T["amax"][:, :], T["identf"][:, :]).then_inc(s_amp, 1)


def layer0_attention(nc, T, DR):
    TILES = 2 * HP * NT
    TILES_P = TILES // QUAD
    TILES_V = TILES - TILES_P
    QUADS = TILES // QUAD
    GROUPS = 4
    PER = NT // GROUPS
    AHEAD = PER
    PREP_STEP = NT - 4 - AHEAD
    EXP_LAG = 2
    COPY_STEP, FIN_STEP, STORE_STEP = 4, 10, 12

    def by_pool(t):
        return t % QUAD == QUAD - 1

    def nth(t):
        return t // QUAD + 1 if by_pool(t) else (QUAD - 1) * (t // QUAD) + t % QUAD + 1

    def prepared_at(hp, mb):
        if hp == HP - 1 and 0 <= mb - PREP_STEP < AHEAD:
            return 1, mb - PREP_STEP
        if hp == 0 and mb + AHEAD < NT:
            return 0, mb + AHEAD
        return None

    def exp_at(hp, mb):
        return prepared_at(hp, mb - EXP_LAG) if mb >= EXP_LAG else None

    with ExitStack() as ctx:
        def sb(name, shape, dt=F32):
            return ctx.enter_context(nc.sbuf_tensor(name, shape, dt))

        def pb(name, shape, dt=F32):
            return ctx.enter_context(nc.psum_tensor(name, shape, dt))

        def sem(name):
            return ctx.enter_context(nc.semaphore("b_" + name))

        A = sb("b_A", [P, NT, QB])
        R = sb("b_R", [P, H, QB])
        am = sb("b_am", [P, QB])
        G = sb("b_G", [P, G_RING, QB])
        PT = sb("b_P", [P, P_RING, QB])
        ones = sb("b_ones", [P, DEN])
        xg = sb("b_xg", [P, SUB, F])
        oT = sb("b_oT", [P, QB])
        dT = sb("b_dT", [P, QB])
        dsum = sb("b_dsum", [P, SUB, 2])
        rden = sb("b_rden", [P, SUB, 2])
        o = sb("b_o", [P, SUB, P])

        acc = [pb(f"b_acc{i}", [P, QB]) for i in range(2)]
        den = [pb(f"b_den{i}", [P, QB]) for i in range(2)]
        fin_o = pb("b_fin_o", [P, SUB, P])
        fin_d = pb("b_fin_d", [P, SUB, P])

        s_passed = sem("waits_passed")
        s_ones = sem("ones")
        s_am = sem("amax_in")
        s_R = [sem(f"r_in{i}") for i in range(HP)]
        s_A = [sem(f"adj_in{i}") for i in range(GROUPS)]
        s_sub = sem("adj_shifted_by_vector")
        s_subp = sem("adj_shifted_by_gpsimd")
        s_exp = sem("adj_exp")
        s_G = sem("g_ready")
        s_U = sem("u_ready")
        s_P = sem("p_by_vector")
        s_Pp = sem("p_by_gpsimd")
        s_used = sem("p_used")
        s_copy = sem("acc_copied")
        s_fin = sem("fin_ready")
        s_chain = sem("vector_chain")
        s_done = sem("x1_part_done")
        s_x = sem("x_in")
        s_out = sem("x1_stored")

        block = ctx.enter_context(nc.Block())

        def in_blocks(eng, body):
            body(0, True, False)
            with eng.Fori(0, NB - 2) as i:
                body(i + 1, False, False)
            body(NB - 1, False, True)

        @block.sync
        def _(sp):
            def load_am(nb):
                sp.dma_start(am[:, :], DR["amax"][bass.ds(nb * QB, QB)].partition_broadcast(P)).then_inc(s_am, 16)

            def load_r(nb, hp):
                for x in range(2):
                    src = DR["r"][2 * hp + x, bass.ds(nb * QB, QB)]
                    sp.dma_start(R[:, 2 * hp + x, :], src.partition_broadcast(P)).then_inc(s_R[hp], 16)

            def load_a(nb, i):
                src = DR["adjT"][i * PER * P:(i + 1) * PER * P, bass.ds(nb * QB, QB)]
                sp.dma_start(A[:, i * PER:(i + 1) * PER, :], src.rearrange("(m p) n -> p m n", p=P)).then_inc(s_A[i], 16)

            def store(nb):
                wait_apart(sp, s_done, nb * HP + (HP + 1), s_passed)
                sp.dma_start(DR["x1"][bass.ds(nb * QB, QB), :].rearrange("(s p) f -> p s f", p=P), xg[:, :, :]).then_inc(s_out, 16)
                wait_apart(sp, s_out, nb * 16 + 16, s_passed)

            load_am(0)
            load_a(0, 0)
            load_r(0, 0)
            for i in range(1, GROUPS):
                load_a(0, i)
            for hp in range(1, HP):
                load_r(0, hp)

            def body(nb, first, last):
                for hp in range(HP):
                    for mb in range(NT):
                        step = hp * NT + mb
                        if hp == 0 and mb == STORE_STEP:
                            if not first:
                                store(nb - 1)
                            sp.dma_start(xg[:, :, :], DR["x"][bass.ds(nb * QB, QB), :].rearrange("(s p) f -> p s f", p=P)).then_inc(s_x, 16)
                        if last:
                            continue
                        if hp == 0 and mb == NT - 1:
                            wait_apart(sp, s_sub, nb * (NT // 2) + NT // 2, s_passed)
                            wait_apart(sp, s_subp, nb * (NT // 2) + NT // 2, s_passed)
                            load_am(nb + 1)
                        if mb == NT - 1:
                            t = 2 * step + 1
                            wait_apart(sp, s_G, nb * TILES_V + nth(t - 1), s_passed)
                            wait_apart(sp, s_U, nb * TILES_P + nth(t), s_passed)
                            load_r(nb + 1, hp)
                        if hp == HP - 1 and mb % PER == PER - 1:
                            t = 2 * step + 1
                            wait_apart(sp, s_P, nb * TILES_V + (TILES_V + nth(t - 1)), s_passed)
                            wait_apart(sp, s_Pp, nb * TILES_P + (TILES_P + nth(t)), s_passed)
                            load_a(nb + 1, mb // PER)

            in_blocks(sp, body)
            store(NB - 1)

        def shift_adj(eng, engine, nb, m):
            if m < 2:
                engine.wait_ge(s_am, nb * 16 + 16)
            engine.wait_ge(s_A[m // PER], nb * 16 + 16)
            eng.tensor_tensor(A[:, m, :], A[:, m, :], am[:, :], ALU.subtract).then_inc(s_sub if m % 2 else s_subp, 1)

        @block.gpsimd
        def _(pool):
            pool.memset(ones[:, :], 1.0).then_inc(s_ones, 1)
            pool.sem_inc(s_Pp, TILES_P)
            for m in range(0, AHEAD, 2):
                shift_adj(nc.gpsimd, pool, 0, m)

            def body(nb, first, last):
                for hp in range(HP):
                    for mb in range(NT):
                        prep = prepared_at(hp, mb)
                        if prep and prep[1] % 2 == 0 and not (last and prep[0]):
                            shift_adj(nc.gpsimd, pool, nb + prep[0], prep[1])
                        t = 2 * (hp * NT + mb) + 1
                        if not by_pool(t):
                            continue
                        if hp == 0:
                            pool.wait_ge(s_exp, nb * NT + (mb + 1))
                        pool.wait_ge(s_used, nb * QUADS + (t // QUAD + 1))
                        pool.wait_ge(s_U, nb * TILES_P + nth(t))
                        nc.gpsimd.tensor_tensor(PT[:, t % P_RING, :], G[:, t % G_RING, :], A[:, mb, :], ALU.mult).then_inc(s_Pp, 1)

            in_blocks(pool, body)

        @block.scalar
        def _(act):
            def exp_adj(nb, m):
                act.wait_ge(s_sub if m % 2 else s_subp, nb * (NT // 2) + (m // 2 + 1))
                nc.scalar.activation(A[:, m, :], A[:, m, :], ACT.Exp).then_inc(s_exp, 1)

            for m in range(AHEAD):
                exp_adj(0, m)

            def body(nb, first, last):
                for hp in range(HP):
                    act.wait_ge(s_R[hp], nb * 32 + 32)
                    for mb in range(NT):
                        for x in range(2):
                            t = 2 * (hp * NT + mb) + x
                            if by_pool(t):
                                continue
                            act.wait_ge(s_P, nb * TILES_V + (TILES_V + nth(t) - G_RING // QUAD * (QUAD - 1)))
                            head = 2 * hp + x
                            nc.scalar.activation(G[:, t % G_RING, :], R[:, head, :], ACT.Relu,
                                                 bias=T["nv"][:, mb, head:head + 1],
                                                 scale=T["w"][:, mb, head:head + 1]).then_inc(s_G, 1)
                        prep = exp_at(hp, mb)
                        if prep and not (last and prep[0]):
                            exp_adj(nb + prep[0], prep[1])

            in_blocks(act, body)

        @block.vector
        def _(dve):
            dve.sem_inc(s_P, TILES_V)

            def copy_acc(nb, hp):
                dve.wait_ge(s_used, nb * QUADS + (P_RING // QUAD + (hp + 1) * 2 * NT // QUAD))
                nc.vector.tensor_copy(oT[:, :], acc[hp % 2][:, :]).then_inc(s_copy, 1)
                nc.vector.tensor_copy(dT[:, :], den[hp % 2][:, :]).then_inc(s_copy, 1)

            def divide(nb, hp):
                dve.wait_ge(s_fin, nb * HP + (hp + 1))
                view = fin_d[:, :, :].rearrange("p s (e j c) -> p s j e c", e=2, j=2)[:, :, :, :, 0]
                nc.vector.tensor_reduce(dsum[:, :, :], view, AX.X, ALU.add).then_inc(s_chain, 1)
                at = nb * (HP * 3) + hp * 3
                dve.wait_ge(s_chain, at + 1)
                nc.vector.reciprocal(rden[:, :, :], dsum[:, :, :]).then_inc(s_chain, 1)
                dve.wait_ge(s_chain, at + 2)
                nc.vector.tensor_tensor(o[:, :, :].rearrange("p s (j d) -> p s j d", j=2),
                                        fin_o[:, :, :].rearrange("p s (j d) -> p s j d", j=2),
                                        rden[:, :, :].unsqueeze(3).to_broadcast([P, SUB, 2, D]), ALU.mult).then_inc(s_chain, 1)
                dve.wait_ge(s_chain, at + 3)
                if hp == 0:
                    dve.wait_ge(s_x, nb * 16 + 16)
                cols = slice(hp * P, (hp + 1) * P)
                nc.vector.tensor_tensor(xg[:, :, cols], xg[:, :, cols], o[:, :, :], ALU.add).then_inc(s_done, 1)

            def finish(nb, hp, mb):
                if mb == COPY_STEP:
                    copy_acc(nb, hp)
                if mb == FIN_STEP:
                    divide(nb, hp)

            for m in range(1, AHEAD, 2):
                shift_adj(nc.vector, dve, 0, m)

            def body(nb, first, last):
                for hp in range(HP):
                    for mb in range(NT):
                        q, head = 2 * (hp * NT + mb) // QUAD, 2 * hp + 1
                        prep = prepared_at(hp, mb)
                        if prep and prep[1] % 2 and not (last and prep[0]):
                            shift_adj(nc.vector, dve, nb + prep[0], prep[1])
                        if mb % 2 == 0:
                            t = QUAD * q + QUAD - 1
                            if mb == 0:
                                dve.wait_ge(s_R[hp], nb * 32 + 32)
                            dve.wait_ge(s_Pp, nb * TILES_P + (TILES_P + nth(t) - G_RING // QUAD))
                            nc.vector.tensor_scalar(G[:, t % G_RING, :], R[:, head, :], T["w"][:, mb + 1, head:head + 1],
                                                    T["v"][:, mb + 1, head:head + 1], ALU.mult, ALU.max).then_inc(s_U, 1)
                            dve.wait_ge(s_used, nb * QUADS + (q + 1))
                        if hp == 0:
                            dve.wait_ge(s_exp, nb * NT + (mb + 1))
                        for x in range(2):
                            t = 2 * (hp * NT + mb) + x
                            if by_pool(t):
                                continue
                            dve.wait_ge(s_G, nb * TILES_V + nth(t))
                            nc.vector.scalar_tensor_tensor(out=PT[:, t % P_RING, :], in0=G[:, t % G_RING, :],
                                                           scalar=T["v"][:, mb, 2 * hp + x:2 * hp + x + 1], in1=A[:, mb, :],
                                                           op0=ALU.add, op1=ALU.mult).then_inc(s_P, 1)
                        if hp:
                            finish(nb, hp - 1, mb)
                        elif not first:
                            finish(nb - 1, HP - 1, mb)

            in_blocks(dve, body)
            for mb in range(NT):
                finish(NB - 1, HP - 1, mb)

        @block.tensor
        def _(pe):
            pe.wait_ge(s_ones, 1)
            pe.sem_inc(s_used, P_RING // QUAD)
            pe.sem_inc(s_copy, 4)
            pe.sem_inc(s_done, 1)

            def transposes(nb, hp):
                pe.wait_ge(s_copy, nb * (2 * HP) + (2 * hp + 6))
                pe.wait_ge(s_done, nb * HP + (hp + 1))
                for s in range(SUB):
                    nc.tensor.transpose(fin_o[:, s, :], oT[:, s * P:(s + 1) * P], T["identf"][:, :])
                for s in range(SUB):
                    mm = nc.tensor.transpose(fin_d[:, s, :], dT[:, s * P:(s + 1) * P], T["identf"][:, :])
                mm.then_inc(s_fin, 1)

            def body(nb, first, last):
                for hp in range(HP):
                    pe.wait_ge(s_copy, nb * (2 * HP) + (2 * hp + 2))
                    for j in range(2 * NT // QUAD):
                        t0 = 2 * hp * NT + QUAD * j
                        for i in range(QUAD):
                            t = t0 + i
                            mb, x = (t // 2) % NT, t % 2
                            head = 2 * hp + x
                            if by_pool(t):
                                pe.wait_ge(s_Pp, nb * TILES_P + (TILES_P + nth(t)))
                            else:
                                pe.wait_ge(s_P, nb * TILES_V + (TILES_V + nth(t)))
                            nc.tensor.matmul(acc[hp % 2][x * D:(x + 1) * D, :], T["V"][:, mb, head * D:(head + 1) * D],
                                             PT[:, t % P_RING, :], start=(mb == 0), stop=(mb == NT - 1))
                        for i in range(QUAD):
                            t = t0 + i
                            mm = nc.tensor.matmul(den[hp % 2][i * DEN:(i + 1) * DEN, :], ones[:, :], PT[:, t % P_RING, :],
                                                  start=(j == 0), stop=(j == 2 * NT // QUAD - 1), tile_position=(0, i * DEN))
                        mm.then_inc(s_used, 1)
                        if j == 3 and hp:
                            transposes(nb, hp - 1)
                        elif j == 3 and not first:
                            transposes(nb - 1, HP - 1)

            in_blocks(pe, body)
            transposes(NB - 1, HP - 1)


def layer1_project(nc, T, DR):
    RING = 4
    PAIRS = 2 * HP
    with ExitStack() as ctx:
        def sb(name, shape, dt=F32):
            return ctx.enter_context(nc.sbuf_tensor(name, shape, dt))

        def pb(name, shape, dt=F32):
            return ctx.enter_context(nc.psum_tensor(name, shape, dt))

        def sem(name):
            return ctx.enter_context(nc.semaphore("c_" + name))

        xg = sb("c_xg", [P, SUB, F])
        h = sb("c_h", [P, SUB, F])
        hT = sb("c_hT", [P, KC, QB])
        wq = sb("c_wq", [P, KC, F])
        wk = sb("c_wk", [P, KC, F])
        wv = sb("c_wv", [P, KC, F])
        stats = sb("c_stats", [P, SUB, 6])
        mv = sb("c_mv", [P, SUB, 2])
        std = sb("c_std", [P, SUB])
        rstd = sb("c_rstd", [P, SUB])
        nmr = sb("c_nmr", [P, SUB])
        eps = sb("c_eps", [P, 1])
        hi = sb("c_hi", [P, RING, QB], F16)
        lo = sb("c_lo", [P, RING, QB], F16)
        vt = sb("c_vt", [P, SUB, HP, 2, P], F16)

        tp = [pb(f"c_tp{i}", [P, QB]) for i in range(2)]
        qp = [pb(f"c_qp{i}", [P, QB]) for i in range(2)]
        vp = [pb(f"c_vp{i}", [P, F]) for i in range(2)]

        s_passed = sem("waits_passed")
        s_w = sem("w_in")
        s_x = [sem(f"x_in{s}") for s in range(SUB)]
        s_chain = sem("vector_chain")
        s_eps = sem("eps")
        s_mv = sem("variance")
        s_std = sem("std")
        s_norm = sem("norm")
        s_h = sem("h")
        s_tp = sem("transposed")
        s_hT = sem("hT")
        s_qp = sem("qk_psum")
        s_hi = sem("hi")
        s_lo = sem("lo")
        s_qout = [sem(f"qk_stored{i}") for i in range(RING)]
        s_vp = sem("v_psum")
        s_vh = sem("v_high")
        s_v = sem("v_split")
        s_vout = sem("v_stored")

        block = ctx.enter_context(nc.Block())

        @block.sync
        def _(sp):
            for w, name in ((wq, "Wq"), (wk, "Wk"), (wv, "Wv")):
                sp.dma_start(w[:, :, :], DR[name].rearrange("(c p) n -> p c n", p=P)).then_inc(s_w, 16)
            for i in range(RING):
                sp.sem_inc(s_qout[i], 32)
            sp.sem_inc(s_vout, 16 * SUB)
            with sp.Fori(0, NB) as g:
                for j in range(PAIRS):
                    sp.wait_ge(s_lo, g * PAIRS + (j + 1))
                    row, i, to = (j % HP) * P, j % RING, "qk"[j // HP]
                    for half, tile in (("h", hi), ("l", lo)):
                        sp.dma_start(DR[to + half][row:row + P, bass.ds(g * QB, QB)], tile[:, i, :]).then_inc(s_qout[i], 16)
                for s in range(SUB):
                    sp.wait_ge(s_v, g * SUB + (s + 3))
                    sp.dma_start(DR["v1"][:, bass.ds(g * QB + s * P, P), :].rearrange("h p k -> p h k"),
                                 vt[:, s, :, :, :].rearrange("p h a k -> p h (a k)")).then_inc(s_vout, 16)
            for i in range(RING):
                sp.wait_ge(s_qout[i], 32 * (NB * PAIRS // RING + 1))
            sp.wait_ge(s_vout, 16 * SUB * (NB + 1))

        @block.gpsimd
        def _(pool):
            pool.memset(eps[:, :], EPS).then_inc(s_eps, 1)
            pool.sem_inc(s_h, SUB)
            with pool.Fori(0, NB) as g:
                for s in range(SUB):
                    wait_apart(pool, s_h, g * SUB + (s + 1), s_passed)
                    pool.dma_start(xg[:, s, :], DR["x1"][bass.ds(g * QB + s * P, P), :]).then_inc(s_x[s], 16)

        @block.vector
        def _(dve):
            with dve.Fori(0, NB) as g:
                for s in range(SUB):
                    dve.wait_ge(s_x[s], g * 16 + 16)
                    nc.vector.bn_stats(stats[:, s, :], xg[:, s, :]).then_inc(s_chain, 1)
                wait_apart(dve, s_chain, g * (SUB + 1) + SUB, s_passed)
                for s in range(SUB):
                    nc.vector.bn_aggr(mv[:, s, :], stats[:, s, :]).then_inc(s_mv, 1)
                dve.wait_ge(s_std, g + 1)
                nc.vector.reciprocal(rstd[:, :], std[:, :]).then_inc(s_chain, 1)
                dve.wait_ge(s_chain, g * (SUB + 1) + (SUB + 1))
                nc.vector.scalar_tensor_tensor(out=nmr[:, :], in0=mv[:, :, 0], scalar=-1.0, in1=rstd[:, :],
                                               op0=ALU.mult, op1=ALU.mult).then_inc(s_norm, 1)
                for j in range(PAIRS):
                    dve.wait_ge(s_hi, g * PAIRS + (j + 1))
                    nc.vector.scalar_tensor_tensor(out=lo[:, j % RING, :], in0=qp[j % 2][:, :], scalar=QK_SCALE,
                                                   in1=hi[:, j % RING, :], op0=ALU.mult, op1=ALU.subtract).then_inc(s_lo, 1)
                for s in range(SUB):
                    dve.wait_ge(s_vh, g * SUB + (s + 1))
                    nc.vector.scalar_tensor_tensor(out=vt[:, s, :, 1, :], in0=vp[s % 2][:, :].rearrange("p (h k) -> p h k", h=HP),
                                                   scalar=QK_SCALE, in1=vt[:, s, :, 0, :], op0=ALU.mult,
                                                   op1=ALU.subtract).then_inc(s_v, 1)

        @block.scalar
        def _(act):
            act.wait_ge(s_eps, 1)
            with act.Fori(0, NB) as g:
                act.wait_ge(s_mv, g * SUB + SUB)
                nc.scalar.activation(std[:, :], mv[:, :, 1], ACT.Sqrt, bias=eps[:, :]).then_inc(s_std, 1)
                act.wait_ge(s_norm, g + 1)
                for s in range(SUB):
                    nc.scalar.activation(h[:, s, :], xg[:, s, :], ACT.Relu, bias=nmr[:, s:s + 1],
                                         scale=rstd[:, s:s + 1]).then_inc(s_h, 1)
                for c in range(KC):
                    act.wait_ge(s_tp, g * KC + (c + 1))
                    nc.scalar.activation(hT[:, c, :], tp[c % 2][:, :], ACT.Copy).then_inc(s_hT, 1)
                for j in range(PAIRS):
                    act.wait_ge(s_qout[j % RING], g * (32 * PAIRS // RING) + 32 * (j // RING + 1))
                    act.wait_ge(s_qp, g * PAIRS + (j + 1))
                    nc.scalar.activation(hi[:, j % RING, :], qp[j % 2][:, :], ACT.Copy, scale=QK_SCALE).then_inc(s_hi, 1)
                act.wait_ge(s_vout, g * (16 * SUB) + 16 * SUB)
                for s in range(SUB):
                    act.wait_ge(s_vp, g * SUB + (s + 1))
                    nc.scalar.activation(vt[:, s, :, 0, :], vp[s % 2][:, :].rearrange("p (h k) -> p h k", h=HP), ACT.Copy,
                                         scale=QK_SCALE).then_inc(s_vh, 1)

        @block.tensor
        def _(pe):
            pe.wait_ge(s_w, 16 * 3)
            pe.sem_inc(s_hT, 2)
            pe.sem_inc(s_v, 2)
            with pe.Fori(0, NB) as g:
                pe.wait_ge(s_h, g * SUB + 2 * SUB)
                for c in range(KC):
                    pe.wait_ge(s_hT, g * KC + (c + 1))
                    for s in range(SUB):
                        mm = nc.tensor.transpose(tp[c % 2][:, s * P:(s + 1) * P], h[:, s, c * P:(c + 1) * P],
                                                 T["identf"][:, :])
                    mm.then_inc(s_tp, 1)
                pe.wait_ge(s_hT, g * KC + KC + 2)
                for j in range(PAIRS):
                    if j >= 2:
                        pe.wait_ge(s_lo, g * PAIRS + (j - 1))
                    w, col = (wq, wk)[j // HP], (j % HP) * P
                    for c in range(KC):
                        mm = nc.tensor.matmul(qp[j % 2][:, :], w[:, c, col:col + P], hT[:, c, :],
                                              start=(c == 0), stop=(c == KC - 1))
                    mm.then_inc(s_qp, 1)
                for s in range(SUB):
                    pe.wait_ge(s_v, g * SUB + (s + 1))
                    for c in range(KC):
                        mm = nc.tensor.matmul(vp[s % 2][:, :], hT[:, c, s * P:(s + 1) * P], wv[:, c, :],
                                              start=(c == 0), stop=(c == KC - 1))
                    mm.then_inc(s_vp, 1)
                pe.wait_ge(s_lo, g * PAIRS + PAIRS)


def layer1_attention(nc, T, DR):
    TILES = 2 * HP * NT
    PAIR = 2 * NT
    STEPS = HP * NT
    LAG = 2
    F_RING, H_RING = 4, 8
    H_STEPS = H_RING // 2
    GROUPS = 4
    PER = NT // GROUPS
    MC = N // QB
    GUARDS = 2 * SUB * MC
    CW = 1024
    CH = N // CW
    CHUNKS = SUB * CH
    M1_USES = HP + SUB
    ROW_OPS = 2 * CH + 3
    MASK_OPS = 1 + SUB * ROW_OPS
    FIRST_G, LAST_G = 5, 27
    MT_STEP = 10
    COPY_STEP, SPREAD_STEP, WO_STEP, STORE_STEP = LAG, 3, 10, 28
    EXP_SCALE = 1.0 / (QK_SCALE * QK_SCALE * D ** 0.5)
    P_SHIFT = math.log(4096.0) / EXP_SCALE
    MASK_SCALE = 1e16 / EXP_SCALE
    MASK_FLOOR = -32768.0 / EXP_SCALE

    def guards_of(mb):
        def upto(step):
            return GUARDS * min(max(step - FIRST_G + 1, 0), LAST_G - FIRST_G + 1) // (LAST_G - FIRST_G + 1)
        return range(upto(mb - 1), upto(mb))

    def crow_of(mb):
        for x in range(2):
            if mb == 2 + next(m for m in range(NT) if (x + 1) * GUARDS // 2 - 1 in guards_of(m)):
                return x
        return None

    def mt_of(hp, mb):
        if hp == HP - 1 and mb >= MT_STEP:
            return mb - MT_STEP
        if hp == 0 and mb < MT_STEP:
            return mb + NT - MT_STEP
        return None

    AHEAD = NT - MT_STEP
    m0_index, use = {}, 0
    for hp_ in range(HP):
        for mb_ in range(NT):
            if mt_of(hp_, mb_) is not None:
                m0_index["mask", hp_, mb_] = use
                use += 1
            if crow_of(mb_) is not None:
                m0_index["crow", hp_, crow_of(mb_)] = use
                use += 1
    M0_USES = use
    M0_START = AHEAD + 2

    FIRST_C, LAST_C = (HP - 2) * NT + 20, (HP - 1) * NT + 5
    CHUNK_STEPS = [*range(FIRST_C, FIRST_C + CHUNKS - CH), *range(LAST_C, LAST_C + CH)]

    def recip_step(hp):
        return 4 if hp == HP - 1 else 12

    def by_pool(t):
        return t % F_RING == F_RING - 1

    def split_count(t):
        return t // F_RING + 1 if by_pool(t) else (F_RING - 1) * (t // F_RING) + t % F_RING + 1

    with ExitStack() as ctx:
        def sb(name, shape, dt=F32):
            return ctx.enter_context(nc.sbuf_tensor(name, shape, dt))

        def pb(name, shape, dt=F32):
            return ctx.enter_context(nc.psum_tensor(name, shape, dt))

        def sem(name):
            return ctx.enter_context(nc.semaphore("d_" + name))

        KA = sb("d_KA", [P, 2, 2, N], F16)
        KB = sb("d_KB", [P, 2, N], F16)
        V = sb("d_V", [P, NT, 2, P], F16)
        QA = sb("d_QA", [P, 2, 2, QB], F16)
        QL = sb("d_QL", [P, 2, 2, QB], F16)
        MR = sb("d_MR", [P, SUB, N], BF16)
        MT = sb("d_MT", [P, NT, QB], BF16)
        stage = sb("d_stage", [P, 2, CW])
        dblk = sb("d_dblk", [P, SUB, P])
        brow = sb("d_brow", [P, SUB])
        PF = sb("d_PF", [P, F_RING, QB])
        PH = sb("d_PH", [P, H_RING, QB], F16)
        PL = sb("d_PL", [P, H_RING, QB], F16)
        oN = sb("d_oN", [P, HP, QB])
        wo = sb("d_wo", [P, HP, F])
        xr = sb("d_xr", [P, SUB, F])
        rb = sb("d_rb", [P, QB])
        dT = sb("d_dT", [P, QB])
        junk = sb("d_junk", [P, 2, QB], BF16)
        gm = sb("d_gm", [P, SUB, MC])
        cm = sb("d_cm", [P, SUB])
        dg = sb("d_dg", [P, SUB, P], F16)
        shift = sb("d_shift", [P, 1])
        scale1 = sb("d_scale1", [P, DEN], F16)
        selc = sb("d_selc", [P, P], F16)
        seld = sb("d_seld", [P, P])
        idh = sb("d_idh", [P, P], F16)

        sc = [pb(f"d_sc{i}", [P, QB]) for i in range(2)]
        gd = [pb(f"d_gd{i}", [P, QB]) for i in range(2)]
        acc = pb("d_acc", [P, QB])
        den = pb("d_den", [P, QB])
        misc0 = pb("d_misc0", [P, QB])
        misc1 = pb("d_misc1", [P, QB])
        misc0h = misc0[:, :].bitcast(BF16)

        s_passed = sem("waits_passed")
        s_const = sem("const_in")
        s_set = sem("constants_set")
        s_KA = [[sem(f"ka_in{i}{x}") for x in range(2)] for i in range(2)]
        s_Q = [sem(f"q_in{i}") for i in range(2)]
        s_KB = [sem(f"kb_in{i}") for i in range(GROUPS)]
        s_V = [sem(f"v_in{i}") for i in range(GROUPS)]
        s_stage = [sem(f"adj_in{i}") for i in range(2)]
        s_dblk = sem("adj_diagonal_in")
        s_mk = sem("mask_made")
        s_mtp = sem("mask_transposed")
        s_m0 = sem("misc0_read")
        s_S = sem("scores")
        s_P = sem("exp_done")
        s_low = sem("low_by_vector")
        s_lowp = sem("low_by_gpsimd")
        s_used = sem("steps_used")
        s_G = sem("guard_scores")
        s_gm = sem("guard_max")
        s_cm = sem("row_max")
        s_dg = sem("row_max_diagonal")
        s_crow = sem("max_row")
        s_ac = sem("acc_copied")
        s_dc = sem("den_copied")
        s_m1w = sem("misc1_written")
        s_m1 = sem("misc1_read")
        s_rb = sem("reciprocal")
        s_oN = sem("normalised")
        s_x = sem("x1_in")
        s_out = sem("out_stored")

        block = ctx.enter_context(nc.Block())

        def load_ka(sp, par, hp):
            for x in range(2):
                row = (2 * hp + x) * D
                sp.dma_start(KA[0:D, par, x, :], DR["kh"][row:row + D, :]).then_inc(s_KA[par][x], 16)
                sp.dma_start(KA[D:P, par, x, :], DR["kl"][row:row + D, :]).then_inc(s_KA[par][x], 16)

        def load_q(sp, par, hp, nb):
            for x in range(2):
                row = (2 * hp + x) * D
                for half in range(2):
                    sp.dma_start(QA[half * D:(half + 1) * D, par, x, :], DR["qh"][row:row + D, bass.ds(nb * QB, QB)]).then_inc(s_Q[par], 16)
                sp.dma_start(QL[0:D, par, x, :], DR["ql"][row:row + D, bass.ds(nb * QB, QB)]).then_inc(s_Q[par], 16)

        def load_kb(sp, hp, i):
            cols = slice(i * PER * P, (i + 1) * PER * P)
            for x in range(2):
                row = (2 * hp + x) * D
                sp.dma_start(KB[0:D, x, cols], DR["kh"][row:row + D, cols]).then_inc(s_KB[i], 16)

        def load_v(sp, hp, i):
            rows = slice(i * PER * P, (i + 1) * PER * P)
            sp.dma_start(V[:, i * PER:(i + 1) * PER, :, :].rearrange("p m a n -> p m (a n)"),
                         DR["v1"][hp, rows, :].rearrange("(m p) k -> p m k", p=P)).then_inc(s_V[i], 16)

        def load_diagonals(sp, nb):
            for s in range(SUB):
                rows = bass.ds(nb * QB + s * P, P)
                sp.dma_start(dblk[:, s, :], DR["adj"][rows, bass.ds(nb * QB + s * P, P)]).then_inc(s_dblk, 16)

        def load_chunk(sp, nb, ci):
            s, c = divmod(ci, CH)
            sp.dma_start(stage[:, ci % 2, :], DR["adj"][bass.ds(nb * QB + s * P, P), c * CW:(c + 1) * CW]).then_inc(s_stage[ci % 2], 16)

        def chunk_done(ci):
            return 1 + ROW_OPS * (ci // CH) + 2 * (ci % CH) + 2

        @block.sync
        def _(sp):
            for tile, name in ((selc, "selc"), (seld, "seld"), (idh, "idh")):
                sp.dma_start(tile[:, :], DR[name]).then_inc(s_const, 16)
            sp.dma_start(wo[:, :, :], DR["Wo"].rearrange("(c p) n -> p c n", p=P)).then_inc(s_const, 16)
            load_diagonals(sp, 0)
            for ci in range(2):
                load_chunk(sp, 0, ci)
            load_ka(sp, 0, 0)
            load_q(sp, 0, 0, 0)
            for ci in range(2, CHUNKS):
                sp.wait_ge(s_mk, chunk_done(ci - 2))
                load_chunk(sp, 0, ci)
            for i in range(GROUPS):
                load_kb(sp, 0, i)
                load_v(sp, 0, i)

            def store(nb):
                wait_apart(sp, s_m1, nb * M1_USES + (M1_USES + 1), s_passed)
                sp.dma_start(DR["out"][bass.ds(nb * QB, QB), :].rearrange("(s p) f -> p s f", p=P), xr[:, :, :]).then_inc(s_out, 16)
                wait_apart(sp, s_out, nb * 16 + 16, s_passed)

            def body(nb, first):
                for hp in range(HP):
                    nxt, par = (hp + 1) % HP, (hp + 1) % 2
                    for mb in range(NT):
                        step = hp * NT + mb
                        if mb == 0:
                            sp.wait_ge(s_S, nb * TILES + (hp * PAIR + CREDIT))
                            load_ka(sp, par, nxt)
                            load_q(sp, par, nxt, nb if hp < HP - 1 else (nb + 1) % NB)
                        if mb % PER == PER - 1:
                            sp.wait_ge(s_S, nb * TILES + (hp * PAIR + 2 * (mb + 1) + CREDIT))
                            load_kb(sp, nxt, mb // PER)
                        if mb % PER == LAG:
                            i = (mb // PER - 1) % GROUPS
                            if not (first and step < PER):
                                sp.wait_ge(s_used, nb * STEPS + (step - LAG + H_STEPS))
                                load_v(sp, nxt if mb > PER else hp, i)
                        if step == FIRST_C - 3:
                            wait_apart(sp, s_mk, nb * MASK_OPS + MASK_OPS, s_passed)
                            load_diagonals(sp, (nb + 1) % NB)
                            chunks = range(2)
                        else:
                            chunks = [CHUNK_STEPS.index(step) + 2] if step in CHUNK_STEPS[:CHUNKS - 2] else []
                        for ci in chunks:
                            done = chunk_done(ci - 2) if ci >= 2 else chunk_done(CHUNKS + ci - 2) - MASK_OPS
                            wait_apart(sp, s_mk, nb * MASK_OPS + (MASK_OPS + done), s_passed)
                            load_chunk(sp, (nb + 1) % NB, ci)
                        if step == STORE_STEP:
                            if not first:
                                store(nb - 1)
                            sp.dma_start(xr[:, :, :], DR["x1"][bass.ds(nb * QB, QB), :].rearrange("(s p) f -> p s f", p=P)).then_inc(s_x, 16)

            body(0, True)
            with sp.Fori(0, NB - 1) as i:
                body(i + 1, False)
            store(NB - 1)
            for par in range(2):
                for x in range(2):
                    sp.wait_ge(s_KA[par][x], 32 * (2 * NB + 1 - par))
                sp.wait_ge(s_Q[par], 96 * (2 * NB + 1 - par))
            for i in range(GROUPS):
                sp.wait_ge(s_KB[i], 32 * (HP * NB + 1))
                sp.wait_ge(s_V[i], 16 * (HP * NB + (1 if i < GROUPS - 1 else 0)))

        def split(eng, engine, nb, t):
            engine.wait_ge(s_P, nb * TILES + (CREDIT + t + 1))
            eng.tensor_tensor(PL[:, t % H_RING, :], PF[:, t % F_RING, :], PH[:, t % H_RING, :],
                              ALU.subtract).then_inc(s_lowp if by_pool(t) else s_low, 1)

        @block.gpsimd
        def _(pool):
            pool.sem_inc(s_lowp, 1)
            with pool.Fori(0, NB) as nb:
                for t in range(TILES):
                    if by_pool(t):
                        split(nc.gpsimd, pool, nb, t)

        @block.scalar
        def _(act):
            act.wait_ge(s_const, 16 * 4)
            act.wait_ge(s_set, 5)
            act.sem_inc(s_P, CREDIT)
            act.sem_inc(s_ac, 1)

            def copy_crow(count, par, x):
                act.wait_ge(s_crow, count)
                nc.scalar.activation(QL[D:P, par, x, :], misc0[D:P, :], ACT.Identity, bias=shift[D:P, :]).then_inc(s_m0, 1)

            def copy_mask(count, m):
                act.wait_ge(s_mtp, count)
                nc.scalar.activation(MT[:, m, :], misc0h[:, 0:QB], ACT.Copy).then_inc(s_m0, 1)

            def copy_acc(nb, hp):
                act.wait_ge(s_used, nb * STEPS + ((hp + 1) * NT + H_STEPS))
                nc.scalar.activation(oN[:, hp, :], acc[:, :], ACT.Copy).then_inc(s_ac, 1)

            for x in range(2):
                copy_crow(x + 1, 0, x)
            for m in range(AHEAD):
                copy_mask(m + 1, m)

            def body(nb, first):
                for hp in range(HP):
                    for mb in range(NT):
                        if mb == COPY_STEP:
                            if hp:
                                if hp == 1:
                                    act.wait_ge(s_m1w, nb * M1_USES + 1)
                                copy_acc(nb, hp - 1)
                            elif not first:
                                copy_acc(nb - 1, HP - 1)
                        for x in range(2):
                            t = hp * PAIR + 2 * mb + x
                            act.wait_ge(s_S, nb * TILES + (CREDIT + t + 1))
                            if by_pool(t):
                                act.wait_ge(s_lowp, nb * (TILES // F_RING) + split_count(t))
                            else:
                                act.wait_ge(s_low, nb * (TILES // F_RING * (F_RING - 1)) + split_count(t))
                            nc.scalar.activation(PF[:, t % F_RING, :], sc[t % 2][:, :], ACT.Exp, scale=EXP_SCALE)
                            if x == 0:
                                act.wait_ge(s_used, nb * STEPS + (hp * NT + mb + 1))
                            nc.scalar.activation(PH[:, t % H_RING, :], sc[t % 2][:, :], ACT.Exp, scale=EXP_SCALE).then_inc(s_P, 1)
                        m = mt_of(hp, mb)
                        if m is not None:
                            copy_mask(nb * NT + ((AHEAD if hp else 0) + m + (1 if not hp else 1 + NT - AHEAD)), m)
                        if crow_of(mb) is not None:
                            copy_crow(nb * (2 * HP) + (2 * hp + crow_of(mb) + 3), (hp + 1) % 2, crow_of(mb))

            body(0, True)
            with act.Fori(0, NB - 1) as i:
                body(i + 1, False)
            copy_acc(NB - 1, HP - 1)

        @block.vector
        def _(dve):
            nc.vector.memset(scale1[:, :], QK_SCALE).then_inc(s_set, 1)
            nc.vector.memset(KB[D:P, :, :], 0.0).then_inc(s_set, 1)
            nc.vector.memset(shift[:, :], 0.0).then_inc(s_set, 1)
            dve.wait_ge(s_set, 3)
            nc.vector.memset(KB[D:D + 1, :, :], C_ROW).then_inc(s_set, 1)
            nc.vector.memset(shift[D:D + 1, :], P_SHIFT / C_ROW).then_inc(s_set, 1)
            dve.wait_ge(s_const, 16 * 4)
            dve.sem_inc(s_low, F_RING - 1)
            dve.sem_inc(s_dc, 1)
            dve.sem_inc(s_m1, 1)

            def mask_setup(nb):
                nc.vector.tensor_scalar(brow[:, :], T["amax"][:, bass.ds(nb * SUB, SUB)], 1.0, -1.0,
                                        ALU.max, ALU.add).then_inc(s_mk, 1)

            def mask_chunk(run, nb, ci):
                s, c = divmod(ci, CH)
                at = run * MASK_OPS + (chunk_done(ci) - 2)
                dve.wait_ge(s_stage[ci % 2], run * (16 * CHUNKS // 2) + 16 * (ci // 2 + 1))
                dve.wait_ge(s_mk, at)
                nc.vector.tensor_scalar(stage[:, ci % 2, :], stage[:, ci % 2, :], -1.0, brow[:, s:s + 1],
                                        ALU.add, ALU.subtract).then_inc(s_mk, 1)
                dve.wait_ge(s_mk, at + 1)
                nc.vector.tensor_scalar(MR[:, s, c * CW:(c + 1) * CW], stage[:, ci % 2, :], MASK_SCALE, MASK_FLOOR,
                                        ALU.mult, ALU.max).then_inc(s_mk, 1)
                if c < CH - 1:
                    return
                dve.wait_ge(s_dblk, run * (16 * SUB) + 16 * SUB)
                at = at + 2
                nc.vector.tensor_tensor(dblk[:, s, :], dblk[:, s, :], T["identf"][:, :], ALU.max).then_inc(s_mk, 1)
                dve.wait_ge(s_mk, at + 1)
                nc.vector.tensor_scalar(dblk[:, s, :], dblk[:, s, :], -1.0, brow[:, s:s + 1],
                                        ALU.add, ALU.subtract).then_inc(s_mk, 1)
                dve.wait_ge(s_mk, at + 2)
                nc.vector.tensor_scalar(MR[:, s, bass.ds(nb * QB + s * P, P)], dblk[:, s, :], MASK_SCALE, MASK_FLOOR,
                                        ALU.mult, ALU.max).then_inc(s_mk, 1)

            def guard(it, gi, mask_count=None):
                x, s, c = gi // (SUB * MC), gi // MC % SUB, gi % MC
                if mask_count is not None:
                    dve.wait_ge(s_mk, mask_count)
                if gi >= 2 or not isinstance(it, int):
                    dve.wait_ge(s_gm, it * GUARDS + (gi - 1))
                wait_apart(dve, s_G, it * GUARDS + (gi + 1), s_passed)
                nc.vector.tensor_tensor_reduce(out=junk[:, gi % 2, :], in0=gd[gi % 2][:, :], in1=MR[:, s, c * QB:(c + 1) * QB],
                                               scale=1.0, scalar=-3.0e38, op0=ALU.add, op1=ALU.max,
                                               accum_out=gm[:, s, c:c + 1]).then_inc(s_gm, 1)
                if c == MC - 1:
                    n = x * SUB + s
                    dve.wait_ge(s_gm, it * GUARDS + (gi + 1))
                    nc.vector.reduce_max(cm[:, s:s + 1], gm[:, s, :], AX.X).then_inc(s_cm, 1)
                    dve.wait_ge(s_cm, it * (2 * SUB) + (n + 1))
                    if s == 0 and not (isinstance(it, int) and it == 0 and x == 0):
                        dve.wait_ge(s_crow, it * 2 + x)
                    nc.vector.tensor_scalar(dg[:, s, :], idh[:, :], cm[:, s:s + 1], -1.0 / C_ROW,
                                            ALU.mult, ALU.mult).then_inc(s_dg, 1)

            def copy_den(nb, hp):
                dve.wait_ge(s_used, nb * STEPS + ((hp + 1) * NT + H_STEPS))
                nc.vector.tensor_copy(dT[:, :], den[:, :]).then_inc(s_dc, 1)

            def reciprocal(nb, hp, k):
                dve.wait_ge(s_m1w, nb * M1_USES + (hp + 2))
                ins = nc.vector.reciprocal(rb[:, k * P:(k + 1) * P], misc1[:, k * P:(k + 1) * P])
                ins.then_inc(s_m1 if k == SUB - 1 else s_rb, 1)

            def normalise(nb, hp):
                dve.wait_ge(s_m1, nb * M1_USES + (hp + 2))
                dve.wait_ge(s_ac, nb * HP + (hp + 2))
                nc.vector.tensor_tensor(oN[:, hp, :], oN[:, hp, :], rb[:, :], ALU.mult).then_inc(s_oN, 1)

            def add_rows(nb, s):
                if s == 0:
                    dve.wait_ge(s_x, nb * 16 + 16)
                dve.wait_ge(s_m1w, nb * M1_USES + (HP + s + 2))
                nc.vector.tensor_tensor(xr[:, s, :], misc1[:, :], xr[:, s, :], ALU.add).then_inc(s_m1, 1)

            def finish(nb, hp, mb):
                if mb == COPY_STEP:
                    copy_den(nb, hp)
                if recip_step(hp) <= mb < recip_step(hp) + SUB:
                    reciprocal(nb, hp, mb - recip_step(hp))
                if mb == recip_step(hp) + SUB:
                    normalise(nb, hp)
                s = (mb - WO_STEP - 1) // 3
                if hp == HP - 1 and (mb - WO_STEP - 1) % 3 == 0 and 0 <= s < SUB:
                    add_rows(nb, s)

            mask_setup(0)
            dve.wait_ge(s_mk, 1)
            for ci in range(CHUNKS):
                mask_chunk(0, 0, ci)
            dve.wait_ge(s_mk, MASK_OPS)
            for gi in range(GUARDS):
                guard(0, gi)

            def body(nb, first):
                for hp in range(HP):
                    for mb in range(NT):
                        step = hp * NT + mb
                        if hp:
                            finish(nb, hp - 1, mb)
                        elif not first:
                            finish(nb - 1, HP - 1, mb)
                        guards = list(guards_of(mb))
                        for x in range(2):
                            t = 2 * (step - 1) + x
                            if t >= 0 and not by_pool(t):
                                split(nc.vector, dve, nb, t)
                            elif t < 0 and not first and not by_pool(t + TILES):
                                split(nc.vector, dve, nb - 1, t + TILES)
                            for gi in guards[:1] if x == 0 else guards[1:]:
                                row_at = gi // MC % SUB + 1
                                count = nb * MASK_OPS + (MASK_OPS + 1 + ROW_OPS * row_at) if hp == HP - 1 and gi < SUB * MC and gi % MC == 0 else None
                                guard(nb * HP + (hp + 1), gi, count)
                        if step == FIRST_C:
                            dve.wait_ge(s_mtp, nb * NT + NT)
                            mask_setup((nb + 1) % NB)
                            dve.wait_ge(s_mk, nb * MASK_OPS + (MASK_OPS + 1))
                        if step in CHUNK_STEPS:
                            mask_chunk(nb + 1, (nb + 1) % NB, CHUNK_STEPS.index(step))

            body(0, True)
            with dve.Fori(0, NB - 1) as i:
                body(i + 1, False)
            for x in range(2):
                if not by_pool(TILES - 2 + x):
                    split(nc.vector, dve, NB - 1, TILES - 2 + x)
            for mb in range(NT):
                finish(NB - 1, HP - 1, mb)

        @block.tensor
        def _(pe):
            pe.wait_ge(s_const, 16 * 4)
            pe.wait_ge(s_set, 5)
            pe.sem_inc(s_S, CREDIT)
            pe.sem_inc(s_used, H_STEPS)
            pe.sem_inc(s_m1w, 1)

            def guard(it, par, gi, count):
                x, s, c = gi // (SUB * MC), gi // MC % SUB, gi % MC
                if s == 0 and c == 0:
                    if x == 0:
                        pe.wait_ge(s_Q[par], count * 96 + 96)
                    pe.wait_ge(s_KA[par][x], count * 32 + 32)
                if gi >= 2 or not isinstance(it, int):
                    pe.wait_ge(s_gm, it * GUARDS + (gi - 1))
                nc.tensor.matmul(gd[gi % 2][:, :], QA[:, par, x, s * P:(s + 1) * P], KA[:, par, x, c * QB:(c + 1) * QB],
                                 start=True, stop=True).then_inc(s_G, 1)

            def crow(it, x, uses):
                pe.wait_ge(s_dg, it * (2 * SUB) + SUB * (x + 1))
                if uses is not None:
                    pe.wait_ge(s_m0, uses)
                for s in range(SUB):
                    mm = nc.tensor.matmul(misc0[:, s * P:(s + 1) * P], selc[:, :], dg[:, s, :], start=True, stop=True)
                mm.then_inc(s_crow, 1)

            def transpose_mask(m, uses):
                pe.wait_ge(s_m0, uses)
                for s in range(SUB):
                    mm = nc.tensor.transpose(misc0h[:, s * P:(s + 1) * P], MR[:, s, m * P:(m + 1) * P], T["identb"][:, :])
                mm.then_inc(s_mtp, 1)

            def scores(nb, hp, mb, x):
                par, t = hp % 2, hp * PAIR + 2 * mb + x
                pe.wait_ge(s_P, nb * TILES + (CREDIT + t - 1))
                bank = sc[t % 2][:, :]
                nc.tensor.matmul(bank, KA[:, par, x, mb * P:(mb + 1) * P], QA[:, par, x, :], start=True, stop=False)
                nc.tensor.matmul(bank, KB[:, x, mb * P:(mb + 1) * P], QL[:, par, x, :], start=False, stop=False)
                nc.tensor.matmul(bank, T["identb"][:, :], MT[:, mb, :], start=False, stop=True).then_inc(s_S, 1)

            def products(nb, step):
                hp, mb = divmod(step, NT)
                if mb == 0:
                    pe.wait_ge(s_ac, nb * HP + (hp + 1))
                    pe.wait_ge(s_dc, nb * HP + (hp + 1))
                if mb % PER == 0:
                    pe.wait_ge(s_V[mb // PER], nb * (16 * HP) + 16 * (hp + 1))
                pe.wait_ge(s_P, nb * TILES + (CREDIT + 2 * step + 2))
                first, last = mb == 0, mb == NT - 1
                for half in range(2):
                    for x in range(2):
                        nc.tensor.matmul(acc[x * D:(x + 1) * D, :], V[:, mb, half, x * D:(x + 1) * D],
                                         PH[:, (2 * step + x) % H_RING, :], start=first and half == 0, stop=False)
                for x in range(2):
                    t = 2 * step + x
                    if by_pool(t):
                        pe.wait_ge(s_lowp, nb * (TILES // F_RING) + (1 + split_count(t)))
                    else:
                        pe.wait_ge(s_low, nb * (TILES // F_RING * (F_RING - 1)) + (F_RING - 1 + split_count(t)))
                    nc.tensor.matmul(acc[x * D:(x + 1) * D, :], V[:, mb, 0, x * D:(x + 1) * D],
                                     PL[:, t % H_RING, :], start=False, stop=last)
                for i in range(QUAD):
                    x, half = divmod(i, 2)
                    mm = nc.tensor.matmul(den[i * DEN:(i + 1) * DEN, :], scale1[:, :], (PH, PL)[half][:, (2 * step + x) % H_RING, :],
                                          start=first, stop=last, tile_position=(0, i * DEN))
                mm.then_inc(s_used, 1)

            def spread_den(nb, hp):
                pe.wait_ge(s_dc, nb * HP + (hp + 2))
                pe.wait_ge(s_m1, nb * M1_USES + (hp + 1))
                nc.tensor.matmul(misc1[:, :], seld[:, :], dT[:, :], start=True, stop=True).then_inc(s_m1w, 1)

            def project_out(nb, s):
                if s == 0:
                    pe.wait_ge(s_oN, nb * HP + HP)
                pe.wait_ge(s_m1, nb * M1_USES + (HP + s + 1))
                for c in range(HP):
                    mm = nc.tensor.matmul(misc1[:, :], oN[:, c, s * P:(s + 1) * P], wo[:, c, :],
                                          start=(c == 0), stop=(c == HP - 1))
                mm.then_inc(s_m1w, 1)

            def finish(nb, hp, mb):
                if mb == SPREAD_STEP:
                    spread_den(nb, hp)
                s = (mb - WO_STEP) // 3
                if hp == HP - 1 and (mb - WO_STEP) % 3 == 0 and 0 <= s < SUB:
                    project_out(nb, s)

            pe.wait_ge(s_mk, MASK_OPS)
            for gi in range(GUARDS):
                guard(0, 0, gi, 0)
                if gi == GUARDS // 2 + 2:
                    crow(0, 0, None)
            crow(0, 1, 1)
            for m in range(AHEAD):
                transpose_mask(m, m + 2)

            def body(nb, first):
                for hp in range(HP):
                    uses = nb * M0_USES + M0_START
                    for mb in range(NT):
                        step = hp * NT + mb
                        if mb == 0:
                            count = nb * 2 + hp // 2
                            pe.wait_ge(s_Q[hp % 2], count * 96 + 96)
                            for x in range(2):
                                pe.wait_ge(s_KA[hp % 2][x], count * 32 + 32)
                            if hp:
                                pe.wait_ge(s_m0, uses + (m0_index["crow", hp - 1, 1] + 1))
                            else:
                                pe.wait_ge(s_m0, uses - 1)
                        if hp == 0 and mb >= AHEAD - 1:
                            at = 0 if mb < AHEAD else m0_index["mask", 0, mb - AHEAD] + 1
                            pe.wait_ge(s_m0, uses + at)
                        if mb % PER == 0:
                            pe.wait_ge(s_KB[mb // PER], nb * (32 * HP) + 32 * (hp + 1))
                        guards = list(guards_of(mb))
                        it, par, count = nb * HP + (hp + 1), (hp + 1) % 2, nb * 2 + (hp + 1) // 2
                        scores(nb, hp, mb, 0)
                        for gi in guards[:1]:
                            guard(it, par, gi, count)
                        if mt_of(hp, mb) is not None:
                            if hp and mb == MT_STEP:
                                pe.wait_ge(s_mk, nb * MASK_OPS + 2 * MASK_OPS)
                            transpose_mask(mt_of(hp, mb), uses + m0_index["mask", hp, mb])
                        scores(nb, hp, mb, 1)
                        for gi in guards[1:]:
                            guard(it, par, gi, count)
                        if crow_of(mb) is not None:
                            x = crow_of(mb)
                            crow(it, x, uses + m0_index["crow", hp, x])
                        if step >= LAG:
                            products(nb, step - LAG)
                        elif not first:
                            products(nb - 1, step - LAG + STEPS)
                        if hp:
                            finish(nb, hp - 1, mb)
                        elif not first:
                            finish(nb - 1, HP - 1, mb)

            body(0, True)
            with pe.Fori(0, NB - 1) as i:
                body(i + 1, False)
            for step in range(STEPS - LAG, STEPS):
                products(NB - 1, step)
            for mb in range(NT):
                finish(NB - 1, HP - 1, mb)


def build(nc, DR):
    with ExitStack() as ctx:
        def sb(name, shape, dt=F32):
            return ctx.enter_context(nc.sbuf_tensor(name, shape, dt))

        T = {
            "identf": sb("identf", [P, P]), "identb": sb("identb", [P, P], BF16),
            "amax": sb("amax", [P, NT]),
        }
        with ExitStack() as layer0:
            def sb0(name, shape, dt=F32):
                return layer0.enter_context(nc.sbuf_tensor(name, shape, dt))

            T["V"] = sb0("V0", [P, NT, F])
            T["w"], T["v"], T["nv"] = (sb0(x, [P, NT, H]) for x in ("w", "v", "nv"))
            layer0_project(nc, T, DR)
            layer0_attention(nc, T, DR)
        layer1_project(nc, T, DR)
        layer1_attention(nc, T, DR)


_SCRATCH = [("amax", (N,), F32), ("r", (H, N), F32), ("x1", (N, F), F32), ("v1", (HP, N, 2 * P), F16),
            ("qh", (F, N), F16), ("ql", (F, N), F16), ("kh", (F, N), F16), ("kl", (F, N), F16)]


def kernel(**inputs):
    import numpy as np
    import concourse.bacc as bacc
    from concourse.bass_utils import run_bass_kernel_spmd

    a = {k: np.asarray(v) for k, v in inputs.items()}
    proj = np.zeros((F, 2 * H), np.float32)
    for hd in range(H):
        proj[hd * D:(hd + 1) * D, hd] = a["L0_gnn_src_proj"][0, hd]
        proj[hd * D:(hd + 1) * D, H + hd] = a["L0_gnn_trg_proj"][0, hd]
    arrays = {
        "x": a["x"], "adj": a["adj"], "adjT": a["adj"].T, "W0": a["L0_gnn_W"], "W0T": a["L0_gnn_W"].T,
        "b": a["L0_gnn_b"], "bcol": a["L0_gnn_b"].reshape(KC, P).T, "proj": proj,
        "Wk": a["L1_gnn_Wks"].transpose(1, 0, 2).reshape(F, F), "Wq": a["L1_gnn_Wqs"].transpose(1, 0, 2).reshape(F, F),
        "Wv": a["L1_gnn_Wvs"].transpose(1, 0, 2).reshape(F, F), "Wo": a["L1_gnn_Wo"].reshape(F, F),
        "selc": np.eye(1, P, D, dtype=np.float16).repeat(P, 0),
        "seld": np.eye(P, dtype=np.float32)[[0, 64]].repeat(D, 0).T + np.eye(P, dtype=np.float32)[[32, 96]].repeat(D, 0).T,
        "idh": np.eye(P, dtype=np.float16),
        "identf": np.eye(P, dtype=np.float32), "identb": np.eye(P, dtype=np.float32).astype(mybir.dt.np(BF16)),
    }
    arrays = {f"in_{k}": np.ascontiguousarray(v) for k, v in arrays.items()}
    nc = bacc.Bacc("TRN2", target_bir_lowering=False, num_devices=1)
    DR = {k[3:]: nc.dram_tensor(k, v.shape, mybir.dt.from_np(v.dtype), kind="ExternalInput").ap() for k, v in arrays.items()}
    DR |= {k: nc.dram_tensor(f"scratch_{k}", shape, dt, kind="Internal").ap() for k, shape, dt in _SCRATCH}
    DR["out"] = nc.dram_tensor("out_dram", (N, F), F32, kind="ExternalOutput").ap()
    build(nc, DR)
    return run_bass_kernel_spmd(nc, [arrays], core_ids=[0]).results[0]["out_dram"]
```

```python
import math
from contextlib import ExitStack

import concourse.bass as bass
from concourse import mybir

F32 = mybir.dt.float32
F16 = mybir.dt.float16
BF16 = mybir.dt.bfloat16
ALU = mybir.AluOpType
ACT = mybir.ActivationFunctionType
AX = mybir.AxisListType

P = 128
N = 4096
F = 512
H = 8
D = 64
HP = H // 2
NT = N // P
KC = F // P
QB = 512
NB = N // QB
SUB = QB // P
EPS = 1e-5

G_RING = 8
P_RING = 8
DEN = 32
QUAD = P // DEN
QK_SCALE = 256.0
W_SCALE = 256.0
H_SCALE = 16.0
TERMS = ((0, 0), (0, 1), (1, 0))
C_ROW = 4096.0
CREDIT = 2 * HP * NT


def wait_apart(eng, sem, value, passed):
    eng.wait_ge(sem, value)
    eng.sem_inc(passed, 1)


def layer0_project(nc, T, DR):
    with ExitStack() as ctx:
        def sb(name, shape, dt=F32):
            return ctx.enter_context(nc.sbuf_tensor(name, shape, dt))

        def pb(name, shape, dt=F32):
            return ctx.enter_context(nc.psum_tensor(name, shape, dt))

        def sem(name):
            return ctx.enter_context(nc.semaphore("a_" + name))

        rows = [sb(f"a_rows{s}", [P, N]) for s in range(SUB)]
        xg = sb("a_xg", [P, SUB, F])
        h = sb("a_h", [P, SUB, F])
        hT = sb("a_hT", [P, 2, KC, QB], F16)
        wT = sb("a_wT", [P, KC, F])
        wS = sb("a_wS", [P, 2, KC, F], F16)
        wn = sb("a_wn", [P, KC, F])
        pj = sb("a_pj", [P, KC, 2 * H])
        wpj = sb("a_wpj", [P, KC, 2 * H])
        wpjS = sb("a_wpjS", [P, 2, KC, 2 * H], F16)
        bcol = sb("a_bcol", [P, KC])
        bias = sb("a_bias", [P, F])
        bp = sb("a_bp", [2 * H, 1])
        stats = sb("a_stats", [P, SUB, 6])
        mv = sb("a_mv", [P, SUB, 2])
        std = sb("a_std", [P, SUB])
        rstd = sb("a_rstd", [P, SUB])
        nmr = sb("a_nmr", [P, SUB])
        eps = sb("a_eps", [P, 1])
        st = sb("a_st", [2 * H, QB])
        r_sb = sb("a_r", [H, QB])
        am_row = sb("a_am_row", [NT, P])

        tp = [pb(f"a_tp{i}", [P, QB]) for i in range(2)]
        vp = [pb(f"a_vp{i}", [P, F]) for i in range(SUB)]
        stp = pb("a_stp", [2 * H, QB])
        small = pb("a_small", [P, 3, P])
        tq = small[:, 0, 0:SUB * 2 * H].rearrange("p (s k) -> p s k", s=SUB)
        setup, amp = small[:, 1, 0:KC * 2 * H], small[0:NT, 2, :]

        s_passed = sem("waits_passed")
        s_w = sem("w_in")
        s_row = [sem(f"row_in{s}") for s in range(SUB)]
        s_x = [sem(f"x_in{s}") for s in range(SUB)]
        s_rank = sem("row_ranked")
        s_wh = sem("weights_high")
        s_ws = sem("weights_split")
        s_hTh = sem("hT_high")
        s_nv = sem("nv_done")
        s_chain = sem("vector_chain")
        s_eps = sem("eps")
        s_mv = sem("variance")
        s_std = sem("std")
        s_norm = sem("norm")
        s_h = sem("h")
        s_tp = sem("transposed")
        s_hT = sem("hT")
        s_set = sem("projected_weights")
        s_setc = sem("projected_weights_copied")
        s_stp = sem("st_psum")
        s_st = sem("st")
        s_tq = sem("t_columns")
        s_wv = sem("wv")
        s_r = sem("r")
        s_rout = sem("r_stored")
        s_vp = sem("v_psum")
        s_v = sem("v_done")
        s_amp = sem("amax_transposed")
        s_am = sem("amax_row")
        s_amout = sem("amax_stored")

        block = ctx.enter_context(nc.Block())

        @block.sync
        def _(sp):
            sp.dma_start(T["identf"][:, :], DR["identf"]).then_inc(s_w, 16)
            sp.dma_start(T["identb"][:, :], DR["identb"]).then_inc(s_w, 16)
            sp.dma_start(wT[:, :, :], DR["W0T"].rearrange("(c p) n -> p c n", p=P)).then_inc(s_w, 16)
            sp.dma_start(wn[:, :, :], DR["W0"].rearrange("(c p) n -> p c n", p=P)).then_inc(s_w, 16)
            sp.dma_start(pj[:, :, :], DR["proj"].rearrange("(c p) n -> p c n", p=P)).then_inc(s_w, 16)
            sp.dma_start(bcol[:, :], DR["bcol"]).then_inc(s_w, 16)
            sp.dma_start(bias[:, :], DR["b"].partition_broadcast(P)).then_inc(s_w, 16)
            sp.sem_inc(s_rank, SUB)
            with sp.Fori(0, NB) as g:
                for s in range(SUB):
                    sp.wait_ge(s_rank, g * SUB + (s + 1))
                    sp.dma_start(rows[s][:, :], DR["adj"][bass.ds(g * QB + s * P, P), :]).then_inc(s_row[s], 16)
            sp.wait_ge(s_am, 1)
            sp.dma_start(DR["amax"].rearrange("(t p) -> t p", p=P), am_row[:, :]).then_inc(s_amout, 16)
            sp.wait_ge(s_amout, 16)

        def load_x(pool, g):
            for s in range(SUB):
                wait_apart(pool, s_h, g * SUB + (s + 1), s_passed)
                pool.dma_start(xg[:, s, :], DR["x"][bass.ds(g * QB + s * P, P), :]).then_inc(s_x[s], 16)

        def in_blocks(eng, body):
            with eng.Fori(0, NB - 1) as g:
                body(g, False)
            body(NB - 1, True)

        @block.gpsimd
        def _(pool):
            pool.memset(eps[:, :], EPS).then_inc(s_eps, 1)
            pool.sem_inc(s_h, SUB)
            load_x(pool, 0)

            def body(g, last):
                if not last:
                    load_x(pool, g + 1)

            in_blocks(pool, body)

        @block.vector
        def _(dve):
            dve.wait_ge(s_set, 1)
            nc.vector.tensor_copy(wpj[:, :, :], setup.rearrange("p (c k) -> p c k", c=KC)).then_inc(s_setc, 1)
            dve.wait_ge(s_set, 2)
            nc.vector.tensor_copy(bp[:, :], setup[0:2 * H, 0:1]).then_inc(s_setc, 1)
            dve.wait_ge(s_wh, 1)
            nc.vector.scalar_tensor_tensor(out=wS[:, 1, :, :], in0=wT[:, :, :], scalar=W_SCALE, in1=wS[:, 0, :, :],
                                           op0=ALU.mult, op1=ALU.subtract).then_inc(s_ws, 1)
            dve.wait_ge(s_wh, 2)
            nc.vector.scalar_tensor_tensor(out=wpjS[:, 1, :, :], in0=wpj[:, :, :], scalar=W_SCALE, in1=wpjS[:, 0, :, :],
                                           op0=ALU.mult, op1=ALU.subtract).then_inc(s_ws, 1)

            def bn(g, s):
                dve.wait_ge(s_x[s], g * 16 + 16)
                nc.vector.bn_stats(stats[:, s, :], xg[:, s, :]).then_inc(s_chain, 1)

            def aggregate(g):
                wait_apart(dve, s_chain, g * (SUB + 1) + SUB, s_passed)
                for s in range(SUB):
                    nc.vector.bn_aggr(mv[:, s, :], stats[:, s, :]).then_inc(s_mv, 1)

            def norm(g):
                dve.wait_ge(s_std, g + 1)
                nc.vector.reciprocal(rstd[:, :], std[:, :]).then_inc(s_chain, 1)
                dve.wait_ge(s_chain, g * (SUB + 1) + (SUB + 1))
                nc.vector.scalar_tensor_tensor(out=nmr[:, :], in0=mv[:, :, 0], scalar=-1.0, in1=rstd[:, :],
                                               op0=ALU.mult, op1=ALU.mult).then_inc(s_norm, 1)

            def rank(g, s):
                dve.wait_ge(s_row[s], g * 16 + 16)
                nc.vector.reduce_max(T["amax"][:, bass.ds(g * SUB + s, 1)], rows[s][:, :], AX.X).then_inc(s_rank, 1)

            def store_v(g, s):
                dve.wait_ge(s_vp, g * SUB + (s + 1))
                nc.vector.scalar_tensor_tensor(out=T["V"][:, bass.ds(g * SUB + s, 1), :].rearrange("p a n -> p (a n)"),
                                               in0=vp[s][:, :], scalar=1.0 / (W_SCALE * H_SCALE), in1=bias[:, :],
                                               op0=ALU.mult, op1=ALU.add).then_inc(s_v, 1)

            for s in range(SUB):
                bn(0, s)
            aggregate(0)
            norm(0)

            def body(g, last):
                for c in range(KC):
                    dve.wait_ge(s_hTh, g * KC + (c + 1))
                    nc.vector.scalar_tensor_tensor(out=hT[:, 1, c, :], in0=tp[c % 2][:, :], scalar=H_SCALE, in1=hT[:, 0, c, :],
                                                   op0=ALU.mult, op1=ALU.subtract).then_inc(s_hT, 1)
                rank(g, 0)
                if not last:
                    for s in range(SUB):
                        bn(g + 1, s)
                    aggregate(g + 1)
                store_v(g, 0)
                store_v(g, 1)
                rank(g, 1)
                if not last:
                    norm(g + 1)
                dve.wait_ge(s_wv, g * 2 + 2)
                nc.vector.tensor_scalar(T["nv"][:, bass.ds(g * SUB, SUB), :], T["v"][:, bass.ds(g * SUB, SUB), :],
                                        -1.0, None, ALU.mult).then_inc(s_nv, 1)
                store_v(g, 2)
                store_v(g, 3)
                rank(g, 2)
                rank(g, 3)

            in_blocks(dve, body)
            dve.wait_ge(s_amp, 1)
            nc.vector.tensor_copy(am_row[:, :], amp).then_inc(s_am, 1)

        @block.scalar
        def _(act):
            act.wait_ge(s_w, 16 * 7)
            nc.scalar.activation(wS[:, 0, :, :], wT[:, :, :], ACT.Copy, scale=W_SCALE).then_inc(s_wh, 1)
            act.wait_ge(s_setc, 2)
            nc.scalar.activation(wpjS[:, 0, :, :], wpj[:, :, :], ACT.Copy, scale=W_SCALE).then_inc(s_wh, 1)
            act.wait_ge(s_eps, 1)
            act.sem_inc(s_rout, 16)

            def root(g):
                act.wait_ge(s_mv, g * SUB + SUB)
                nc.scalar.activation(std[:, :], mv[:, :, 1], ACT.Sqrt, bias=eps[:, :]).then_inc(s_std, 1)

            def relu(g):
                act.wait_ge(s_norm, g + 1)
                for s in range(SUB):
                    nc.scalar.activation(h[:, s, :], xg[:, s, :], ACT.Relu, bias=nmr[:, s:s + 1],
                                         scale=rstd[:, s:s + 1]).then_inc(s_h, 1)

            root(0)
            relu(0)

            def body(g, last):
                for c in range(KC):
                    act.wait_ge(s_tp, g * KC + (c + 1))
                    nc.scalar.activation(hT[:, 0, c, :], tp[c % 2][:, :], ACT.Copy, scale=H_SCALE).then_inc(s_hTh, 1)
                act.wait_ge(s_stp, g + 1)
                nc.scalar.activation(st[:, :], stp[:, :], ACT.Identity, bias=bp[:, :],
                                     scale=1.0 / (W_SCALE * H_SCALE)).then_inc(s_st, 1)
                act.wait_ge(s_rout, g * 16 + 16)
                act.wait_ge(s_st, g + 1)
                nc.scalar.activation(r_sb[:, :], st[0:H, :], ACT.Exp, scale=0.99).then_inc(s_r, 1)
                act.wait_ge(s_r, g + 1)
                act.dma_start(DR["r"][:, bass.ds(g * QB, QB)], r_sb[:, :]).then_inc(s_rout, 16)
                act.wait_ge(s_tq, g + 1)
                nc.scalar.activation(T["w"][:, bass.ds(g * SUB, SUB), :], tq[:, :, H:2 * H], ACT.Exp).then_inc(s_wv, 1)
                nc.scalar.activation(T["v"][:, bass.ds(g * SUB, SUB), :], tq[:, :, H:2 * H], ACT.Exp,
                                     scale=0.01).then_inc(s_wv, 1)
                if not last:
                    root(g + 1)
                    relu(g + 1)

            in_blocks(act, body)
            act.wait_ge(s_rout, 16 * NB + 16)

        @block.tensor
        def _(pe):
            pe.wait_ge(s_w, 16 * 7)
            for c in range(KC):
                for k in range(KC):
                    mm = nc.tensor.matmul(setup[:, c * 2 * H:(c + 1) * 2 * H], wn[:, k, c * P:(c + 1) * P], pj[:, k, :],
                                          start=(k == 0), stop=(k == KC - 1), skip_group_check=True)
            mm.then_inc(s_set, 1)
            pe.wait_ge(s_setc, 1)
            for k in range(KC):
                mm = nc.tensor.matmul(setup[0:2 * H, 0:1], pj[:, k, :], bcol[:, k:k + 1],
                                      start=(k == 0), stop=(k == KC - 1))
            mm.then_inc(s_set, 1)
            pe.sem_inc(s_hT, 2)
            pe.sem_inc(s_v, SUB)
            pe.wait_ge(s_ws, 2)

            def body(g, last):
                for c in range(KC):
                    if c == 0:
                        pe.wait_ge(s_h, g * SUB + 2 * SUB)
                    pe.wait_ge(s_hT, g * KC + (c + 1))
                    for s in range(SUB):
                        mm = nc.tensor.transpose(tp[c % 2][:, s * P:(s + 1) * P], h[:, s, c * P:(c + 1) * P],
                                                 T["identf"][:, :])
                    mm.then_inc(s_tp, 1)
                pe.wait_ge(s_hT, g * KC + KC + 2)
                for c in range(KC):
                    for i, j in TERMS:
                        mm = nc.tensor.matmul(stp[:, :], wpjS[:, i, c, :], hT[:, j, c, :],
                                              start=(c == 0 and i == j == 0), stop=(c == KC - 1 and i == 1))
                mm.then_inc(s_stp, 1)
                for s in range(SUB):
                    pe.wait_ge(s_v, g * SUB + (s + 1))
                    for c in range(KC):
                        for i, j in TERMS:
                            mm = nc.tensor.matmul(vp[s][:, :], hT[:, i, c, s * P:(s + 1) * P], wS[:, j, c, :],
                                                  start=(c == 0 and i == j == 0), stop=(c == KC - 1 and i == 1))
                    mm.then_inc(s_vp, 1)
                    if s == 1:
                        wait_apart(pe, s_st, g + 1, s_passed)
                        for u in range(SUB):
                            mm = nc.tensor.transpose(tq[:, u, :], st[:, u * P:(u + 1) * P], T["identf"][0:2 * H, 0:2 * H])
                        mm.then_inc(s_tq, 1)

            in_blocks(pe, body)
            pe.wait_ge(s_rank, SUB + NT)
            nc.tensor.transpose(amp, T["amax"][:, :], T["identf"][:, :]).then_inc(s_amp, 1)


def layer0_attention(nc, T, DR):
    TILES = 2 * HP * NT
    TILES_P = TILES // QUAD
    TILES_V = TILES - TILES_P
    QUADS = TILES // QUAD
    GROUPS = 4
    PER = NT // GROUPS
    AHEAD = PER
    PREP_STEP = NT - 4 - AHEAD
    EXP_LAG = 2
    COPY_STEP, FIN_STEP, STORE_STEP = 4, 10, 12

    def by_pool(t):
        return t % QUAD == QUAD - 1

    def nth(t):
        return t // QUAD + 1 if by_pool(t) else (QUAD - 1) * (t // QUAD) + t % QUAD + 1

    def prepared_at(hp, mb):
        if hp == HP - 1 and 0 <= mb - PREP_STEP < AHEAD:
            return 1, mb - PREP_STEP
        if hp == 0 and mb + AHEAD < NT:
            return 0, mb + AHEAD
        return None

    def exp_at(hp, mb):
        return prepared_at(hp, mb - EXP_LAG) if mb >= EXP_LAG else None

    with ExitStack() as ctx:
        def sb(name, shape, dt=F32):
            return ctx.enter_context(nc.sbuf_tensor(name, shape, dt))

        def pb(name, shape, dt=F32):
            return ctx.enter_context(nc.psum_tensor(name, shape, dt))

        def sem(name):
            return ctx.enter_context(nc.semaphore("b_" + name))

        A = sb("b_A", [P, NT, QB])
        R = sb("b_R", [P, H, QB])
        am = sb("b_am", [P, QB])
        G = sb("b_G", [P, G_RING, QB])
        PT = sb("b_P", [P, P_RING, QB])
        ones = sb("b_ones", [P, DEN])
        xg = sb("b_xg", [P, SUB, F])
        oT = sb("b_oT", [P, QB])
        dT = sb("b_dT", [P, QB])
        dsum = sb("b_dsum", [P, SUB, 2])
        rden = sb("b_rden", [P, SUB, 2])
        o = sb("b_o", [P, SUB, P])

        acc = [pb(f"b_acc{i}", [P, QB]) for i in range(2)]
        den = [pb(f"b_den{i}", [P, QB]) for i in range(2)]
        fin_o = pb("b_fin_o", [P, SUB, P])
        fin_d = pb("b_fin_d", [P, SUB, P])

        s_passed = sem("waits_passed")
        s_ones = sem("ones")
        s_am = sem("amax_in")
        s_R = [sem(f"r_in{i}") for i in range(HP)]
        s_A = [sem(f"adj_in{i}") for i in range(GROUPS)]
        s_sub = sem("adj_shifted_by_vector")
        s_subp = sem("adj_shifted_by_gpsimd")
        s_exp = sem("adj_exp")
        s_G = sem("g_ready")
        s_U = sem("u_ready")
        s_P = sem("p_by_vector")
        s_Pp = sem("p_by_gpsimd")
        s_used = sem("p_used")
        s_copy = sem("acc_copied")
        s_fin = sem("fin_ready")
        s_chain = sem("vector_chain")
        s_done = sem("x1_part_done")
        s_x = sem("x_in")
        s_out = sem("x1_stored")

        block = ctx.enter_context(nc.Block())

        def in_blocks(eng, body):
            body(0, True, False)
            with eng.Fori(0, NB - 2) as i:
                body(i + 1, False, False)
            body(NB - 1, False, True)

        @block.sync
        def _(sp):
            def load_am(nb):
                sp.dma_start(am[:, :], DR["amax"][bass.ds(nb * QB, QB)].partition_broadcast(P)).then_inc(s_am, 16)

            def load_r(nb, hp):
                for x in range(2):
                    src = DR["r"][2 * hp + x, bass.ds(nb * QB, QB)]
                    sp.dma_start(R[:, 2 * hp + x, :], src.partition_broadcast(P)).then_inc(s_R[hp], 16)

            def load_a(nb, i):
                src = DR["adjT"][i * PER * P:(i + 1) * PER * P, bass.ds(nb * QB, QB)]
                sp.dma_start(A[:, i * PER:(i + 1) * PER, :], src.rearrange("(m p) n -> p m n", p=P)).then_inc(s_A[i], 16)

            def store(nb):
                wait_apart(sp, s_done, nb * HP + (HP + 1), s_passed)
                sp.dma_start(DR["x1"][bass.ds(nb * QB, QB), :].rearrange("(s p) f -> p s f", p=P), xg[:, :, :]).then_inc(s_out, 16)
                wait_apart(sp, s_out, nb * 16 + 16, s_passed)

            load_am(0)
            load_a(0, 0)
            load_r(0, 0)
            for i in range(1, GROUPS):
                load_a(0, i)
            for hp in range(1, HP):
                load_r(0, hp)

            def body(nb, first, last):
                for hp in range(HP):
                    for mb in range(NT):
                        step = hp * NT + mb
                        if hp == 0 and mb == STORE_STEP:
                            if not first:
                                store(nb - 1)
                            sp.dma_start(xg[:, :, :], DR["x"][bass.ds(nb * QB, QB), :].rearrange("(s p) f -> p s f", p=P)).then_inc(s_x, 16)
                        if last:
                            continue
                        if hp == 0 and mb == NT - 1:
                            wait_apart(sp, s_sub, nb * (NT // 2) + NT // 2, s_passed)
                            wait_apart(sp, s_subp, nb * (NT // 2) + NT // 2, s_passed)
                            load_am(nb + 1)
                        if mb == NT - 1:
                            t = 2 * step + 1
                            wait_apart(sp, s_G, nb * TILES_V + nth(t - 1), s_passed)
                            wait_apart(sp, s_U, nb * TILES_P + nth(t), s_passed)
                            load_r(nb + 1, hp)
                        if hp == HP - 1 and mb % PER == PER - 1:
                            t = 2 * step + 1
                            wait_apart(sp, s_P, nb * TILES_V + (TILES_V + nth(t - 1)), s_passed)
                            wait_apart(sp, s_Pp, nb * TILES_P + (TILES_P + nth(t)), s_passed)
                            load_a(nb + 1, mb // PER)

            in_blocks(sp, body)
            store(NB - 1)

        def shift_adj(eng, engine, nb, m):
            if m < 2:
                engine.wait_ge(s_am, nb * 16 + 16)
            engine.wait_ge(s_A[m // PER], nb * 16 + 16)
            eng.tensor_tensor(A[:, m, :], A[:, m, :], am[:, :], ALU.subtract).then_inc(s_sub if m % 2 else s_subp, 1)

        @block.gpsimd
        def _(pool):
            pool.memset(ones[:, :], 1.0).then_inc(s_ones, 1)
            pool.sem_inc(s_Pp, TILES_P)
            for m in range(0, AHEAD, 2):
                shift_adj(nc.gpsimd, pool, 0, m)

            def body(nb, first, last):
                for hp in range(HP):
                    for mb in range(NT):
                        prep = prepared_at(hp, mb)
                        if prep and prep[1] % 2 == 0 and not (last and prep[0]):
                            shift_adj(nc.gpsimd, pool, nb + prep[0], prep[1])
                        t = 2 * (hp * NT + mb) + 1
                        if not by_pool(t):
                            continue
                        if hp == 0:
                            pool.wait_ge(s_exp, nb * NT + (mb + 1))
                        pool.wait_ge(s_used, nb * QUADS + (t // QUAD + 1))
                        pool.wait_ge(s_U, nb * TILES_P + nth(t))
                        nc.gpsimd.tensor_tensor(PT[:, t % P_RING, :], G[:, t % G_RING, :], A[:, mb, :], ALU.mult).then_inc(s_Pp, 1)

            in_blocks(pool, body)

        @block.scalar
        def _(act):
            def exp_adj(nb, m):
                act.wait_ge(s_sub if m % 2 else s_subp, nb * (NT // 2) + (m // 2 + 1))
                nc.scalar.activation(A[:, m, :], A[:, m, :], ACT.Exp).then_inc(s_exp, 1)

            for m in range(AHEAD):
                exp_adj(0, m)

            def body(nb, first, last):
                for hp in range(HP):
                    act.wait_ge(s_R[hp], nb * 32 + 32)
                    for mb in range(NT):
                        for x in range(2):
                            t = 2 * (hp * NT + mb) + x
                            if by_pool(t):
                                continue
                            act.wait_ge(s_P, nb * TILES_V + (TILES_V + nth(t) - G_RING // QUAD * (QUAD - 1)))
                            head = 2 * hp + x
                            nc.scalar.activation(G[:, t % G_RING, :], R[:, head, :], ACT.Relu,
                                                 bias=T["nv"][:, mb, head:head + 1],
                                                 scale=T["w"][:, mb, head:head + 1]).then_inc(s_G, 1)
                        prep = exp_at(hp, mb)
                        if prep and not (last and prep[0]):
                            exp_adj(nb + prep[0], prep[1])

            in_blocks(act, body)

        @block.vector
        def _(dve):
            dve.sem_inc(s_P, TILES_V)

            def copy_acc(nb, hp):
                dve.wait_ge(s_used, nb * QUADS + (P_RING // QUAD + (hp + 1) * 2 * NT // QUAD))
                nc.vector.tensor_copy(oT[:, :], acc[hp % 2][:, :]).then_inc(s_copy, 1)
                nc.vector.tensor_copy(dT[:, :], den[hp % 2][:, :]).then_inc(s_copy, 1)

            def divide(nb, hp):
                dve.wait_ge(s_fin, nb * HP + (hp + 1))
                view = fin_d[:, :, :].rearrange("p s (e j c) -> p s j e c", e=2, j=2)[:, :, :, :, 0]
                nc.vector.tensor_reduce(dsum[:, :, :], view, AX.X, ALU.add).then_inc(s_chain, 1)
                at = nb * (HP * 3) + hp * 3
                dve.wait_ge(s_chain, at + 1)
                nc.vector.reciprocal(rden[:, :, :], dsum[:, :, :]).then_inc(s_chain, 1)
                dve.wait_ge(s_chain, at + 2)
                nc.vector.tensor_tensor(o[:, :, :].rearrange("p s (j d) -> p s j d", j=2),
                                        fin_o[:, :, :].rearrange("p s (j d) -> p s j d", j=2),
                                        rden[:, :, :].unsqueeze(3).to_broadcast([P, SUB, 2, D]), ALU.mult).then_inc(s_chain, 1)
                dve.wait_ge(s_chain, at + 3)
                if hp == 0:
                    dve.wait_ge(s_x, nb * 16 + 16)
                cols = slice(hp * P, (hp + 1) * P)
                nc.vector.tensor_tensor(xg[:, :, cols], xg[:, :, cols], o[:, :, :], ALU.add).then_inc(s_done, 1)

            def finish(nb, hp, mb):
                if mb == COPY_STEP:
                    copy_acc(nb, hp)
                if mb == FIN_STEP:
                    divide(nb, hp)

            for m in range(1, AHEAD, 2):
                shift_adj(nc.vector, dve, 0, m)

            def body(nb, first, last):
                for hp in range(HP):
                    for mb in range(NT):
                        q, head = 2 * (hp * NT + mb) // QUAD, 2 * hp + 1
                        prep = prepared_at(hp, mb)
                        if prep and prep[1] % 2 and not (last and prep[0]):
                            shift_adj(nc.vector, dve, nb + prep[0], prep[1])
                        if mb % 2 == 0:
                            t = QUAD * q + QUAD - 1
                            if mb == 0:
                                dve.wait_ge(s_R[hp], nb * 32 + 32)
                            dve.wait_ge(s_Pp, nb * TILES_P + (TILES_P + nth(t) - G_RING // QUAD))
                            nc.vector.tensor_scalar(G[:, t % G_RING, :], R[:, head, :], T["w"][:, mb + 1, head:head + 1],
                                                    T["v"][:, mb + 1, head:head + 1], ALU.mult, ALU.max).then_inc(s_U, 1)
                            dve.wait_ge(s_used, nb * QUADS + (q + 1))
                        if hp == 0:
                            dve.wait_ge(s_exp, nb * NT + (mb + 1))
                        for x in range(2):
                            t = 2 * (hp * NT + mb) + x
                            if by_pool(t):
                                continue
                            dve.wait_ge(s_G, nb * TILES_V + nth(t))
                            nc.vector.scalar_tensor_tensor(out=PT[:, t % P_RING, :], in0=G[:, t % G_RING, :],
                                                           scalar=T["v"][:, mb, 2 * hp + x:2 * hp + x + 1], in1=A[:, mb, :],
                                                           op0=ALU.add, op1=ALU.mult).then_inc(s_P, 1)
                        if hp:
                            finish(nb, hp - 1, mb)
                        elif not first:
                            finish(nb - 1, HP - 1, mb)

            in_blocks(dve, body)
            for mb in range(NT):
                finish(NB - 1, HP - 1, mb)

        @block.tensor
        def _(pe):
            pe.wait_ge(s_ones, 1)
            pe.sem_inc(s_used, P_RING // QUAD)
            pe.sem_inc(s_copy, 4)
            pe.sem_inc(s_done, 1)

            def transposes(nb, hp):
                pe.wait_ge(s_copy, nb * (2 * HP) + (2 * hp + 6))
                pe.wait_ge(s_done, nb * HP + (hp + 1))
                for s in range(SUB):
                    nc.tensor.transpose(fin_o[:, s, :], oT[:, s * P:(s + 1) * P], T["identf"][:, :])
                for s in range(SUB):
                    mm = nc.tensor.transpose(fin_d[:, s, :], dT[:, s * P:(s + 1) * P], T["identf"][:, :])
                mm.then_inc(s_fin, 1)

            def body(nb, first, last):
                for hp in range(HP):
                    pe.wait_ge(s_copy, nb * (2 * HP) + (2 * hp + 2))
                    for j in range(2 * NT // QUAD):
                        t0 = 2 * hp * NT + QUAD * j
                        for i in range(QUAD):
                            t = t0 + i
                            mb, x = (t // 2) % NT, t % 2
                            head = 2 * hp + x
                            if by_pool(t):
                                pe.wait_ge(s_Pp, nb * TILES_P + (TILES_P + nth(t)))
                            else:
                                pe.wait_ge(s_P, nb * TILES_V + (TILES_V + nth(t)))
                            nc.tensor.matmul(acc[hp % 2][x * D:(x + 1) * D, :], T["V"][:, mb, head * D:(head + 1) * D],
                                             PT[:, t % P_RING, :], start=(mb == 0), stop=(mb == NT - 1))
                        for i in range(QUAD):
                            t = t0 + i
                            mm = nc.tensor.matmul(den[hp % 2][i * DEN:(i + 1) * DEN, :], ones[:, :], PT[:, t % P_RING, :],
                                                  start=(j == 0), stop=(j == 2 * NT // QUAD - 1), tile_position=(0, i * DEN))
                        mm.then_inc(s_used, 1)
                        if j == 3 and hp:
                            transposes(nb, hp - 1)
                        elif j == 3 and not first:
                            transposes(nb - 1, HP - 1)

            in_blocks(pe, body)
            transposes(NB - 1, HP - 1)


def layer1_project(nc, T, DR):
    RING = 4
    UNSCALE = QK_SCALE / (W_SCALE * H_SCALE)
    PAIRS = 2 * HP
    with ExitStack() as ctx:
        def sb(name, shape, dt=F32):
            return ctx.enter_context(nc.sbuf_tensor(name, shape, dt))

        def pb(name, shape, dt=F32):
            return ctx.enter_context(nc.psum_tensor(name, shape, dt))

        def sem(name):
            return ctx.enter_context(nc.semaphore("c_" + name))

        xg = sb("c_xg", [P, SUB, F])
        h = sb("c_h", [P, SUB, F])
        hT = sb("c_hT", [P, 2, KC, QB], F16)
        W = [sb(f"c_w{x}", [P, KC, F]) for x in "qkv"]
        WS = [sb(f"c_w{x}S", [P, 2, KC, F], F16) for x in "qkv"]
        stats = sb("c_stats", [P, SUB, 6])
        mv = sb("c_mv", [P, SUB, 2])
        std = sb("c_std", [P, SUB])
        rstd = sb("c_rstd", [P, SUB])
        nmr = sb("c_nmr", [P, SUB])
        eps = sb("c_eps", [P, 1])
        hi = sb("c_hi", [P, RING, QB], F16)
        lo = sb("c_lo", [P, RING, QB], F16)
        vt = sb("c_vt", [P, SUB, HP, 2, P], F16)

        tp = [pb(f"c_tp{i}", [P, QB]) for i in range(KC)]
        qp = [pb(f"c_qp{i}", [P, QB]) for i in range(2)]
        vp = [pb(f"c_vp{i}", [P, F]) for i in range(2)]

        s_passed = sem("waits_passed")
        s_w = sem("w_in")
        s_x = [sem(f"x_in{s}") for s in range(SUB)]
        s_chain = sem("vector_chain")
        s_eps = sem("eps")
        s_mv = sem("variance")
        s_std = sem("std")
        s_norm = sem("norm")
        s_h = sem("h")
        s_wh = sem("weights_high")
        s_ws = sem("weights_split")
        s_hTh = sem("hT_high")
        s_tp = sem("transposed")
        s_hT = sem("hT")
        s_qp = sem("qk_psum")
        s_hi = sem("hi")
        s_lo = sem("lo")
        s_qout = [sem(f"qk_stored{i}") for i in range(RING)]
        s_vp = sem("v_psum")
        s_vh = sem("v_high")
        s_v = sem("v_split")
        s_vout = sem("v_stored")

        block = ctx.enter_context(nc.Block())

        @block.sync
        def _(sp):
            for w, name in zip(W, ("Wq", "Wk", "Wv")):
                sp.dma_start(w[:, :, :], DR[name].rearrange("(c p) n -> p c n", p=P)).then_inc(s_w, 16)
            for i in range(RING):
                sp.sem_inc(s_qout[i], 32)
            sp.sem_inc(s_vout, 16 * SUB)
            with sp.Fori(0, NB) as g:
                for j in range(PAIRS):
                    sp.wait_ge(s_lo, g * PAIRS + (j + 1))
                    row, i, to = (j % HP) * P, j % RING, "qk"[j // HP]
                    for half, tile in (("h", hi), ("l", lo)):
                        sp.dma_start(DR[to + half][row:row + P, bass.ds(g * QB, QB)], tile[:, i, :]).then_inc(s_qout[i], 16)
                for s in range(SUB):
                    sp.wait_ge(s_v, g * SUB + (s + 3))
                    sp.dma_start(DR["v1"][:, bass.ds(g * QB + s * P, P), :].rearrange("h p k -> p h k"),
                                 vt[:, s, :, :, :].rearrange("p h a k -> p h (a k)")).then_inc(s_vout, 16)
            for i in range(RING):
                sp.wait_ge(s_qout[i], 32 * (NB * PAIRS // RING + 1))
            sp.wait_ge(s_vout, 16 * SUB * (NB + 1))

        def in_blocks(eng, body):
            with eng.Fori(0, NB - 1) as g:
                body(g, False)
            body(NB - 1, True)

        @block.gpsimd
        def _(pool):
            pool.memset(eps[:, :], EPS).then_inc(s_eps, 1)
            pool.sem_inc(s_h, SUB)
            with pool.Fori(0, NB) as g:
                for s in range(SUB):
                    wait_apart(pool, s_h, g * SUB + (s + 1), s_passed)
                    pool.dma_start(xg[:, s, :], DR["x1"][bass.ds(g * QB + s * P, P), :]).then_inc(s_x[s], 16)

        @block.vector
        def _(dve):
            def bn(g, s):
                dve.wait_ge(s_x[s], g * 16 + 16)
                nc.vector.bn_stats(stats[:, s, :], xg[:, s, :]).then_inc(s_chain, 1)

            def aggregate(g):
                wait_apart(dve, s_chain, g * (SUB + 1) + SUB, s_passed)
                for s in range(SUB):
                    nc.vector.bn_aggr(mv[:, s, :], stats[:, s, :]).then_inc(s_mv, 1)

            def norm(g):
                dve.wait_ge(s_std, g + 1)
                nc.vector.reciprocal(rstd[:, :], std[:, :]).then_inc(s_chain, 1)
                dve.wait_ge(s_chain, g * (SUB + 1) + (SUB + 1))
                nc.vector.scalar_tensor_tensor(out=nmr[:, :], in0=mv[:, :, 0], scalar=-1.0, in1=rstd[:, :],
                                               op0=ALU.mult, op1=ALU.mult).then_inc(s_norm, 1)

            for s in range(SUB):
                bn(0, s)
            aggregate(0)
            norm(0)
            for i in range(3):
                dve.wait_ge(s_wh, i + 1)
                nc.vector.scalar_tensor_tensor(out=WS[i][:, 1, :, :], in0=W[i][:, :, :], scalar=W_SCALE, in1=WS[i][:, 0, :, :],
                                               op0=ALU.mult, op1=ALU.subtract).then_inc(s_ws, 1)

            def body(g, last):
                for c in range(KC):
                    dve.wait_ge(s_hTh, g * KC + (c + 1))
                    nc.vector.scalar_tensor_tensor(out=hT[:, 1, c, :], in0=tp[c][:, :], scalar=H_SCALE, in1=hT[:, 0, c, :],
                                                   op0=ALU.mult, op1=ALU.subtract).then_inc(s_hT, 1)
                for j in range(PAIRS):
                    dve.wait_ge(s_hi, g * PAIRS + (j + 1))
                    nc.vector.scalar_tensor_tensor(out=lo[:, j % RING, :], in0=qp[j % 2][:, :], scalar=UNSCALE,
                                                   in1=hi[:, j % RING, :], op0=ALU.mult, op1=ALU.subtract).then_inc(s_lo, 1)
                    if not last and j < SUB:
                        bn(g + 1, j)
                    if not last and j == SUB:
                        aggregate(g + 1)
                    if not last and j == SUB + 1:
                        norm(g + 1)
                for s in range(SUB):
                    dve.wait_ge(s_vh, g * SUB + (s + 1))
                    nc.vector.scalar_tensor_tensor(out=vt[:, s, :, 1, :], in0=vp[s % 2][:, :].rearrange("p (h k) -> p h k", h=HP),
                                                   scalar=UNSCALE, in1=vt[:, s, :, 0, :], op0=ALU.mult,
                                                   op1=ALU.subtract).then_inc(s_v, 1)

            in_blocks(dve, body)

        @block.scalar
        def _(act):
            act.wait_ge(s_eps, 1)

            def root(g):
                act.wait_ge(s_mv, g * SUB + SUB)
                nc.scalar.activation(std[:, :], mv[:, :, 1], ACT.Sqrt, bias=eps[:, :]).then_inc(s_std, 1)

            def relu(g, s):
                if s == 0:
                    act.wait_ge(s_norm, g + 1)
                nc.scalar.activation(h[:, s, :], xg[:, s, :], ACT.Relu, bias=nmr[:, s:s + 1],
                                     scale=rstd[:, s:s + 1]).then_inc(s_h, 1)

            act.wait_ge(s_w, 16 * 3)
            for i in range(3):
                nc.scalar.activation(WS[i][:, 0, :, :], W[i][:, :, :], ACT.Copy, scale=W_SCALE).then_inc(s_wh, 1)
            root(0)
            for s in range(SUB):
                relu(0, s)

            def body(g, last):
                for c in range(KC):
                    act.wait_ge(s_tp, g * KC + (c + 1))
                    nc.scalar.activation(hT[:, 0, c, :], tp[c][:, :], ACT.Copy, scale=H_SCALE).then_inc(s_hTh, 1)
                for j in range(PAIRS):
                    act.wait_ge(s_qout[j % RING], g * (32 * PAIRS // RING) + 32 * (j // RING + 1))
                    act.wait_ge(s_qp, g * PAIRS + (j + 1))
                    nc.scalar.activation(hi[:, j % RING, :], qp[j % 2][:, :], ACT.Copy, scale=UNSCALE).then_inc(s_hi, 1)
                    if not last and j == SUB:
                        root(g + 1)
                act.wait_ge(s_vout, g * (16 * SUB) + 16 * SUB)
                for s in range(SUB):
                    act.wait_ge(s_vp, g * SUB + (s + 1))
                    nc.scalar.activation(vt[:, s, :, 0, :], vp[s % 2][:, :].rearrange("p (h k) -> p h k", h=HP), ACT.Copy,
                                         scale=UNSCALE).then_inc(s_vh, 1)
                    if not last:
                        relu(g + 1, s)

            in_blocks(act, body)

        @block.tensor
        def _(pe):
            pe.wait_ge(s_ws, 3)
            pe.sem_inc(s_hT, KC)
            pe.sem_inc(s_v, 2)

            def body(g, last):
                pe.wait_ge(s_h, g * SUB + 2 * SUB)
                for c in range(KC):
                    pe.wait_ge(s_hT, g * KC + (c + 1))
                    for s in range(SUB):
                        mm = nc.tensor.transpose(tp[c][:, s * P:(s + 1) * P], h[:, s, c * P:(c + 1) * P],
                                                 T["identf"][:, :])
                    mm.then_inc(s_tp, 1)
                pe.wait_ge(s_hT, g * KC + 2 * KC)
                for j in range(PAIRS):
                    if j >= 2:
                        pe.wait_ge(s_lo, g * PAIRS + (j - 1))
                    w, col = WS[j // HP], (j % HP) * P
                    for c in range(KC):
                        for a, b in TERMS:
                            mm = nc.tensor.matmul(qp[j % 2][:, :], w[:, a, c, col:col + P], hT[:, b, c, :],
                                                  start=(c == 0 and a == b == 0), stop=(c == KC - 1 and a == 1))
                    mm.then_inc(s_qp, 1)
                for s in range(SUB):
                    pe.wait_ge(s_v, g * SUB + (s + 1))
                    for c in range(KC):
                        for a, b in TERMS:
                            mm = nc.tensor.matmul(vp[s % 2][:, :], hT[:, a, c, s * P:(s + 1) * P], WS[2][:, b, c, :],
                                                  start=(c == 0 and a == b == 0), stop=(c == KC - 1 and a == 1))
                    mm.then_inc(s_vp, 1)
                pe.wait_ge(s_lo, g * PAIRS + PAIRS)

            in_blocks(pe, body)


def layer1_attention(nc, T, DR):
    TILES = 2 * HP * NT
    PAIR = 2 * NT
    STEPS = HP * NT
    LAG = 2
    F_RING, H_RING = 4, 8
    H_STEPS = H_RING // 2
    GROUPS = 4
    PER = NT // GROUPS
    MC = N // QB
    GUARDS = 2 * SUB * MC
    CW = 1024
    CH = N // CW
    CHUNKS = SUB * CH
    M1_USES = HP + SUB
    ROW_OPS = 2 * CH + 3
    MASK_OPS = 1 + SUB * ROW_OPS
    FIRST_G, LAST_G = 5, 29
    MT_STEP = 10
    COPY_STEP, SPREAD_STEP, WO_STEP, STORE_STEP = LAG, 3, 11, 28
    EXP_SCALE = 1.0 / (QK_SCALE * QK_SCALE * D ** 0.5)
    P_SHIFT = math.log(4096.0) / EXP_SCALE
    MASK_SCALE = 1e16 / EXP_SCALE
    MASK_FLOOR = -32768.0 / EXP_SCALE

    def guards_of(mb):
        def upto(step):
            return GUARDS * min(max(step - FIRST_G + 1, 0), LAST_G - FIRST_G + 1) // (LAST_G - FIRST_G + 1)
        return range(upto(mb - 1), upto(mb))

    def crow_of(mb):
        for x in range(2):
            if mb == 2 + next(m for m in range(NT) if (x + 1) * GUARDS // 2 - 1 in guards_of(m)):
                return x
        return None

    def mt_of(hp, mb):
        if hp == HP - 1 and mb >= MT_STEP:
            return mb - MT_STEP
        if hp == 0 and mb < MT_STEP:
            return mb + NT - MT_STEP
        return None

    AHEAD = NT - MT_STEP
    m0_index, use = {}, 0
    for hp_ in range(HP):
        for mb_ in range(NT):
            if mt_of(hp_, mb_) is not None:
                m0_index["mask", hp_, mb_] = use
                use += 1
            if crow_of(mb_) is not None:
                m0_index["crow", hp_, crow_of(mb_)] = use
                use += 1
    M0_USES = use
    M0_START = AHEAD + 2

    START, uses_, tile_ = [], 0, 0
    for gi_ in range(GUARDS):
        START.append(("guard", gi_, None))
        if gi_ > GUARDS // 2 and gi_ % 2 == 1 and tile_ < AHEAD:
            START.append(("mask", tile_, uses_ or None))
            tile_, uses_ = tile_ + 1, uses_ + 1
        if gi_ == GUARDS // 2 + 2:
            START.append(("crow", 0, uses_))
            uses_ += 1
    START.append(("crow", 1, uses_))
    START += [("mask", m, uses_ + 1 + m - tile_) for m in range(tile_, AHEAD)]

    FIRST_C, LAST_C = (HP - 2) * NT + 20, (HP - 1) * NT + 5
    CHUNK_STEPS = [*range(FIRST_C, FIRST_C + CHUNKS - CH), *range(LAST_C, LAST_C + CH)]

    def recip_step(hp):
        return 5 if hp == HP - 1 else 12

    POOL_SLOTS = (0, 1, 2, 3)
    PER_RING = (F_RING - len(POOL_SLOTS), len(POOL_SLOTS))
    SPLITS = tuple(n * TILES // F_RING for n in PER_RING)

    def by_pool(t):
        return t % F_RING in POOL_SLOTS

    def split_count(t):
        return sum(by_pool(k) == by_pool(t) for k in range(t + 1))

    with ExitStack() as ctx:
        def sb(name, shape, dt=F32):
            return ctx.enter_context(nc.sbuf_tensor(name, shape, dt))

        def pb(name, shape, dt=F32):
            return ctx.enter_context(nc.psum_tensor(name, shape, dt))

        def sem(name):
            return ctx.enter_context(nc.semaphore("d_" + name))

        KA = sb("d_KA", [P, 2, 2, N], F16)
        KB = sb("d_KB", [P, 2, N], F16)
        V = sb("d_V", [P, NT, 2, P], F16)
        QA = sb("d_QA", [P, 2, 2, QB], F16)
        QL = sb("d_QL", [P, 2, 2, QB], F16)
        MR = sb("d_MR", [P, SUB, N], BF16)
        MT = sb("d_MT", [P, NT, QB], BF16)
        stage = sb("d_stage", [P, 2, CW])
        dblk = sb("d_dblk", [P, SUB, P])
        brow = sb("d_brow", [P, SUB])
        PF = sb("d_PF", [P, F_RING, QB])
        PH = sb("d_PH", [P, H_RING, QB], F16)
        PL = sb("d_PL", [P, H_RING, QB], F16)
        oN = sb("d_oN", [P, HP, QB])
        wo = sb("d_wo", [P, HP, F])
        xr = sb("d_xr", [P, SUB, F])
        rb = sb("d_rb", [P, QB])
        dT = sb("d_dT", [P, QB])
        junk = sb("d_junk", [P, 2, QB], BF16)
        gm = sb("d_gm", [P, SUB, MC])
        cm = sb("d_cm", [P, SUB])
        dg = sb("d_dg", [P, SUB, P], F16)
        shift = sb("d_shift", [P, 1])
        scale1 = sb("d_scale1", [P, DEN], F16)
        selc = sb("d_selc", [P, P], F16)
        seld = sb("d_seld", [P, P])
        idh = sb("d_idh", [P, P], F16)

        sc = [pb(f"d_sc{i}", [P, QB]) for i in range(2)]
        gd = [pb(f"d_gd{i}", [P, QB]) for i in range(2)]
        acc = pb("d_acc", [P, QB])
        den = pb("d_den", [P, QB])
        misc0 = pb("d_misc0", [P, QB])
        misc1 = pb("d_misc1", [P, QB])
        misc0h = misc0[:, :].bitcast(BF16)

        s_passed = sem("waits_passed")
        s_const = sem("const_in")
        s_set = sem("constants_set")
        s_KA = [[sem(f"ka_in{i}{x}") for x in range(2)] for i in range(2)]
        s_Q = [sem(f"q_in{i}") for i in range(2)]
        s_KB = [sem(f"kb_in{i}") for i in range(GROUPS)]
        s_V = [sem(f"v_in{i}") for i in range(GROUPS)]
        s_stage = [sem(f"adj_in{i}") for i in range(2)]
        s_dblk = sem("adj_diagonal_in")
        s_mk = sem("mask_made")
        s_mtp = sem("mask_transposed")
        s_m0 = sem("misc0_read")
        s_S = sem("scores")
        s_P = sem("exp_done")
        s_low = sem("low_by_vector")
        s_lowp = sem("low_by_gpsimd")
        s_used = sem("steps_used")
        s_G = sem("guard_scores")
        s_gm = sem("guard_max")
        s_cm = sem("row_max")
        s_dg = sem("row_max_diagonal")
        s_crow = sem("max_row")
        s_ac = sem("acc_copied")
        s_dc = sem("den_copied")
        s_m1w = sem("misc1_written")
        s_m1 = sem("misc1_read")
        s_rb = sem("reciprocal")
        s_oN = sem("normalised")
        s_x = sem("x1_in")
        s_out = sem("out_stored")

        block = ctx.enter_context(nc.Block())

        def load_ka(sp, par, hp):
            for x in range(2):
                row = (2 * hp + x) * D
                sp.dma_start(KA[0:D, par, x, :], DR["kh"][row:row + D, :]).then_inc(s_KA[par][x], 16)
                sp.dma_start(KA[D:P, par, x, :], DR["kl"][row:row + D, :]).then_inc(s_KA[par][x], 16)

        def load_q(sp, par, hp, nb):
            for x in range(2):
                row = (2 * hp + x) * D
                for half in range(2):
                    sp.dma_start(QA[half * D:(half + 1) * D, par, x, :], DR["qh"][row:row + D, bass.ds(nb * QB, QB)]).then_inc(s_Q[par], 16)
                sp.dma_start(QL[0:D, par, x, :], DR["ql"][row:row + D, bass.ds(nb * QB, QB)]).then_inc(s_Q[par], 16)

        def load_kb(sp, hp, i):
            cols = slice(i * PER * P, (i + 1) * PER * P)
            for x in range(2):
                row = (2 * hp + x) * D
                sp.dma_start(KB[0:D, x, cols], DR["kh"][row:row + D, cols]).then_inc(s_KB[i], 16)

        def load_v(sp, hp, i):
            rows = slice(i * PER * P, (i + 1) * PER * P)
            sp.dma_start(V[:, i * PER:(i + 1) * PER, :, :].rearrange("p m a n -> p m (a n)"),
                         DR["v1"][hp, rows, :].rearrange("(m p) k -> p m k", p=P)).then_inc(s_V[i], 16)

        def load_diagonals(sp, nb):
            for s in range(SUB):
                rows = bass.ds(nb * QB + s * P, P)
                sp.dma_start(dblk[:, s, :], DR["adj"][rows, bass.ds(nb * QB + s * P, P)]).then_inc(s_dblk, 16)

        def load_chunk(sp, nb, ci):
            s, c = divmod(ci, CH)
            sp.dma_start(stage[:, ci % 2, :], DR["adj"][bass.ds(nb * QB + s * P, P), c * CW:(c + 1) * CW]).then_inc(s_stage[ci % 2], 16)

        def chunk_done(ci):
            return 1 + ROW_OPS * (ci // CH) + 2 * (ci % CH) + 2

        @block.sync
        def _(sp):
            for tile, name in ((selc, "selc"), (seld, "seld"), (idh, "idh")):
                sp.dma_start(tile[:, :], DR[name]).then_inc(s_const, 16)
            sp.dma_start(wo[:, :, :], DR["Wo"].rearrange("(c p) n -> p c n", p=P)).then_inc(s_const, 16)
            load_diagonals(sp, 0)
            for ci in range(2):
                load_chunk(sp, 0, ci)
            load_ka(sp, 0, 0)
            load_q(sp, 0, 0, 0)
            for ci in range(2, CHUNKS):
                sp.wait_ge(s_mk, chunk_done(ci - 2))
                load_chunk(sp, 0, ci)
            for i in range(GROUPS):
                load_kb(sp, 0, i)
                load_v(sp, 0, i)

            def store(nb):
                wait_apart(sp, s_m1, nb * M1_USES + (M1_USES + 1), s_passed)
                sp.dma_start(DR["out"][bass.ds(nb * QB, QB), :].rearrange("(s p) f -> p s f", p=P), xr[:, :, :]).then_inc(s_out, 16)
                wait_apart(sp, s_out, nb * 16 + 16, s_passed)

            def body(nb, first):
                for hp in range(HP):
                    nxt, par = (hp + 1) % HP, (hp + 1) % 2
                    for mb in range(NT):
                        step = hp * NT + mb
                        if mb == 0:
                            sp.wait_ge(s_S, nb * TILES + (hp * PAIR + CREDIT))
                            load_ka(sp, par, nxt)
                            load_q(sp, par, nxt, nb if hp < HP - 1 else (nb + 1) % NB)
                        if mb % PER == PER - 1:
                            sp.wait_ge(s_S, nb * TILES + (hp * PAIR + 2 * (mb + 1) + CREDIT))
                            load_kb(sp, nxt, mb // PER)
                        if mb % PER == LAG:
                            i = (mb // PER - 1) % GROUPS
                            if not (first and step < PER):
                                sp.wait_ge(s_used, nb * STEPS + (step - LAG + H_STEPS))
                                load_v(sp, nxt if mb > PER else hp, i)
                        if step == FIRST_C - 3:
                            wait_apart(sp, s_mk, nb * MASK_OPS + MASK_OPS, s_passed)
                            load_diagonals(sp, (nb + 1) % NB)
                            chunks = range(2)
                        else:
                            chunks = [CHUNK_STEPS.index(step) + 2] if step in CHUNK_STEPS[:CHUNKS - 2] else []
                        for ci in chunks:
                            done = chunk_done(ci - 2) if ci >= 2 else chunk_done(CHUNKS + ci - 2) - MASK_OPS
                            wait_apart(sp, s_mk, nb * MASK_OPS + (MASK_OPS + done), s_passed)
                            load_chunk(sp, (nb + 1) % NB, ci)
                        if step == STORE_STEP:
                            if not first:
                                store(nb - 1)
                            sp.dma_start(xr[:, :, :], DR["x1"][bass.ds(nb * QB, QB), :].rearrange("(s p) f -> p s f", p=P)).then_inc(s_x, 16)

            body(0, True)
            with sp.Fori(0, NB - 1) as i:
                body(i + 1, False)
            store(NB - 1)
            for par in range(2):
                for x in range(2):
                    sp.wait_ge(s_KA[par][x], 32 * (2 * NB + 1 - par))
                sp.wait_ge(s_Q[par], 96 * (2 * NB + 1 - par))
            for i in range(GROUPS):
                sp.wait_ge(s_KB[i], 32 * (HP * NB + 1))
                sp.wait_ge(s_V[i], 16 * (HP * NB + (1 if i < GROUPS - 1 else 0)))

        def split(eng, engine, nb, t):
            engine.wait_ge(s_P, nb * TILES + (CREDIT + t + 1))
            eng.tensor_tensor(PL[:, t % H_RING, :], PF[:, t % F_RING, :], PH[:, t % H_RING, :],
                              ALU.subtract).then_inc(s_lowp if by_pool(t) else s_low, 1)

        @block.gpsimd
        def _(pool):
            pool.sem_inc(s_lowp, PER_RING[1])
            with pool.Fori(0, NB) as nb:
                for t in range(TILES):
                    if by_pool(t):
                        split(nc.gpsimd, pool, nb, t)

        @block.scalar
        def _(act):
            act.wait_ge(s_const, 16 * 4)
            act.wait_ge(s_set, 5)
            act.sem_inc(s_P, CREDIT)
            act.sem_inc(s_ac, 1)

            def copy_crow(count, par, x):
                act.wait_ge(s_crow, count)
                nc.scalar.activation(QL[D:P, par, x, :], misc0[D:P, :], ACT.Identity, bias=shift[D:P, :]).then_inc(s_m0, 1)

            def copy_mask(count, m):
                act.wait_ge(s_mtp, count)
                nc.scalar.activation(MT[:, m, :], misc0h[:, 0:QB], ACT.Copy).then_inc(s_m0, 1)

            def copy_acc(nb, hp):
                act.wait_ge(s_used, nb * STEPS + ((hp + 1) * NT + H_STEPS))
                nc.scalar.activation(oN[:, hp, :], acc[:, :], ACT.Copy).then_inc(s_ac, 1)

            for what, k, _ in START:
                if what == "crow":
                    copy_crow(k + 1, 0, k)
                if what == "mask":
                    copy_mask(k + 1, k)

            def body(nb, first):
                for hp in range(HP):
                    for mb in range(NT):
                        if mb == COPY_STEP:
                            if hp:
                                if hp == 1:
                                    act.wait_ge(s_m1w, nb * M1_USES + 1)
                                copy_acc(nb, hp - 1)
                            elif not first:
                                copy_acc(nb - 1, HP - 1)
                        for x in range(2):
                            t = hp * PAIR + 2 * mb + x
                            act.wait_ge(s_S, nb * TILES + (CREDIT + t + 1))
                            act.wait_ge(s_lowp if by_pool(t) else s_low, nb * SPLITS[by_pool(t)] + split_count(t))
                            nc.scalar.activation(PF[:, t % F_RING, :], sc[t % 2][:, :], ACT.Exp, scale=EXP_SCALE)
                            if x == 0:
                                act.wait_ge(s_used, nb * STEPS + (hp * NT + mb + 1))
                            nc.scalar.activation(PH[:, t % H_RING, :], sc[t % 2][:, :], ACT.Exp, scale=EXP_SCALE).then_inc(s_P, 1)
                        m = mt_of(hp, mb)
                        if m is not None:
                            copy_mask(nb * NT + ((AHEAD if hp else 0) + m + (1 if not hp else 1 + NT - AHEAD)), m)
                        if crow_of(mb) is not None:
                            copy_crow(nb * (2 * HP) + (2 * hp + crow_of(mb) + 3), (hp + 1) % 2, crow_of(mb))

            body(0, True)
            with act.Fori(0, NB - 1) as i:
                body(i + 1, False)
            copy_acc(NB - 1, HP - 1)

        @block.vector
        def _(dve):
            nc.vector.memset(scale1[:, :], QK_SCALE).then_inc(s_set, 1)
            nc.vector.memset(KB[D:P, :, :], 0.0).then_inc(s_set, 1)
            nc.vector.memset(shift[:, :], 0.0).then_inc(s_set, 1)
            dve.wait_ge(s_set, 3)
            nc.vector.memset(KB[D:D + 1, :, :], C_ROW).then_inc(s_set, 1)
            nc.vector.memset(shift[D:D + 1, :], P_SHIFT / C_ROW).then_inc(s_set, 1)
            dve.wait_ge(s_const, 16 * 4)
            if PER_RING[0]:
                dve.sem_inc(s_low, PER_RING[0])
            dve.sem_inc(s_dc, 1)
            dve.sem_inc(s_m1, 1)

            def mask_setup(nb):
                nc.vector.tensor_scalar(brow[:, :], T["amax"][:, bass.ds(nb * SUB, SUB)], 1.0, -1.0,
                                        ALU.max, ALU.add).then_inc(s_mk, 1)

            def mask_chunk(run, nb, ci):
                s, c = divmod(ci, CH)
                at = run * MASK_OPS + (chunk_done(ci) - 2)
                dve.wait_ge(s_stage[ci % 2], run * (16 * CHUNKS // 2) + 16 * (ci // 2 + 1))
                dve.wait_ge(s_mk, at)
                nc.vector.tensor_scalar(stage[:, ci % 2, :], stage[:, ci % 2, :], -1.0, brow[:, s:s + 1],
                                        ALU.add, ALU.subtract).then_inc(s_mk, 1)
                dve.wait_ge(s_mk, at + 1)
                nc.vector.tensor_scalar(MR[:, s, c * CW:(c + 1) * CW], stage[:, ci % 2, :], MASK_SCALE, MASK_FLOOR,
                                        ALU.mult, ALU.max).then_inc(s_mk, 1)
                if c < CH - 1:
                    return
                dve.wait_ge(s_dblk, run * (16 * SUB) + 16 * SUB)
                at = at + 2
                nc.vector.tensor_tensor(dblk[:, s, :], dblk[:, s, :], T["identf"][:, :], ALU.max).then_inc(s_mk, 1)
                dve.wait_ge(s_mk, at + 1)
                nc.vector.tensor_scalar(dblk[:, s, :], dblk[:, s, :], -1.0, brow[:, s:s + 1],
                                        ALU.add, ALU.subtract).then_inc(s_mk, 1)
                dve.wait_ge(s_mk, at + 2)
                nc.vector.tensor_scalar(MR[:, s, bass.ds(nb * QB + s * P, P)], dblk[:, s, :], MASK_SCALE, MASK_FLOOR,
                                        ALU.mult, ALU.max).then_inc(s_mk, 1)

            def guard(it, gi, mask_count=None):
                x, s, c = gi // (SUB * MC), gi // MC % SUB, gi % MC
                if mask_count is not None:
                    dve.wait_ge(s_mk, mask_count)
                if gi >= 2 or not isinstance(it, int):
                    dve.wait_ge(s_gm, it * GUARDS + (gi - 1))
                wait_apart(dve, s_G, it * GUARDS + (gi + 1), s_passed)
                nc.vector.tensor_tensor_reduce(out=junk[:, gi % 2, :], in0=gd[gi % 2][:, :], in1=MR[:, s, c * QB:(c + 1) * QB],
                                               scale=1.0, scalar=-3.0e38, op0=ALU.add, op1=ALU.max,
                                               accum_out=gm[:, s, c:c + 1]).then_inc(s_gm, 1)
                if c == MC - 1:
                    n = x * SUB + s
                    dve.wait_ge(s_gm, it * GUARDS + (gi + 1))
                    nc.vector.reduce_max(cm[:, s:s + 1], gm[:, s, :], AX.X).then_inc(s_cm, 1)
                    dve.wait_ge(s_cm, it * (2 * SUB) + (n + 1))
                    if s == 0 and not (isinstance(it, int) and it == 0 and x == 0):
                        dve.wait_ge(s_crow, it * 2 + x)
                    nc.vector.tensor_scalar(dg[:, s, :], idh[:, :], cm[:, s:s + 1], -1.0 / C_ROW,
                                            ALU.mult, ALU.mult).then_inc(s_dg, 1)

            def copy_den(nb, hp):
                dve.wait_ge(s_used, nb * STEPS + ((hp + 1) * NT + H_STEPS))
                nc.vector.tensor_copy(dT[:, :], den[:, :]).then_inc(s_dc, 1)

            def reciprocal(nb, hp, k):
                dve.wait_ge(s_m1w, nb * M1_USES + (hp + 2))
                ins = nc.vector.reciprocal(rb[:, k * P:(k + 1) * P], misc1[:, k * P:(k + 1) * P])
                ins.then_inc(s_m1 if k == SUB - 1 else s_rb, 1)

            def normalise(nb, hp):
                dve.wait_ge(s_m1, nb * M1_USES + (hp + 2))
                dve.wait_ge(s_ac, nb * HP + (hp + 2))
                nc.vector.tensor_tensor(oN[:, hp, :], oN[:, hp, :], rb[:, :], ALU.mult).then_inc(s_oN, 1)

            def add_rows(nb, s):
                if s == 0:
                    dve.wait_ge(s_x, nb * 16 + 16)
                dve.wait_ge(s_m1w, nb * M1_USES + (HP + s + 2))
                nc.vector.tensor_tensor(xr[:, s, :], misc1[:, :], xr[:, s, :], ALU.add).then_inc(s_m1, 1)

            def finish(nb, hp, mb):
                if mb == COPY_STEP:
                    copy_den(nb, hp)
                if recip_step(hp) <= mb < recip_step(hp) + SUB:
                    reciprocal(nb, hp, mb - recip_step(hp))
                if mb == recip_step(hp) + SUB:
                    normalise(nb, hp)
                s = (mb - WO_STEP - 2) // 3
                if hp == HP - 1 and (mb - WO_STEP - 2) % 3 == 0 and 0 <= s < SUB:
                    add_rows(nb, s)

            mask_setup(0)
            dve.wait_ge(s_mk, 1)
            for ci in range(CHUNKS):
                mask_chunk(0, 0, ci)
                for gi in range(2 * (ci - CH), 2 * (ci - CH) + 2):
                    if gi >= 0:
                        guard(0, gi, 1 + ROW_OPS * (gi // MC + 1) if gi % MC == 0 else None)
            dve.wait_ge(s_mk, MASK_OPS)
            for gi in range(2 * (CHUNKS - CH), GUARDS):
                guard(0, gi)

            def body(nb, first):
                for hp in range(HP):
                    for mb in range(NT):
                        step = hp * NT + mb
                        if hp:
                            finish(nb, hp - 1, mb)
                        elif not first:
                            finish(nb - 1, HP - 1, mb)
                        guards = list(guards_of(mb))
                        for x in range(2):
                            t = 2 * (step - 1) + x
                            if t >= 0 and not by_pool(t):
                                split(nc.vector, dve, nb, t)
                            elif t < 0 and not first and not by_pool(t + TILES):
                                split(nc.vector, dve, nb - 1, t + TILES)
                            for gi in guards[:1] if x == 0 else guards[1:]:
                                row_at = gi // MC % SUB + 1
                                count = nb * MASK_OPS + (MASK_OPS + 1 + ROW_OPS * row_at) if hp == HP - 1 and gi < SUB * MC and gi % MC == 0 else None
                                guard(nb * HP + (hp + 1), gi, count)
                        if step == FIRST_C:
                            dve.wait_ge(s_mtp, nb * NT + NT)
                            mask_setup((nb + 1) % NB)
                            dve.wait_ge(s_mk, nb * MASK_OPS + (MASK_OPS + 1))
                        if step in CHUNK_STEPS:
                            mask_chunk(nb + 1, (nb + 1) % NB, CHUNK_STEPS.index(step))

            body(0, True)
            with dve.Fori(0, NB - 1) as i:
                body(i + 1, False)
            for x in range(2):
                if not by_pool(TILES - 2 + x):
                    split(nc.vector, dve, NB - 1, TILES - 2 + x)
            for mb in range(NT):
                finish(NB - 1, HP - 1, mb)

        @block.tensor
        def _(pe):
            pe.wait_ge(s_const, 16 * 4)
            pe.wait_ge(s_set, 5)
            pe.sem_inc(s_S, CREDIT)
            pe.sem_inc(s_used, H_STEPS)
            pe.sem_inc(s_m1w, 1)

            def guard(it, par, gi, count):
                x, s, c = gi // (SUB * MC), gi // MC % SUB, gi % MC
                if s == 0 and c == 0:
                    if x == 0:
                        pe.wait_ge(s_Q[par], count * 96 + 96)
                    pe.wait_ge(s_KA[par][x], count * 32 + 32)
                if gi >= 2 or not isinstance(it, int):
                    pe.wait_ge(s_gm, it * GUARDS + (gi - 1))
                nc.tensor.matmul(gd[gi % 2][:, :], QA[:, par, x, s * P:(s + 1) * P], KA[:, par, x, c * QB:(c + 1) * QB],
                                 start=True, stop=True).then_inc(s_G, 1)

            def crow(it, x, uses):
                pe.wait_ge(s_dg, it * (2 * SUB) + SUB * (x + 1))
                pe.wait_ge(s_m0, uses)
                for s in range(SUB):
                    mm = nc.tensor.matmul(misc0[:, s * P:(s + 1) * P], selc[:, :], dg[:, s, :], start=True, stop=True)
                mm.then_inc(s_crow, 1)

            def transpose_mask(m, uses):
                if uses is not None:
                    pe.wait_ge(s_m0, uses)
                for s in range(SUB):
                    mm = nc.tensor.transpose(misc0h[:, s * P:(s + 1) * P], MR[:, s, m * P:(m + 1) * P], T["identb"][:, :])
                mm.then_inc(s_mtp, 1)

            def scores(nb, hp, mb, x):
                par, t = hp % 2, hp * PAIR + 2 * mb + x
                pe.wait_ge(s_P, nb * TILES + (CREDIT + t - 1))
                bank = sc[t % 2][:, :]
                nc.tensor.matmul(bank, KA[:, par, x, mb * P:(mb + 1) * P], QA[:, par, x, :], start=True, stop=False)
                nc.tensor.matmul(bank, KB[:, x, mb * P:(mb + 1) * P], QL[:, par, x, :], start=False, stop=False)
                nc.tensor.matmul(bank, T["identb"][:, :], MT[:, mb, :], start=False, stop=True).then_inc(s_S, 1)

            def products(nb, step):
                hp, mb = divmod(step, NT)
                if mb == 0:
                    pe.wait_ge(s_ac, nb * HP + (hp + 1))
                    pe.wait_ge(s_dc, nb * HP + (hp + 1))
                if mb % PER == 0:
                    pe.wait_ge(s_V[mb // PER], nb * (16 * HP) + 16 * (hp + 1))
                pe.wait_ge(s_P, nb * TILES + (CREDIT + 2 * step + 2))
                first, last = mb == 0, mb == NT - 1
                for half in range(2):
                    for x in range(2):
                        nc.tensor.matmul(acc[x * D:(x + 1) * D, :], V[:, mb, half, x * D:(x + 1) * D],
                                         PH[:, (2 * step + x) % H_RING, :], start=first and half == 0, stop=False)
                for x in range(2):
                    t = 2 * step + x
                    own = by_pool(t)
                    pe.wait_ge(s_lowp if own else s_low, nb * SPLITS[own] + (PER_RING[own] + split_count(t)))
                    nc.tensor.matmul(acc[x * D:(x + 1) * D, :], V[:, mb, 0, x * D:(x + 1) * D],
                                     PL[:, t % H_RING, :], start=False, stop=last)
                for i in range(QUAD):
                    x, half = divmod(i, 2)
                    mm = nc.tensor.matmul(den[i * DEN:(i + 1) * DEN, :], scale1[:, :], (PH, PL)[half][:, (2 * step + x) % H_RING, :],
                                          start=first, stop=last, tile_position=(0, i * DEN))
                mm.then_inc(s_used, 1)

            def spread_den(nb, hp):
                pe.wait_ge(s_dc, nb * HP + (hp + 2))
                pe.wait_ge(s_m1, nb * M1_USES + (hp + 1))
                nc.tensor.matmul(misc1[:, :], seld[:, :], dT[:, :], start=True, stop=True).then_inc(s_m1w, 1)

            def project_out(nb, s):
                if s == 0:
                    pe.wait_ge(s_oN, nb * HP + HP)
                pe.wait_ge(s_m1, nb * M1_USES + (HP + s + 1))
                for c in range(HP):
                    mm = nc.tensor.matmul(misc1[:, :], oN[:, c, s * P:(s + 1) * P], wo[:, c, :],
                                          start=(c == 0), stop=(c == HP - 1))
                mm.then_inc(s_m1w, 1)

            def finish(nb, hp, mb):
                if mb == SPREAD_STEP:
                    spread_den(nb, hp)
                s = (mb - WO_STEP) // 3
                if hp == HP - 1 and (mb - WO_STEP) % 3 == 0 and 0 <= s < SUB:
                    project_out(nb, s)

            for what, k, uses in START:
                if what == "guard":
                    guard(0, 0, k, 0)
                elif what == "crow":
                    crow(0, k, uses)
                else:
                    if k == 0:
                        pe.wait_ge(s_mk, MASK_OPS)
                    transpose_mask(k, uses)

            def body(nb, first):
                for hp in range(HP):
                    uses = nb * M0_USES + M0_START
                    for mb in range(NT):
                        step = hp * NT + mb
                        if mb == 0:
                            count = nb * 2 + hp // 2
                            pe.wait_ge(s_Q[hp % 2], count * 96 + 96)
                            for x in range(2):
                                pe.wait_ge(s_KA[hp % 2][x], count * 32 + 32)
                            if hp:
                                pe.wait_ge(s_m0, uses + (m0_index["crow", hp - 1, 1] + 1))
                            else:
                                pe.wait_ge(s_m0, uses - 1)
                        if hp == 0 and mb >= AHEAD - 1:
                            at = 0 if mb < AHEAD else m0_index["mask", 0, mb - AHEAD] + 1
                            pe.wait_ge(s_m0, uses + at)
                        if mb % PER == 0:
                            pe.wait_ge(s_KB[mb // PER], nb * (32 * HP) + 32 * (hp + 1))
                        guards = list(guards_of(mb))
                        it, par, count = nb * HP + (hp + 1), (hp + 1) % 2, nb * 2 + (hp + 1) // 2
                        scores(nb, hp, mb, 0)
                        for gi in guards[:1]:
                            guard(it, par, gi, count)
                        if mt_of(hp, mb) is not None:
                            if hp and mb == MT_STEP:
                                pe.wait_ge(s_mk, nb * MASK_OPS + 2 * MASK_OPS)
                            transpose_mask(mt_of(hp, mb), uses + m0_index["mask", hp, mb])
                        scores(nb, hp, mb, 1)
                        for gi in guards[1:2]:
                            guard(it, par, gi, count)
                        if crow_of(mb) is not None:
                            x = crow_of(mb)
                            crow(it, x, uses + m0_index["crow", hp, x])
                        if step >= LAG:
                            products(nb, step - LAG)
                        elif not first:
                            products(nb - 1, step - LAG + STEPS)
                        for gi in guards[2:]:
                            guard(it, par, gi, count)
                        if hp:
                            finish(nb, hp - 1, mb)
                        elif not first:
                            finish(nb - 1, HP - 1, mb)

            body(0, True)
            with pe.Fori(0, NB - 1) as i:
                body(i + 1, False)
            for step in range(STEPS - LAG, STEPS):
                products(NB - 1, step)
            for mb in range(NT):
                finish(NB - 1, HP - 1, mb)


def build(nc, DR):
    with ExitStack() as ctx:
        def sb(name, shape, dt=F32):
            return ctx.enter_context(nc.sbuf_tensor(name, shape, dt))

        T = {
            "identf": sb("identf", [P, P]), "identb": sb("identb", [P, P], BF16),
            "amax": sb("amax", [P, NT]),
        }
        with ExitStack() as layer0:
            def sb0(name, shape, dt=F32):
                return layer0.enter_context(nc.sbuf_tensor(name, shape, dt))

            T["V"] = sb0("V0", [P, NT, F])
            T["w"], T["v"], T["nv"] = (sb0(x, [P, NT, H]) for x in ("w", "v", "nv"))
            layer0_project(nc, T, DR)
            layer0_attention(nc, T, DR)
        layer1_project(nc, T, DR)
        layer1_attention(nc, T, DR)


_SCRATCH = [("amax", (N,), F32), ("r", (H, N), F32), ("x1", (N, F), F32), ("v1", (HP, N, 2 * P), F16),
            ("qh", (F, N), F16), ("ql", (F, N), F16), ("kh", (F, N), F16), ("kl", (F, N), F16)]


def kernel(**inputs):
    import numpy as np
    import concourse.bacc as bacc
    from concourse.bass_utils import run_bass_kernel_spmd

    a = {k: np.asarray(v) for k, v in inputs.items()}
    proj = np.zeros((F, 2 * H), np.float32)
    for hd in range(H):
        proj[hd * D:(hd + 1) * D, hd] = a["L0_gnn_src_proj"][0, hd]
        proj[hd * D:(hd + 1) * D, H + hd] = a["L0_gnn_trg_proj"][0, hd]
    arrays = {
        "x": a["x"], "adj": a["adj"], "adjT": a["adj"].T, "W0": a["L0_gnn_W"], "W0T": a["L0_gnn_W"].T,
        "b": a["L0_gnn_b"], "bcol": a["L0_gnn_b"].reshape(KC, P).T, "proj": proj,
        "Wk": a["L1_gnn_Wks"].transpose(1, 0, 2).reshape(F, F), "Wq": a["L1_gnn_Wqs"].transpose(1, 0, 2).reshape(F, F),
        "Wv": a["L1_gnn_Wvs"].transpose(1, 0, 2).reshape(F, F), "Wo": a["L1_gnn_Wo"].reshape(F, F),
        "selc": np.eye(1, P, D, dtype=np.float16).repeat(P, 0),
        "seld": np.eye(P, dtype=np.float32)[[0, 64]].repeat(D, 0).T + np.eye(P, dtype=np.float32)[[32, 96]].repeat(D, 0).T,
        "idh": np.eye(P, dtype=np.float16),
        "identf": np.eye(P, dtype=np.float32), "identb": np.eye(P, dtype=np.float32).astype(mybir.dt.np(BF16)),
    }
    arrays = {f"in_{k}": np.ascontiguousarray(v) for k, v in arrays.items()}
    nc = bacc.Bacc("TRN2", target_bir_lowering=False, num_devices=1)
    DR = {k[3:]: nc.dram_tensor(k, v.shape, mybir.dt.from_np(v.dtype), kind="ExternalInput").ap() for k, v in arrays.items()}
    DR |= {k: nc.dram_tensor(f"scratch_{k}", shape, dt, kind="Internal").ap() for k, shape, dt in _SCRATCH}
    DR["out"] = nc.dram_tensor("out_dram", (N, F), F32, kind="ExternalOutput").ap()
    build(nc, DR)
    return run_bass_kernel_spmd(nc, [arrays], core_ids=[0]).results[0]["out_dram"]
```
